# Optimizing a Trainium2 kernel written in Bass

```python
import numpy as np
import jax
import jax.numpy as jnp

def _softmax(x, axis=-1):
    return jax.nn.softmax(x, axis=axis)

def _gelu(x):
    return jax.nn.gelu(x, approximate=True)

def _silu(x):
    return jax.nn.silu(x)

def _sigmoid(x):
    return jax.nn.sigmoid(x)

def _layernorm(x, axis=-1, eps=1e-05):
    m = jnp.mean(x, axis=axis, keepdims=True)
    v = jnp.var(x, axis=axis, keepdims=True)
    return (x - m) / jnp.sqrt(v + eps)

def _scatter_add(tgt, idx, src, axis=0):
    return tgt.at[idx].add(src)

def _segment_sum(src, seg, n):
    return jax.ops.segment_sum(src, seg, n)
kernel_name = 'mk_xattn_ffn_d2_seqx_r8_cc710c'

def setup_inputs(seed: int=0):
    np.random.seed(seed)
    _w = jnp.asarray

    def _rec_inputs():
        import jax
        import jax.numpy as jnp
        _rk = jax.random.key(seed)
        x = -0.000125 + 0.9999 * jax.random.normal(jax.random.fold_in(_rk, 1), (4, 256, 256), jnp.float32)
        _lenS = 256 - jax.random.randint(jax.random.fold_in(_rk, 7), (4,), 0, max(1, 256 // 4) + 1, jnp.int32)
        _lenS2 = 256 - jax.random.randint(jax.random.fold_in(_rk, 8), (4,), 0, max(1, 256 // 4) + 1, jnp.int32)
        itok_BxS_13_99985 = jax.random.randint(jax.random.fold_in(_rk, 11), (4, 256), 13, 99986, jnp.int32)
        _ctx_2048P = jax.random.normal(jax.random.fold_in(_rk, 12), (4, 16, 256), jnp.float32)
        _ctx_2048c = jax.random.dirichlet(jax.random.fold_in(_rk, 512), 0.3 * jnp.ones((16,), jnp.float32), (4, 256))
        _ctx_2048t = jnp.einsum('bsk,bkd->bsd', _ctx_2048c, _ctx_2048P)
        _ctx_2048t = _ctx_2048t * jax.lax.rsqrt(jnp.mean(jnp.square(_ctx_2048t)) + 1e-12) * 0.953939
        ctx_2048 = 6.82029e-06 + 0.0200006 * (_ctx_2048t + 0.3 * jax.random.normal(jax.random.fold_in(_rk, 612), (4, 256, 256), jnp.float32))
        return (x, itok_BxS_13_99985, ctx_2048)
    x, itok_BxS_13_99985, ctx_2048 = _rec_inputs()

    def _L0_xattn_setup():
        import jax, jax.numpy as jnp
        import numpy as np
        B, S, D = (4, 512, 256)
        E = 4
        F = 1024 // E
        VOCAB = 12500
        key = jax.random.key(seed)
        k1, k2, k3, k4, k5 = jax.random.split(key, 5)
        hidden_states = jax.random.normal(k1, (B, S, D), dtype=jnp.float32)
        token_ids = jax.random.randint(k2, (B, S), 0, VOCAB, dtype=jnp.int64)
        Wg = jax.random.normal(k3, (E, F, D), dtype=jnp.float32) * 0.02
        Wu = jax.random.normal(k4, (E, F, D), dtype=jnp.float32) * 0.02
        Wd = jax.random.normal(k5, (E, D, F), dtype=jnp.float32) * 0.02
        return {'hidden_states': hidden_states, 'token_ids': token_ids, 'Wg': Wg, 'Wu': Wu, 'Wd': Wd}
    _L0_xattn_all = _L0_xattn_setup()
    _L0_xattn_in = {k: v for k, v in _L0_xattn_all.items() if k in ()}
    del _L0_xattn_all

    def _L0_ffn_setup():
        import jax, jax.numpy as jnp
        import numpy as np
        HIDDEN = 256
        INTER = 1024
        COMPRESSION = 128.9

        def _n_ctrl(out_size, in_size):
            return max(16, int(out_size * in_size / COMPRESSION))

        def _catmull_rom_grid(n_ctrl, n_samples):
            t = np.linspace(0.0, n_ctrl - 1.0, n_samples, dtype=np.float64)
            i = np.clip(np.floor(t).astype(np.int64), 0, n_ctrl - 2)
            f = (t - i).astype(np.float32)
            idx = np.stack([np.clip(i + k, 0, n_ctrl - 1) for k in (-1, 0, 1, 2)], axis=0)
            return (jnp.asarray(idx.astype(np.int32)), jnp.asarray(f))

        def spline_reconstruct(control_points, out_size, in_size):
            n = out_size * in_size
            idx, f = _catmull_rom_grid(control_points.shape[0], n)
            p0, p1, p2, p3 = (control_points[idx[0]], control_points[idx[1]], control_points[idx[2]], control_points[idx[3]])
            f2 = f * f
            f3 = f2 * f
            w = 0.5 * (2.0 * p1 + (p2 - p0) * f + (2.0 * p0 - 5.0 * p1 + 4.0 * p2 - p3) * f2 + (3.0 * p1 - p0 - 3.0 * p2 + p3) * f3)
            return w.reshape(out_size, in_size)
        key = jax.random.key(seed)
        k0, k1, k2, k3 = jax.random.split(key, 4)
        hidden_states = jax.random.normal(k0, (4, 256, HIDDEN), dtype=jnp.float32)
        gate_cp = jax.random.normal(k1, (_n_ctrl(INTER, HIDDEN),), dtype=jnp.float32) * 0.02
        up_cp = jax.random.normal(k2, (_n_ctrl(INTER, HIDDEN),), dtype=jnp.float32) * 0.02
        down_cp = jax.random.normal(k3, (_n_ctrl(HIDDEN, INTER),), dtype=jnp.float32) * 0.02
        return {'hidden_states': hidden_states, 'gate_cp': gate_cp, 'up_cp': up_cp, 'down_cp': down_cp}
    _L0_ffn_all = _L0_ffn_setup()
    _L0_ffn_in = {k: v for k, v in _L0_ffn_all.items() if k in ('gate_cp', 'up_cp', 'down_cp')}
    del _L0_ffn_all

    def _L1_xattn_setup():
        import jax, jax.numpy as jnp
        import numpy as np
        D_MODEL = 256
        NUM_HEADS = 16
        HEAD_DIM = D_MODEL // NUM_HEADS

        def _fq_sym(x, axis):
            s = jnp.max(jnp.abs(x), axis=axis, keepdims=True) / 127.0
            s = jnp.maximum(s, 1e-08)
            q = jnp.clip(jnp.round(x / s), -127.0, 127.0) * s
            return x + jax.lax.stop_gradient(q - x)

        def _fq_unsigned(x, axis):
            s = jnp.max(x, axis=axis, keepdims=True) / 255.0
            s = jnp.maximum(s, 1e-08)
            q = jnp.clip(jnp.round(x / s), 0.0, 255.0) * s
            return x + jax.lax.stop_gradient(q - x)
        key = jax.random.key(seed)
        ks = jax.random.split(key, 8)
        B, N, M, C = (2, 256, 64, D_MODEL)
        return {'x': jax.random.normal(ks[0], (B, N, C), jnp.float32), 'cond': jax.random.normal(ks[1], (B, M, C), jnp.float32), 'Wq': jax.random.normal(ks[2], (C, C), jnp.float32) * 0.02, 'bq': jnp.zeros((C,), jnp.float32), 'Wkv': jax.random.normal(ks[3], (C, 2 * C), jnp.float32) * 0.02, 'bkv': jnp.zeros((2 * C,), jnp.float32), 'Wp': jax.random.normal(ks[4], (C, C), jnp.float32) * 0.02, 'bp': jnp.zeros((C,), jnp.float32)}
    _L1_xattn_all = _L1_xattn_setup()
    _L1_xattn_in = {k: v for k, v in _L1_xattn_all.items() if k in ('Wq', 'bq', 'Wkv', 'bkv', 'Wp', 'bp')}
    del _L1_xattn_all

    def _L1_ffn_setup():
        import jax, jax.numpy as jnp
        import numpy as np
        B, S, EMB = (4, 256, 256)
        LAT, HID = (64, 128)
        E, K = (16, 8)
        SCALE = 2.5

        def _w(key, shape, fan_in):
            return jax.random.normal(key, shape, jnp.float32) * fan_in ** (-0.5)

        def _sqrelu(x):
            return jnp.square(jax.nn.relu(x))
        key = jax.random.key(seed)
        ks = jax.random.split(key, 11)
        return {'x': jax.random.normal(ks[0], (B, S, EMB), jnp.float32), 'sw1': _w(ks[1], (HID, EMB), EMB), 'swg': _w(ks[2], (HID, EMB), EMB), 'sw2': _w(ks[3], (EMB, HID), HID), 'rw1': _w(ks[4], (E, HID, LAT), LAT), 'rwg': _w(ks[5], (E, HID, LAT), LAT), 'rw2': _w(ks[6], (E, LAT, HID), HID), 'Wg': _w(ks[7], (E, EMB), EMB), 'Wdown': _w(ks[8], (LAT, EMB), EMB), 'Wup': _w(ks[9], (EMB, LAT), LAT), 'biases': jnp.zeros((E,), jnp.float32)}
    _L1_ffn_all = _L1_ffn_setup()
    _L1_ffn_in = {k: v for k, v in _L1_ffn_all.items() if k in ('sw1', 'swg', 'sw2', 'rw1', 'rwg', 'rw2', 'Wg', 'Wdown', 'Wup', 'biases')}
    del _L1_ffn_all
    return {'x': x, 'itok_BxS_13_99985': itok_BxS_13_99985, 'ctx_2048': ctx_2048, 'L0_ffn_gate_cp': _L0_ffn_in['gate_cp'], 'L0_ffn_up_cp': _L0_ffn_in['up_cp'], 'L0_ffn_down_cp': _L0_ffn_in['down_cp'], 'L1_xattn_Wq': _L1_xattn_in['Wq'], 'L1_xattn_bq': _L1_xattn_in['bq'], 'L1_xattn_Wkv': _L1_xattn_in['Wkv'], 'L1_xattn_bkv': _L1_xattn_in['bkv'], 'L1_xattn_Wp': _L1_xattn_in['Wp'], 'L1_xattn_bp': _L1_xattn_in['bp'], 'L1_ffn_sw1': _L1_ffn_in['sw1'], 'L1_ffn_swg': _L1_ffn_in['swg'], 'L1_ffn_sw2': _L1_ffn_in['sw2'], 'L1_ffn_rw1': _L1_ffn_in['rw1'], 'L1_ffn_rwg': _L1_ffn_in['rwg'], 'L1_ffn_rw2': _L1_ffn_in['rw2'], 'L1_ffn_Wg': _L1_ffn_in['Wg'], 'L1_ffn_Wdown': _L1_ffn_in['Wdown'], 'L1_ffn_Wup': _L1_ffn_in['Wup'], 'L1_ffn_biases': _L1_ffn_in['biases']}

def reference(x, itok_BxS_13_99985, ctx_2048, L0_ffn_gate_cp, L0_ffn_up_cp, L0_ffn_down_cp, L1_xattn_Wq, L1_xattn_bq, L1_xattn_Wkv, L1_xattn_bkv, L1_xattn_Wp, L1_xattn_bp, L1_ffn_sw1, L1_ffn_swg, L1_ffn_sw2, L1_ffn_rw1, L1_ffn_rwg, L1_ffn_rw2, L1_ffn_Wg, L1_ffn_Wdown, L1_ffn_Wup, L1_ffn_biases):
    import jax
    import jax.numpy as jnp

    def _L0_xattn_ref(hidden_states, token_ids, Wg, Wu, Wd):
        import jax, jax.numpy as jnp
        import numpy as np
        B, S, D = (4, 512, 256)
        E = 4
        F = 1024 // E
        VOCAB = 12500
        tokens_per_expert = VOCAB // E
        tid = jnp.clip(token_ids, 0, VOCAB - 1)
        expert_ids = jnp.minimum(tid // tokens_per_expert, E - 1)
        out = jnp.zeros_like(hidden_states)
        for e in range(E):
            g = jax.nn.silu(jnp.einsum('bsd,fd->bsf', hidden_states, Wg[e]))
            u = jnp.einsum('bsd,fd->bsf', hidden_states, Wu[e])
            y = jnp.einsum('bsf,df->bsd', g * u, Wd[e])
            out = jnp.where((expert_ids == e)[..., None], y, out)
        return out

    def _L0_ffn_ref(hidden_states, gate_cp, up_cp, down_cp):
        import jax, jax.numpy as jnp
        import numpy as np
        HIDDEN = 256
        INTER = 1024
        COMPRESSION = 128.9

        def _n_ctrl(out_size, in_size):
            return max(16, int(out_size * in_size / COMPRESSION))

        def _catmull_rom_grid(n_ctrl, n_samples):
            t = np.linspace(0.0, n_ctrl - 1.0, n_samples, dtype=np.float64)
            i = np.clip(np.floor(t).astype(np.int64), 0, n_ctrl - 2)
            f = (t - i).astype(np.float32)
            idx = np.stack([np.clip(i + k, 0, n_ctrl - 1) for k in (-1, 0, 1, 2)], axis=0)
            return (jnp.asarray(idx.astype(np.int32)), jnp.asarray(f))

        def spline_reconstruct(control_points, out_size, in_size):
            n = out_size * in_size
            idx, f = _catmull_rom_grid(control_points.shape[0], n)
            p0, p1, p2, p3 = (control_points[idx[0]], control_points[idx[1]], control_points[idx[2]], control_points[idx[3]])
            f2 = f * f
            f3 = f2 * f
            w = 0.5 * (2.0 * p1 + (p2 - p0) * f + (2.0 * p0 - 5.0 * p1 + 4.0 * p2 - p3) * f2 + (3.0 * p1 - p0 - 3.0 * p2 + p3) * f3)
            return w.reshape(out_size, in_size)
        gate_w = spline_reconstruct(gate_cp, INTER, HIDDEN)
        up_w = spline_reconstruct(up_cp, INTER, HIDDEN)
        down_w = spline_reconstruct(down_cp, HIDDEN, INTER)
        gate = jnp.einsum('bsh,ih->bsi', hidden_states, gate_w)
        up = jnp.einsum('bsh,ih->bsi', hidden_states, up_w)
        inter = jax.nn.silu(gate) * up
        return jnp.einsum('bsi,hi->bsh', inter, down_w)

    def _L1_xattn_ref(x, cond, Wq, bq, Wkv, bkv, Wp, bp):
        import jax, jax.numpy as jnp
        import numpy as np
        D_MODEL = 256
        NUM_HEADS = 16
        HEAD_DIM = D_MODEL // NUM_HEADS

        def _fq_sym(x, axis):
            s = jnp.max(jnp.abs(x), axis=axis, keepdims=True) / 127.0
            s = jnp.maximum(s, 1e-08)
            q = jnp.clip(jnp.round(x / s), -127.0, 127.0) * s
            return x + jax.lax.stop_gradient(q - x)

        def _fq_unsigned(x, axis):
            s = jnp.max(x, axis=axis, keepdims=True) / 255.0
            s = jnp.maximum(s, 1e-08)
            q = jnp.clip(jnp.round(x / s), 0.0, 255.0) * s
            return x + jax.lax.stop_gradient(q - x)
        B, N, C = x.shape
        H, hd = (NUM_HEADS, HEAD_DIM)
        q = (x @ Wq + bq).reshape(1, B * N, H, hd)
        kv = (cond @ Wkv + bkv).reshape(1, -1, 2, H, hd)
        k, v = (kv[:, :, 0], kv[:, :, 1])
        scale = 1.0 / np.sqrt(hd).astype(np.float32)
        q = jnp.transpose(q * scale, (0, 2, 1, 3))
        k = jnp.transpose(k, (0, 2, 1, 3))
        v = jnp.transpose(v, (0, 2, 1, 3))
        q = _fq_sym(q, axis=-1)
        k = _fq_sym(k, axis=-1)
        v = _fq_sym(v, axis=2)
        attn = jnp.einsum('bhqd,bhkd->bhqk', q, k)
        attn = jax.nn.softmax(attn.astype(jnp.float32), axis=-1)
        attn = _fq_unsigned(attn, axis=-1)
        out = jnp.einsum('bhqk,bhkd->bhqd', attn, v)
        out = jnp.transpose(out, (0, 2, 1, 3)).reshape(B, N, C)
        return out @ Wp + bp

    def _L1_ffn_ref(x, sw1, swg, sw2, rw1, rwg, rw2, Wg, Wdown, Wup, biases):
        import jax, jax.numpy as jnp
        import numpy as np
        B, S, EMB = (4, 256, 256)
        LAT, HID = (64, 128)
        E, K = (16, 8)
        SCALE = 2.5

        def _w(key, shape, fan_in):
            return jax.random.normal(key, shape, jnp.float32) * fan_in ** (-0.5)

        def _sqrelu(x):
            return jnp.square(jax.nn.relu(x))
        b, s, d = x.shape
        x2 = x.reshape(-1, d)
        shared = x2 @ sw1.T * _sqrelu(x2 @ swg.T) @ sw2.T
        xl = x2 @ Wdown.T
        probas = jax.nn.sigmoid(x2 @ Wg.T)
        _, idx = jax.lax.top_k(probas + biases, K)
        p = jnp.take_along_axis(probas, idx, axis=-1)
        p = p / p.sum(-1, keepdims=True) * SCALE
        T = x2.shape[0]
        w_dense = jnp.zeros((T, E), x2.dtype).at[jnp.arange(T)[:, None], idx].add(p)
        acc = jnp.zeros_like(xl)
        for e in range(E):
            ye = xl @ rw1[e].T * _sqrelu(xl @ rwg[e].T) @ rw2[e].T
            acc = acc + w_dense[:, e:e + 1] * ye
        out = shared + acc @ Wup.T
        return out.reshape(b, s, d)
    x = x + _L0_xattn_ref(_layernorm(x, axis=-1), itok_BxS_13_99985, ctx_2048, ctx_2048, ctx_2048)
    x = x + _L0_ffn_ref(_layernorm(x, axis=-1), L0_ffn_gate_cp, L0_ffn_up_cp, L0_ffn_down_cp)
    x = x + _L1_xattn_ref(_layernorm(x, axis=-1), ctx_2048, L1_xattn_Wq, L1_xattn_bq, L1_xattn_Wkv, L1_xattn_bkv, L1_xattn_Wp, L1_xattn_bp)
    x = x + _L1_ffn_ref(_layernorm(x, axis=-1), L1_ffn_sw1, L1_ffn_swg, L1_ffn_sw2, L1_ffn_rw1, L1_ffn_rwg, L1_ffn_rw2, L1_ffn_Wg, L1_ffn_Wdown, L1_ffn_Wup, L1_ffn_biases)
    return x

_drawn_inputs = setup_inputs


def setup_inputs(seed=0):
    import zlib

    import numpy as np

    out = dict(_drawn_inputs(seed))
    spreads = {'L1_xattn_bq': (0.0, 2.0),
     'L1_xattn_bkv': (0.0, 0.1),
     'L1_xattn_bp': (0.0, 0.1),
     'L1_ffn_biases': (0.0, 0.1)}
    factors = {'L1_xattn_Wq': 64.0, 'L1_xattn_Wkv': 26.791}
    for name, (base, spread) in spreads.items():
        noise = np.random.default_rng([zlib.crc32(name.encode()), seed]).standard_normal(out[name].shape)
        drawn = base * np.exp(spread * noise) if base else spread * noise
        out[name] = jnp.asarray(drawn.astype(out[name].dtype))
    for name, factor in factors.items():
        out[name] = (out[name] * factor).astype(out[name].dtype)
    return out
```

```python
import math
from contextlib import ExitStack

import numpy as np
import concourse.bass as bass
from concourse import mybir

FP32, FP32R, BF16 = mybir.dt.float32, mybir.dt.float32r, mybir.dt.bfloat16
I32, U16, U8 = mybir.dt.int32, mybir.dt.uint16, mybir.dt.uint8
ACT, ALU, AX = mybir.ActivationFunctionType, mybir.AluOpType, mybir.AxisListType

P = 128
T, D = 1024, 256
NT, NK = T // P, D // P
HALF = 512
NE0 = 4
VOCAB = 12500
INTER = 1024
NC = INTER // P
NCP = int(INTER * D / 128.9)
HEADS, HD = 16, 16
NE, LAT, HID, TOPK = 16, 64, 128, 8
RSCALE = 2.5
EPS = 1e-5
MAGIC = 12582912.0
RING = 4


def spline_tables():
    n = T * D
    t = np.linspace(0.0, NCP - 1.0, n, dtype=np.float64)
    seg = np.clip(np.floor(t).astype(np.int64), 0, NCP - 2).reshape(INTER, 2, P)
    step = (NCP - 1.0) / (n - 1)
    i = np.arange(INTER)
    first = 127 * (i // 64) + 2 * (i % 64)
    cr = 0.5 * np.array([[0, -1, 2, -1], [2, 0, -5, 3], [0, 1, 4, -3], [0, 0, -1, 1]], np.float64)
    a = np.zeros((4, 4, 2, 2, INTER))
    for c in range(2):
        middle = (256.0 * i + 128.0 * c + 63.5) * step
        for side in range(2):
            g = middle - (first - 1 + c + side)
            for q in range(4):
                for p in range(q, 4):
                    a[:, q, side, c] += cr[:, p, None] * math.comb(p, q) * g ** (p - q)
    u = ((np.arange(P) - 63.5) * step)[None, :] ** np.arange(4)[:, None]
    u16 = np.tile(u, (4, 1)).astype(np.float32)
    high = round_12(u16)
    low = round_12((np.tile(u, (4, 1)) - high).astype(np.float32))
    stacked = np.zeros((P, P), np.float32)
    stacked[0:16], stacked[16:32], stacked[32:48], stacked[48:64] = high, low, high, low
    upper = (seg - (first[:, None, None] - 1 + np.arange(2)[None, :, None])).transpose(2, 1, 0)
    assert upper.min() == 0 and upper.max() == 1
    table = np.tile(a.reshape(16, 4, INTER), (4, 1, 1)).astype(np.float32)
    return table, stacked, upper.astype(np.int32)


def round_12(x):
    b = x.view(np.uint32).astype(np.uint64)
    b = (b + 0x7FF + ((b >> 12) & 1)) & 0xFFFFF000
    return b.astype(np.uint32).view(np.float32)


class Chain:

    def __init__(self, eng, sem):
        self.eng, self.sem, self.n, self.loop = eng, sem, 0, 0

    def mark(self, ins):
        ins.then_inc(self.sem, 1)
        self.n += 1

    def wait(self):
        self.eng.wait_ge(self.sem, self.loop + self.n)

    def wait_for(self, n):
        self.eng.wait_ge(self.sem, self.loop + n)

    def link(self, ins):
        self.mark(ins)
        self.wait()


def schedule():
    order = [("norm", 0, n) for n in range(4)]
    order += [("z", j) for j in range(3)] + [("spline", 0)]
    for j in range(16):
        if j + 3 < 16:
            order.append(("z", j + 3))
        order.append(("y", j))
        if 1 + j < 12:
            order.append(("spline", 1 + j))
    order += [("key", n) for n in range(4)] + [("value", n) for n in range(4)]
    order += [("norm", 1, n) for n in range(4)] + [("gu", 16)]
    for j in range(16, 32):
        if j + 1 < 32:
            order.append(("gu", j + 1))
        order.append(("y", j))
        if j == 29:
            order += [("vturn", 0), ("vturn", 1)]
    order += [("norm", 2, n) for n in range(4)] + [("query", n) for n in range(4)]
    order += [("oturn", n) for n in range(4)] + [("proj", n) for n in range(4)]
    order += [("norm", 3, n) for n in range(4)]
    order += [("latent", 0), ("latent", 1), ("router", 0), ("gu", 32), ("gu", 33), ("wturn", 0), ("wturn", 1)]
    return order


BANKS = {"spline": 2, "gu": 2, "y": 0}
ORDER = schedule()
FIRST, _n = {}, 0
for _entry in ORDER:
    FIRST[_entry] = _n
    _n += BANKS.get(_entry[0], 1)
MOE0 = _n
FINAL0 = MOE0 + 4 * NE
KV = range(FIRST[("key", 0)], FIRST[("key", 0)] + 8)
ATTENTION = ORDER.index(("query", 3)) + 1


def drained(n):
    return n + 1 if n < KV[0] else n + 1 - len(KV)


def build(nc, x, ident, ctx_t, tok, cpw, table, stacked, upper, wq, bq, wkv, bkv, bv_t, wp, bp,
          sw1_t, swg_t, sw2_t, rw1_t, rwg_t, rw2_t, wg_t, wdown_t, wup_t, biases, out):
    x_v = x.rearrange("(t p) d -> p t d", p=P)
    out_v = out.rearrange("(t p) d -> p t d", p=P)
    wrow = nc.dram_tensor("router_rows", (NE, T), FP32, kind="Internal").ap()

    es = ExitStack()
    with es:
        limit = nc.sbuf_usable_end
        at = {"": (nc.sbuf_base + 63) // 64 * 64}

        def place(region, name, shape, dt):
            size = int(np.prod(shape[1:])) * {FP32: 4, FP32R: 4, I32: 4, BF16: 2, U16: 2, U8: 1}[dt]
            offset = at[region]
            at[region] = offset + (size + 63) // 64 * 64
            assert at[region] <= limit, (name, at[region], limit)
            return nc.alloc_sbuf_tensor_at(name, shape, dt, offset=offset)

        def sem(name):
            return es.enter_context(nc.semaphore(name))

        X = place("", "X", [P, NT, D], FP32)
        xn = place("", "xn", [P, NT, D], FP32)
        hh = place("", "hh", [P, NK, T], FP32R)
        hl = place("", "hl", [P, NK, T], FP32R)
        idf = place("", "idf", [P, P], FP32)
        idb = place("", "idb", [P, P], BF16)
        NH = 3
        gate_s = [place("", f"gate_s{n}", [P, HALF], FP32) for n in range(NH)]
        prod = [place("", f"prod{n}", [P, HALF], FP32) for n in range(NH)]
        ph = [place("", f"ph{n}", [P, HALF], FP32R) for n in range(NH)]
        pl = [place("", f"pl{n}", [P, HALF], FP32R) for n in range(NH)]
        stats = place("", "stats", [P, NT, 6], FP32)
        mv = place("", "mv", [P, NT, 2], FP32)
        std = place("", "std", [P, NT], FP32)
        rstd = place("", "rstd", [P, NT], FP32)
        eps = place("", "eps", [P, 1], FP32)
        kparts = place("", "kparts", [P, NT, 3, D + HD], BF16)
        vint = place("", "vint", [P, NT, D], BF16)
        sv = place("", "sv", [P, NK], FP32)
        rsv = place("", "rsv", [P, NK], FP32)
        bk = place("", "bk", [P, D], FP32)
        bv = place("", "bv", [P, NK], FP32)
        base = at[""]
        at["A"] = base
        ch = place("A", "ch", [P, NK, T], FP32R)
        cl = place("A", "cl", [P, NK, T], FP32R)
        wkvh = place("A", "wkvh", [P, NK, 2 * D], FP32R)
        wkvl = place("A", "wkvl", [P, NK, 2 * D], FP32R)
        w3h = [place("A", f"w3h{m}", [P, NK, T], FP32R) for m in range(2)]
        w3l = [place("A", f"w3l{m}", [P, NK, T], FP32R) for m in range(2)]
        at["S"] = at["A"]
        dnh = place("A", "dnh", [P, NC, D], FP32R)
        dnl = place("A", "dnl", [P, NC, D], FP32R)
        craw = place("S", "craw", [P, NK, T], FP32)
        wkvraw = place("S", "wkvraw", [P, NK, 2 * D], FP32)
        toki = place("S", "toki", [P, T], I32)
        wraw = [place("A", f"wraw{n}", [P, HALF], FP32) for n in range(2)]
        side = place("A", "side", [P, 2, T], I32)
        u_raw = prod[NH - 1][:, 0:P]
        u_r = place("A", "u_r", [P, P], FP32R)
        mask = [place("A", f"mask{e}", [P, T], BF16) for e in range(NE0)]
        at["K"] = at["A"]
        cps = place("A", "cps", [64, 3, T], FP32)
        tab = place("A", "tab", [64, 4, T], FP32)
        df = [place("A", f"df{n}", [64, HALF], FP32) for n in range(2)]
        dst = [place("A", f"dst{n}", [P, HALF], FP32R) for n in range(4)]
        kraw = place("K", "kraw", [P, NT, D], FP32)
        vt = place("K", "vt", [P, NK, T], FP32)
        kmax = place("K", "kmax", [P, NT * HEADS], FP32)
        ks = place("K", "ks", [P, NT * HEADS], FP32)
        krs = place("K", "krs", [P, NT * HEADS], FP32)
        vround = place("K", "vround", [P, NK, T], BF16)
        at["B"] = base
        qraw = place("B", "qraw", [P, NT, D], FP32)
        qint = place("B", "qint", [P, NT, D + HD], BF16)
        qmax = place("B", "qmax", [P, NT, HEADS], FP32)
        qs = place("B", "qs", [P, NT, HEADS + 1], FP32)
        qrs = place("B", "qrs", [P, NT, HEADS], FP32)
        nqs = place("B", "nqs", [P, NT, HEADS + 1], FP32)
        xq = [place("B", f"xq{n}", [P, NT, P], BF16) for n in range(2)]
        xk = [place("B", f"xk{n}", [P, NT, P], BF16) for n in range(2)]
        qT = [place("B", f"qT{n}", [P, T], BF16) for n in range(2)]
        kT = [place("B", f"kT{n}", [P, T], BF16) for n in range(2)]
        pu = [place("B", f"pu{n}", [P, T], U16) for n in range(4)]
        pT = [place("B", f"pT{n}", [P, T], BF16) for n in range(4)]
        smax = [place("B", f"smax{n}", [P, 2], FP32) for n in range(4)]
        qsh = [place("B", f"qsh{n}", [P, NT], FP32) for n in range(2)]
        nqsh = [place("B", f"nqsh{n}", [P, NT], FP32) for n in range(2)]
        zsum = [place("B", f"zsum{n}", [P, NT], FP32) for n in range(2)]
        rz = [place("B", f"rz{n}", [P, NT], FP32) for n in range(2)]
        O = place("B", "O", [P, NT, D], FP32)
        at["C"] = at["B"]
        wqraw = place("C", "wqraw", [P, NK, D], FP32)
        wqh = place("C", "wqh", [P, NK, D], FP32R)
        wql = place("C", "wql", [P, NK, D], FP32R)
        wpraw = place("C", "wpraw", [P, NK, D], FP32)
        wph = place("C", "wph", [P, NK, D], FP32R)
        wpl = place("C", "wpl", [P, NK, D], FP32R)
        bqb = place("C", "bqb", [P, D], FP32)
        bpb = place("C", "bpb", [P, D], FP32)
        swraw = place("C", "swraw", [P, NK, 2, HID], FP32)
        swh = place("C", "swh", [P, NK, 2, HID], FP32R)
        swl = place("C", "swl", [P, NK, 2, HID], FP32R)
        s2raw = place("C", "s2raw", [P, D], FP32)
        s2h = place("C", "s2h", [P, D], FP32R)
        s2l = place("C", "s2l", [P, D], FP32R)
        wgraw = place("C", "wgraw", [P, NK, NE], FP32)
        wgh = place("C", "wgh", [P, NK, NE], FP32R)
        wgl = place("C", "wgl", [P, NK, NE], FP32R)
        wdraw = place("C", "wdraw", [P, NK, 2 * LAT], FP32)
        wdh = place("C", "wdh", [P, NK, 2 * LAT], FP32R)
        wdl = place("C", "wdl", [P, NK, 2 * LAT], FP32R)
        wuraw = place("C", "wuraw", [P, D], FP32)
        wuh = place("C", "wuh", [P, D], FP32R)
        wul = place("C", "wul", [P, D], FP32R)
        biasb = place("C", "biasb", [P, NE], FP32)
        e1 = place("C", "e1", [P, NE, 2, HID], FP32R)
        e2 = place("C", "e2", [P, NE, 2, LAT], FP32R)
        e1raw = place("C", "e1raw", [P, NE, 2, HID], FP32)
        e2raw = place("C", "e2raw", [P, NE, LAT], FP32)
        e1s = [place("C", f"e1s{n}", [P, 2, HID], FP32R) for n in range(2)]
        e2s = [place("C", f"e2s{n}", [P, 2, LAT], FP32R) for n in range(2)]
        at["D"] = base
        xlh = place("D", "xlh", [P, T], FP32R)
        xll = place("D", "xll", [P, T], FP32R)
        prob = place("D", "prob", [P, NT, NE], FP32)
        pick = place("D", "pick", [P, NT, NE], FP32)
        left = place("D", "left", [P, NT, NE], FP32)
        top8 = place("D", "top8", [P, NT, TOPK], FP32)
        psum8 = place("D", "psum8", [P, NT], FP32)
        wT = place("D", "wT", [NE, T], FP32)
        wb = [place("D", f"wb{n}", [P, T], FP32) for n in range(2)]
        sq = [place("D", f"sq{n}", [P, HALF], FP32)[:, :] for n in range(4)]
        hp = [place("D", f"hp{n}", [P, HALF], FP32)[:, :] for n in range(4)]
        eh = [place("D", f"eh{n}", [P, HALF], FP32R)[:, :] for n in range(4)]
        el = [place("D", f"el{n}", [P, HALF], FP32R)[:, :] for n in range(4)]
        (ah, sh_h), (al, sh_l), res = (hh[:, 0, :], hh[:, 1, :]), (hl[:, 0, :], hl[:, 1, :]), xn
        assert at["D"] <= at["B"], (at["D"], at["B"])

        psum = es.enter_context(nc.psum_tensor("psum", [P, 8, HALF], FP32))
        bank = [psum[:, n, :] for n in range(8)]
        scores = [psum[:, 2 * n:2 * n + 2, :].rearrange("p b k -> p (b k)") for n in range(3)]
        turned = bank[6].bitcast(BF16)
        mixed = bank[7][:, 0:P]

        S = {n: sem(n) for n in (
            "x_in", "ident_in", "identb", "ctx_in", "tok_in", "cp_in", "tab_in", "side_in", "wkv_in", "wq_in", "moe_in",
            "e1_in", "wrow_out", "wb_in0", "wb_in1", "stage_in", "stage_out", "out_done",
            "zeroed", "filled", "drained", "vec_own", "act_own", "summed", "residual",
            "variance", "std_ready", "norm_ready", "norm_high", "ctx_high", "ctx_low", "mask_ready",
            "activated", "masked", "high_ready", "low_ready",
            "control", "control_high", "control_low", "piece_raw", "piece_high", "piece_low",
            "kv_plain", "k_biased", "k_scales", "k_steps", "k_ready", "v_round", "wkv_high", "wkv_low",
            "wq_high", "wq_low", "bp_added", "q_ready", "built", "prepped", "qT_ready", "kT_ready",
            "scored", "maxed", "exped", "turn_done", "evac_v", "evac_a", "mix_done", "head_out",
            "o_high", "moe_high", "moe_low", "e1_low", "latent_high", "latent_low",
            "probs", "weights", "squared", "scaled", "expert_high", "expert_low", "expert_sum",
            "acc_high", "acc_low", "res_ready")}
        block = es.enter_context(nc.Block())
        def half(ap, n):
            return ap[:, n * HALF:(n + 1) * HALF]

        def plain(ap):
            return ap.bitcast(FP32) if ap.dtype == FP32R else ap

        def piece(k, high):
            m, c, h = k // 4, k // 2 % 2, k % 2
            raw = wraw[k % 2][:, :]
            if m < 2:
                return half((w3h if high else w3l)[m][:, c, :], h), raw
            return (dnh if high else dnl)[:, c::2, h * P:(h + 1) * P], raw.rearrange("p (x q) -> p q x", q=4)

        tile_slot = [(1 + t + (t > 5)) % 3 for t in range(NT)]
        prep_slot = (1 + 6) % 3
        assert (NT + 1) % 3 == 0
        PAIR_STEPS = 2 * (NT + 2)

        LOG255 = math.log(255.0)
        MOE_LOADS = 16 * 12

        def expert_halves(eng, step):
            for k in range(4):
                step(k, k // 2, k, True)
            with eng.Fori(1, NE // 2 - 2) as i:
                for u in range(4):
                    step(4 * i + u, 2 * i + u // 2, u, False)
            for k in range(2 * NE - 8, 2 * NE):
                step(k, k // 2, k % 4, False)

        def within(k):
            return not isinstance(k, int) or k < 2 * NE

        LEAD = 3

        @block.sync
        def _(sp):
            def load(dst, src, name):
                sp.dma_start(dst, src).then_inc(S[name], 16)

            def row(v, n):
                return v.rearrange("(a d) -> a d", a=1).broadcast_to((P, n))

            for n in range(2):
                load(X[:, 4 * n:4 * n + 4, :], x_v[:, 4 * n:4 * n + 4, :], "x_in")
            load(craw[:, :, :], ctx_t.rearrange("(k p) t -> p k t", p=P), "ctx_in")
            load(idf[:, :], ident, "ident_in")
            load(u_raw, stacked, "tab_in")
            load(tab[:, :, :], table, "tab_in")
            load(cps[:, :, :], cpw[0], "cp_in")
            load(toki[:, :], row(tok, T), "tok_in")
            load(side[:, :, :], upper, "side_in")
            load(wkvraw[:, :, :], wkv.rearrange("(k p) n -> p k n", p=P), "wkv_in")
            load(bk[:, :], row(bkv[0:D], D), "wkv_in")
            load(bv[:, :], bv_t, "wkv_in")
            for m in range(1, 3):
                sp.wait_ge(S["control"], 8 * m)
                load(cps[:, :, :], cpw[m], "cp_in")
            sp.wait_ge(S["residual"], 2)
            load(wqraw[:, :, :], wq.rearrange("(k p) n -> p k n", p=P), "wq_in")
            load(bqb[:, :], row(bq, D), "wq_in")
            load(wpraw[:, :, :], wp.rearrange("(k p) n -> p k n", p=P), "moe_in")
            load(bpb[:, :], row(bp, D), "moe_in")
            load(swraw[:, :, 0, :], swg_t.rearrange("(k p) n -> p k n", p=P), "moe_in")
            load(swraw[:, :, 1, :], sw1_t.rearrange("(k p) n -> p k n", p=P), "moe_in")
            load(s2raw[:, :], sw2_t, "moe_in")
            load(wgraw[:, :, :], wg_t.rearrange("(k p) n -> p k n", p=P), "moe_in")
            for n in range(2):
                load(wdraw[:, :, n * LAT:(n + 1) * LAT], wdown_t.rearrange("(k p) n -> p k n", p=P), "moe_in")
                load(wuraw[n * LAT:(n + 1) * LAT, :], wup_t, "moe_in")
            load(biasb[:, :], row(biases, NE), "moe_in")
            load(e2raw[:, :, :], rw2_t, "moe_in")
            for n in range(2):
                for m, w in ((0, rwg_t), (1, rw1_t)):
                    load(e1raw[n * LAT:(n + 1) * LAT, :, m, :], w, "e1_in")
            sp.wait_ge(S["drained"], drained(FIRST[("wturn", 1)]))
            sp.dma_start(wrow, wT[:, :]).then_inc(S["wrow_out"], 16)
            sp.wait_ge(S["wrow_out"], 16)

            def spread(e, n, first):
                if not first:
                    sp.wait_ge(S["scaled"], 2 * (e - 1))
                sp.dma_start(wb[n][:, :], wrow[bass.ds(e, 1), :].broadcast_to((P, T))).then_inc(S[f"wb_in{n}"], 16)

            spread(0, 0, True)
            spread(1, 1, True)
            with sp.Fori(1, NE // 2) as i:
                spread(2 * i, 0, False)
                spread(2 * i + 1, 1, False)
            for n in range(4):
                sp.wait_ge(S["res_ready"], n + 1)
                sp.dma_start(out_v[:, 2 * n:2 * n + 2, :], res[:, 2 * n:2 * n + 2, :]).then_inc(S["out_done"], 16)
            sp.wait_ge(S["out_done"], 64)

        @block.gpsimd
        def _(pool):
            pool.memset(eps[:, :], EPS).then_inc(S["zeroed"], 1)
            pool.wait_ge(S["zeroed"], 1)
            for n in range(4):
                pool.memset(dst[n][64:P, :].bitcast(FP32), 0.0).then_inc(S["zeroed"], 1)
            pool.wait_ge(S["ident_in"], 16)
            pool.wait_ge(S["zeroed"], 5)
            pool.tensor_copy(idb[:, :], idf[:, :]).then_inc(S["identb"], 1)

            def control(k):
                m, c, h = k // 4, k // 2 % 2, k % 2
                if k == 0:
                    pool.wait_ge(S["tab_in"], 32)
                if k % 4 == 0:
                    pool.wait_ge(S["cp_in"], 16 * (m + 1))
                for s in range(2):
                    n = 2 * k + s
                    if n >= 2:
                        pool.wait_ge(S["control_low"], n - 1)
                    pool.tensor_tensor(df[n % 2][:, :], half(tab[:, 2 * s + c, :], h),
                                       half(cps[:, c + s, :], h), ALU.mult).then_inc(S["control"], 1)

            pool.wait_ge(S["identb"], 1)
            control(0)
            for entry in ORDER[:ATTENTION]:
                if entry[0] == "z":
                    j = entry[1]
                    if j == 0:
                        pool.wait_ge(S["mask_ready"], 3)
                    pool.wait_ge(S["activated"], j + 1)
                    pool.wait_ge(S["control"], 2 * (1 + max(0, min(11, j - 2))))
                    pool.tensor_tensor(gate_s[j % NH][:, :], gate_s[j % NH][:, :],
                                       half(mask[j // 4][:, :], j % 2), ALU.mult).then_inc(S["masked"], 1)
                elif entry[0] == "spline" and entry[1] + 1 < 12:
                    pool.wait_ge(S["masked"], min(16, 3 + entry[1]))
                    control(entry[1] + 1)
                elif entry == ("norm", 1, 0):
                    pool.wait_ge(S["control"], 24)
                    pool.wait_ge(S["kv_plain"], 4)
                    pool.wait_ge(S["wkv_in"], 48)
                    pool.tensor_tensor(kraw[:, :, :], kraw[:, :, :],
                                       bk[:, :].unsqueeze(1).broadcast_to((P, NT, D)),
                                       ALU.add).then_inc(S["k_biased"], 1)
            kg = kraw[:, :, :].rearrange("p t (h d) -> p (t h) d", d=HD)
            for step, factor in ((1, krs), (2, ks)):
                pool.wait_ge(S["k_scales"], step)
                pool.tensor_tensor(kg, kg, factor[:, :].unsqueeze(2).broadcast_to((P, NT * HEADS, HD)),
                                   ALU.mult).then_inc(S["k_steps"], 1)
            for part in range(2):
                pool.wait_ge(S["k_ready"], part + 1)
                pool.tensor_tensor(kraw[:, :, :], kraw[:, :, :], kparts[:, :, part, 0:D],
                                   ALU.subtract).then_inc(S["k_steps"], 1)
            pool.wait_ge(S["residual"], 2)
            for n in range(2):
                pool.memset(xq[n][:, :, :], 0.0).then_inc(S["zeroed"], 1)
                pool.memset(xk[n][:, :, :], 0.0).then_inc(S["zeroed"], 1)
            pool.memset(qint[:, :, D:], 0.0).then_inc(S["zeroed"], 1)
            pool.memset(kparts[:, :, :, D:], 0.0).then_inc(S["zeroed"], 1)
            pool.memset(qs[:, :, HEADS:], 0.0).then_inc(S["zeroed"], 1)
            pool.memset(nqs[:, :, HEADS:], 0.0).then_inc(S["zeroed"], 1)
            pool.wait_ge(S["zeroed"], 13)
            pool.wait_ge(S["k_ready"], 3)
            pool.wait_ge(S["q_ready"], 4)

            def head(h, n, first):
                if not first:
                    pool.wait_ge(S["prepped"], h - 1)
                    pool.wait_ge(S["exped"], 8 * (h - 1))
                pool.tensor_copy(xq[n][:, :, 0:3 * HD].rearrange("p t (r d) -> p t r d", r=3),
                                 qint[:, :, bass.ds(h * HD, HD)].unsqueeze(2)
                                 .broadcast_to((P, NT, 3, HD))).then_inc(S["built"], 1)
                pool.tensor_copy(xk[n][:, :, 0:3 * HD].rearrange("p t (r d) -> p t r d", r=3),
                                 kparts[:, :, :, bass.ds(h * HD, HD)]).then_inc(S["built"], 1)
                pool.tensor_copy(qsh[n][:, :].unsqueeze(2), qs[:, :, bass.ds(h, 1)]).then_inc(S["built"], 1)
                pool.tensor_copy(nqsh[n][:, :].unsqueeze(2), nqs[:, :, bass.ds(h, 1)]).then_inc(S["built"], 1)

            head(0, 0, True)
            head(1, 1, True)
            pool.wait_ge(S["norm_ready"], 24)
            pool.wait_ge(S["moe_in"], MOE_LOADS)
            pool.tensor_tensor(X[:, :, :], X[:, :, :], bpb[:, :].unsqueeze(1).broadcast_to((P, NT, D)),
                               ALU.add).then_inc(S["bp_added"], 1)

            def low(dst_ap, raw, high, n, name):
                pool.wait_ge(S["moe_high"], n)
                pool.tensor_tensor(dst_ap, raw, plain(high), ALU.subtract).then_inc(S[name], 1)

            low(wpl[:, :, :], wpraw[:, :, :], wph[:, :, :], 1, "moe_low")
            low(swl[:, :, :, :].rearrange("p k m n -> p (k m n)"), swraw[:, :, :, :].rearrange("p k m n -> p (k m n)"),
                swh[:, :, :, :].rearrange("p k m n -> p (k m n)"), 2, "moe_low")
            low(s2l[:, :], s2raw[:, :], s2h[:, :], 3, "moe_low")
            low(wgl[:, :, :], wgraw[:, :, :], wgh[:, :, :], 4, "moe_low")
            low(wdl[:, :, :], wdraw[:, :, :], wdh[:, :, :], 5, "moe_low")
            low(wul[:, :], wuraw[:, :], wuh[:, :], 6, "moe_low")
            low(e2[:, :, 1, :], e2raw[:, :, :], e2[:, :, 0, :], 7, "moe_low")
            head(2, 0, False)
            head(3, 1, False)
            pool.wait_ge(S["built"], 16)
            for g in range(4):
                rows = e1[LAT:P, 4 * g:4 * g + 4, :, :].rearrange("p e m n -> p (e m n)")
                low(rows, e1raw[LAT:P, 4 * g:4 * g + 4, :, :].rearrange("p e m n -> p (e m n)"), rows, 8 + g, "e1_low")
            pool.wait_ge(S["e1_low"], 4)
            with pool.Fori(2, HEADS // 2) as i:
                head(2 * i, 0, False)
                head(2 * i + 1, 1, False)
            head(HEADS, 0, False)

            def scale(k, e, u, first):
                if u % 2 == 0:
                    pool.wait_ge(S[f"wb_in{u // 2}"], 8 * (e - u // 2) + 16)
                pool.wait_ge(S["drained"], drained(MOE0) + 2 * k + 1)
                pool.tensor_tensor(hp[u], hp[u], half(wb[u // 2][:, :], u % 2), ALU.mult).then_inc(S["scaled"], 1)

            expert_halves(pool, scale)

        @block.scalar
        def _(act):
            def copy(o, i, name, **k):
                act.activation(o, i, ACT.Copy, **k).then_inc(S[name], 1)

            act.wait_ge(S["ctx_in"], 16)
            copy(ch[:, :, :], craw[:, :, :], "ctx_high")
            act.wait_ge(S["tab_in"], 32)
            copy(u_r[:, :], u_raw, "ctx_high")

            def controls(k):
                for n in (2 * k, 2 * k + 1):
                    act.wait_ge(S["control"], n + 1)
                    if n >= 4:
                        act.wait_ge(S["filled"], FIRST[("spline", k - 2)] + 2)
                    copy(dst[n % 4][0:64, :], df[n % 2][:, :], "control_high")

            def product_done(j):
                return drained(FIRST[("z", j)] if j < 16 else FIRST[("gu", j)] + 1)

            def highs(j):
                act.wait_ge(S["drained"], product_done(j))
                if j >= NH:
                    act.wait_ge(S["low_ready"], j - NH + 1)
                    act.wait_ge(S["summed"], j - NH + 1)
                copy(ph[j % NH][:, :], prod[j % NH][:, :], "high_ready")

            def root(layer):
                act.wait_ge(S["variance"], layer + 1)
                if layer == 0:
                    act.wait_ge(S["zeroed"], 1)
                act.activation(std[:, :], mv[:, :, 1], ACT.Sqrt, bias=eps[:, :]).then_inc(S["std_ready"], 1)

            def gates(j, n, func):
                act.wait_ge(S["filled"], n + 1)
                if j >= NH:
                    act.wait_ge(S["drained"], product_done(j - NH))
                act.activation(gate_s[j % NH][:, :], bank[n % RING], func).then_inc(S["activated"], 1)

            def norm_highs(entry):
                n, q = FIRST[entry], entry[2]
                act.wait_ge(S["filled"], n + 1)
                copy(half(hh[:, q % 2, :], q // 2), bank[n % RING], "norm_high")

            root(0)
            controls(0)
            for entry in ORDER[:ATTENTION]:
                kind, n = entry[0], FIRST[entry]
                if kind == "norm":
                    layer, q = entry[1:]
                    if q == 0 and layer:
                        root(layer)
                        if layer == 2:
                            act.wait_ge(S["wq_in"], 32)
                            copy(wqh[:, :, :], wqraw[:, :, :], "wq_high")
                    norm_highs(entry)
                elif kind in ("z", "gu"):
                    j = entry[1]
                    gates(j, n, ACT.Silu)
                    if 0 < j < 16:
                        highs(j - 1)
                    if j >= 15:
                        highs(j)
                elif kind == "spline":
                    k = entry[1]
                    act.wait_ge(S["filled"], n + 1)
                    if k >= 2:
                        act.wait_ge(S["piece_low"], k - 1)
                    copy(wraw[k % 2][:, :], bank[n % RING], "piece_raw")
                    if k + 1 < 12:
                        controls(k + 1)
                    act.wait_ge(S["drained"], drained(n + 1))
                    if k == 8:
                        act.wait_ge(S["ctx_low"], 1)
                        act.wait_ge(S["wkv_low"], 1)
                        act.wait_ge(S["mask_ready"], 3)
                    copy(*piece(k, True), "piece_high")
                    if k == 2:
                        act.wait_ge(S["wkv_in"], 48)
                        copy(wkvh[:, :, :], wkvraw[:, :, :], "wkv_high")
                elif kind in ("key", "value"):
                    q = entry[1]
                    act.wait_ge(S["filled"], n + 1)
                    if kind == "key":
                        if q == 0:
                            act.wait_ge(S["control_low"], 24)
                            act.wait_ge(S["filled"], FIRST[("spline", 11)] + 2)
                        copy(kraw[:, 2 * q:2 * q + 2, :].rearrange("p t d -> p (t d)"), bank[n % RING], "kv_plain")
                    else:
                        act.activation(half(vt[:, q // 2, :], q % 2), bank[n % RING], ACT.Identity,
                                       bias=bv[:, q // 2:q // 2 + 1]).then_inc(S["kv_plain"], 1)

            act.wait_ge(S["moe_in"], MOE_LOADS)
            copy(wph[:, :, :], wpraw[:, :, :], "moe_high")
            copy(swh[:, :, :, :].rearrange("p k m n -> p (k m n)"), swraw[:, :, :, :].rearrange("p k m n -> p (k m n)"),
                 "moe_high")
            copy(s2h[:, :], s2raw[:, :], "moe_high")
            copy(wgh[:, :, :], wgraw[:, :, :], "moe_high")
            copy(wdh[:, :, :], wdraw[:, :, :], "moe_high")
            copy(wuh[:, :], wuraw[:, :], "moe_high")
            copy(e2[:, :, 0, :], e2raw[:, :, :], "moe_high")

            def key_turn(h, n):
                act.wait_ge(S["prepped"], h + 1)
                copy(kT[n][:, :], bank[2 * prep_slot + 1].bitcast(BF16), "kT_ready")

            def head_scalar(h, n, first, g0):
                for t in range(NT):
                    g = g0 + t
                    if not (first and n == 0 and t < 4):
                        act.wait_ge(S["turn_done"], g - 3)
                    if t == 0 and not first:
                        act.wait_ge(S["head_out"], h - 1)
                    act.wait_ge(S["maxed"], g + 1)
                    act.activation(pu[t % 4][:, :], scores[tile_slot[t]], ACT.Exp, bias=smax[t % 4][:, 1:2],
                                   scale=qsh[n][:, t:t + 1], accum_out=zsum[n][:, t:t + 1]).then_inc(S["exped"], 1)
                    if t == 5:
                        key_turn(h + 1, 1 - n)
                    if t % 2 and not (first and n == 0 and t == 1):
                        evac_scalar(g - 2, (t - 2) % 8, first and n == 0 and t < 7)

            def evac_scalar(g, t, fresh):
                act.wait_ge(S["turn_done"], g + 1)
                if not fresh:
                    act.wait_ge(S["mix_done"], g - 3)
                copy(pT[t % 4][:, :], turned.bitcast(U16), "evac_a")

            act.wait_ge(S["prepped"], 1)
            copy(kT[0][:, :], bank[2 * prep_slot + 1].bitcast(BF16), "kT_ready")
            head_scalar(0, 0, True, 0)
            act.wait_ge(S["e1_in"], 64)
            for g in range(4):
                copy(e1[:, 4 * g:4 * g + 4, :, :].rearrange("p e m n -> p (e m n)"),
                     e1raw[:, 4 * g:4 * g + 4, :, :].rearrange("p e m n -> p (e m n)"), "moe_high")
            head_scalar(1, 1, True, 8)
            with act.Fori(1, HEADS // 2) as i:
                head_scalar(2 * i, 0, False, 16 * i)
                head_scalar(2 * i + 1, 1, False, 16 * i + 8)
            evac_scalar(8 * HEADS - 1, 7, False)

            for q in range(4):
                n = FIRST[("oturn", q)]
                act.wait_ge(S["filled"], n + 1)
                copy(half(hh[:, q % 2, :], q // 2), bank[n % RING], "o_high", scale=sv[:, q % 2:q % 2 + 1])
            root(3)
            for q in range(4):
                norm_highs(("norm", 3, q))
            act.wait_ge(S["built"], 4 * (HEADS + 1))
            for q in range(2):
                n = FIRST[("latent", q)]
                act.wait_ge(S["filled"], n + 1)
                copy(half(xlh[:, :], q), bank[n % RING], "latent_high")
            n = FIRST[("router", 0)]
            act.wait_ge(S["filled"], n + 1)
            act.activation(prob[:, :, :].rearrange("p t e -> p (t e)"), bank[n % RING][:, 0:P], ACT.Sigmoid)\
               .then_inc(S["probs"], 1)
            for q in range(2):
                j, n = 32 + q, FIRST[("gu", 32 + q)]
                gates(j, n, ACT.Relu)
                act.wait_ge(S["activated"], j + 1)
                act.activation(gate_s[j % NH][:, :], gate_s[j % NH][:, :], ACT.Square).then_inc(S["squared"], 1)
            act.wait_ge(S["filled"], FIRST[("gu", 33)] + 2)
            for q in range(2):
                act.wait_ge(S["drained"], drained(FIRST[("gu", 32 + q)] + 1))
                copy(half(sh_h, q), prod[(32 + q) % NH][:, :], "high_ready")

            def rectify(k, u, first):
                act.wait_ge(S["filled"], MOE0 + 2 * k + 1)
                if not first:
                    act.wait_ge(S["drained"], drained(MOE0) + 2 * (k - 4) + 1)
                act.activation(sq[u], bank[(MOE0 + 2 * u) % RING], ACT.Relu).then_inc(S["act_own"], 1)
                act.wait_ge(S["act_own"], k + 1)
                act.activation(sq[u], sq[u], ACT.Square).then_inc(S["squared"], 1)

            def expert_scalar(k, e, u, first):
                act.wait_ge(S["scaled"], k + 1)
                if not first:
                    act.wait_ge(S["expert_low"], k - 3)
                    act.wait_ge(S["expert_sum"], k - 3)
                copy(eh[u], hp[u], "expert_high")
                if within(k + LEAD):
                    rectify(k + LEAD, (u + LEAD) % 4, first and u + LEAD < 4)

            for k in range(LEAD):
                rectify(k, k, True)
            expert_halves(act, expert_scalar)
            for h in range(2):
                act.wait_ge(S["expert_sum"], 2 * NE)
                copy(half(ah, h), bank[4 + h], "acc_high")

        @block.vector
        def _(dve):
            own = Chain(dve, S["vec_own"])

            def sub(o, a, b, name, k=1):
                dve.tensor_tensor(o, plain(a), plain(b), ALU.subtract).then_inc(S[name], k)

            def norm(layer):
                if layer == 0:
                    dve.wait_ge(S["x_in"], 32)
                for t in range(NT):
                    own.mark(dve.bn_stats(stats[:, t, :], X[:, t, :]))
                own.wait()
                for t in range(NT):
                    ins = dve.bn_aggr(mv[:, t, :], stats[:, t, :])
                ins.then_inc(S["variance"], 1)
                dve.wait_ge(S["std_ready"], layer + 1)
                own.link(dve.reciprocal(rstd[:, :], std[:, :]))
                for t in range(NT):
                    dve.tensor_scalar(xn[:, t, :], X[:, t, :], mv[:, t, 0:1], rstd[:, t:t + 1],
                                      ALU.subtract, ALU.mult).then_inc(S["norm_ready"], 1)

            def norm_lows(entry):
                n, (layer, q) = FIRST[entry], entry[1:]
                dve.wait_ge(S["norm_high"], 4 * layer + q + 1)
                sub(half(hl[:, q % 2, :], q // 2), bank[n % RING], half(hh[:, q % 2, :], q // 2), "drained")

            def product(j, n, b):
                if j < 16:
                    dve.wait_ge(S["masked"], j + 1)
                elif j < 32:
                    dve.wait_ge(S["activated"], j + 1)
                    dve.wait_ge(S["filled"], n + 2)
                else:
                    dve.wait_ge(S["squared"], j - 31)
                    dve.wait_ge(S["filled"], n + 2)
                if j >= NH:
                    dve.wait_ge(S["high_ready"], j - NH + 1)
                    dve.wait_ge(S["low_ready"], j - NH + 1)
                dve.tensor_tensor(prod[j % NH][:, :], gate_s[j % NH][:, :], bank[b % RING],
                                  ALU.mult).then_inc(S["drained"], 1 + b - n)

            def lows(j):
                dve.wait_ge(S["high_ready"], j + 1)
                if j >= NH:
                    dve.wait_ge(S["summed"], j - NH + 1)
                sub(pl[j % NH][:, :], prod[j % NH][:, :], ph[j % NH][:, :], "low_ready")

            def add_sums(layer):
                dve.wait_ge(S["summed"], 16 * (layer + 1))
                for b in range(4):
                    o = X[:, 2 * b:2 * b + 2, :].rearrange("p t d -> p (t d)")
                    ins = dve.tensor_tensor(o, o, bank[4 + b], ALU.add)
                    own.mark(ins) if b < 3 else ins.then_inc(S["residual"], 1)
                own.wait()
                dve.wait_ge(S["residual"], layer + 1)

            def masks():
                dve.wait_ge(S["tok_in"], 16)
                per = VOCAB // NE0
                for e in range(1, NE0):
                    own.mark(dve.tensor_scalar(mask[e][:, :], toki[:, :], float(per * e), None, ALU.is_ge))
                own.wait()
                dve.tensor_scalar(mask[0][:, :], mask[1][:, :], -1.0, 1.0, ALU.mult, ALU.add).then_inc(S["mask_ready"], 1)
                dve.wait_ge(S["mask_ready"], 1)
                for e in range(1, NE0 - 1):
                    sub(mask[e][:, :], mask[e][:, :], mask[e + 1][:, :], "mask_ready")
                    dve.wait_ge(S["mask_ready"], 1 + e)

            def control_lows(k):
                for n in (2 * k, 2 * k + 1):
                    dve.wait_ge(S["control_high"], n + 1)
                    d = dst[n % 4][32:64, :]
                    sub(d, df[n % 2][32:64, :], d, "control_low")

            def key_value_steps():
                kg = kraw[:, :, :].rearrange("p t (h d) -> p (t h) d", d=HD)
                kf = kraw[:, :, :].rearrange("p t d -> p (t d)")
                dve.wait_ge(S["k_biased"], 1)
                own.link(dve.tensor_reduce(kmax[:, :], kg, AX.X, ALU.max, apply_absolute_value=True))
                own.link(dve.tensor_scalar(ks[:, :], kmax[:, :], 1.0 / 127.0, 1e-8, ALU.mult, ALU.max))
                dve.reciprocal(krs[:, :], ks[:, :]).then_inc(S["k_scales"], 1)
                yield
                dve.wait_ge(S["kv_plain"], 8)
                own.link(dve.tensor_reduce(sv[:, :], vt[:, :, :], AX.X, ALU.max, apply_absolute_value=True))
                own.link(dve.tensor_scalar(sv[:, :], sv[:, :], 1.0 / 127.0, 1e-8, ALU.mult, ALU.max))
                own.link(dve.reciprocal(rsv[:, :], sv[:, :]))
                yield
                dve.wait_ge(S["k_steps"], 1)
                dve.tensor_scalar(kf, kf, MAGIC, -MAGIC, ALU.add, ALU.add).then_inc(S["k_scales"], 1)
                yield
                for part in range(3):
                    if part < NK:
                        k = part
                        own.link(dve.tensor_scalar(vt[:, k, :], vt[:, k, :], rsv[:, k:k + 1], MAGIC, ALU.mult, ALU.add))
                        dve.tensor_scalar(vround[:, k, :], vt[:, k, :], -MAGIC, None, ALU.add).then_inc(S["v_round"], 1)
                    yield
                    dve.wait_ge(S["k_steps"], part + 2)
                    dve.tensor_copy(kparts[:, :, part, 0:D], kraw[:, :, :]).then_inc(S["k_ready"], 1)
                    yield

            norm(0)
            dve.wait_ge(S["ctx_high"], 1)
            sub(cl[:, :, :], craw[:, :, :], ch[:, :, :], "ctx_low")
            kv = key_value_steps()
            for entry in ORDER[:ATTENTION]:
                kind, n = entry[0], FIRST[entry]
                if kind == "norm":
                    layer, q = entry[1:]
                    if q == 0 and layer:
                        add_sums(layer - 1)
                        norm(layer)
                        if layer == 2:
                            dve.wait_ge(S["wq_high"], 1)
                            sub(wql[:, :, :], wqraw[:, :, :], wqh[:, :, :], "wq_low")
                    norm_lows(entry)
                    if q == 3 and layer == 0:
                        masks()
                        control_lows(0)
                elif kind == "z":
                    j = entry[1]
                    product(j, n, n)
                    if j:
                        lows(j - 1)
                    if j == 15:
                        lows(j)
                elif kind == "gu":
                    j = entry[1]
                    product(j, n, n + 1)
                    lows(j)
                    next(kv, None)
                elif kind == "spline":
                    k = entry[1]
                    if k == 0:
                        dve.wait_ge(S["side_in"], 16)
                    dve.wait_ge(S["piece_raw"], k + 1)
                    dve.wait_ge(S["filled"], n + 2)
                    c, h = k // 2 % 2, k % 2
                    dve.copy_predicated(wraw[k % 2][:, :], half(side[:, c, :], h),
                                        bank[(n + 1) % RING]).then_inc(S["drained"], 2)
                    if k + 1 < 12:
                        control_lows(k + 1)
                    dve.wait_ge(S["piece_high"], k + 1)
                    o, raw = piece(k, False)
                    sub(o, raw, piece(k, True)[0], "piece_low")
                    if k == 2:
                        dve.wait_ge(S["wkv_high"], 1)
                        sub(wkvl[:, :, :], wkvraw[:, :, :], wkvh[:, :, :], "wkv_low")
                elif kind == "vturn":
                    k = entry[1]
                    if k == 0:
                        for _ in kv:
                            pass
                    dve.wait_ge(S["filled"], n + 1)
                    dve.tensor_copy(vint[:, :, k * P:(k + 1) * P],
                                    bank[n % RING].bitcast(BF16).rearrange("p (t d) -> p t d", t=NT))\
                       .then_inc(S["drained"], 1)
                elif kind == "query":
                    q = entry[1]
                    t2 = slice(2 * q, 2 * q + 2)
                    qf = qraw[:, t2, :].rearrange("p t d -> p (t d)")
                    qg = qraw[:, t2, :].rearrange("p t (h d) -> p (t h) d", d=HD)
                    if q == 0:
                        dve.wait_ge(S["wq_in"], 32)
                        dve.wait_ge(S["zeroed"], 13)
                    dve.wait_ge(S["filled"], n + 1)
                    dve.tensor_tensor(qraw[:, t2, :], bank[n % RING].rearrange("p (t d) -> p t d", t=2),
                                      bqb[:, :].unsqueeze(1).broadcast_to((P, 2, D)), ALU.add).then_inc(S["drained"], 1)
                    dve.wait_ge(S["drained"], drained(n))
                    own.link(dve.tensor_reduce(qmax[:, t2, :], qg.rearrange("p (t h) d -> p t h d", t=2),
                                               AX.X, ALU.max, apply_absolute_value=True))
                    own.link(dve.tensor_scalar(qs[:, t2, 0:HEADS], qmax[:, t2, :], 0.25 / 127.0, 1e-8, ALU.mult, ALU.max))
                    own.mark(dve.tensor_scalar(nqs[:, t2, 0:HEADS], qs[:, t2, 0:HEADS], -1.0, None, ALU.mult))
                    own.link(dve.reciprocal(qrs[:, t2, :], qs[:, t2, 0:HEADS]))
                    own.link(dve.tensor_scalar(qrs[:, t2, :], qrs[:, t2, :], 0.25, None, ALU.mult))
                    own.link(dve.tensor_tensor(qg, qg, qrs[:, t2, :].rearrange("p t h -> p (t h)").unsqueeze(2)
                                               .broadcast_to((P, 2 * HEADS, HD)), ALU.mult))
                    dve.tensor_scalar(qint[:, t2, 0:D], qraw[:, t2, :], MAGIC, -MAGIC,
                                      ALU.add, ALU.add).then_inc(S["q_ready"], 1)

            def evac_vector(g, t, fresh):
                dve.wait_ge(S["turn_done"], g + 1)
                if not fresh:
                    dve.wait_ge(S["mix_done"], g - 3)
                dve.tensor_copy(pT[t % 4][:, :], turned.bitcast(U16)).then_inc(S["evac_v"], 1)

            def head_scale(h, n):
                dve.wait_ge(S["exped"], 8 * (h + 1))
                own.link(dve.reciprocal(rz[n][:, :], zsum[n][:, :]))
                own.mark(dve.tensor_scalar(rz[n][:, :], rz[n][:, :], 1e-8, None, ALU.max))

            def head_output(h, n):
                dve.wait_ge(S["mix_done"], 8 * h + 8)
                dve.tensor_tensor(O[:, :, bass.ds(h * HD, HD)], mixed.rearrange("p (t d) -> p t d", t=NT),
                                  rz[n][:, :].unsqueeze(2).broadcast_to((P, NT, HD)), ALU.mult).then_inc(S["head_out"], 1)

            def head_vector(h, n, first, g0):
                begin = first and n == 0
                dve.wait_ge(S["built"], 4 * h + 4)
                for t in range(NT):
                    g = g0 + t
                    dve.wait_ge(S["scored"], g + 1)
                    if not (first and n == 0 and t < 4):
                        dve.wait_ge(S["exped"], g - 3)
                    own.mark(dve.reduce_max(smax[t % 4][:, 0:1], scores[tile_slot[t]], AX.X))
                    read = own.n
                    if t == 2 and not begin:
                        head_scale(h - 1, 1 - n)
                    if t == 6:
                        dve.wait_ge(S["prepped"], h + 2)
                        dve.tensor_copy(qT[1 - n][:, :], bank[2 * prep_slot].bitcast(BF16)).then_inc(S["qT_ready"], 1)
                    own.wait_for(read)
                    dve.tensor_scalar(smax[t % 4][:, 1:2], smax[t % 4][:, 0:1], nqsh[n][:, t:t + 1], LOG255,
                                      ALU.mult, ALU.add).then_inc(S["maxed"], 1)
                    if t % 2 and not (begin and t == 1):
                        evac_vector(g - 3, (t - 3) % 8, begin and t < 7)
                    if t == 3 and not begin:
                        own.wait()
                        head_output(h - 1, 1 - n)

            dve.wait_ge(S["prepped"], 1)
            dve.tensor_copy(qT[0][:, :], bank[2 * prep_slot].bitcast(BF16)).then_inc(S["qT_ready"], 1)
            head_vector(0, 0, True, 0)
            head_vector(1, 1, True, 8)
            before = own.n
            with dve.Fori(1, HEADS // 2) as i:
                own.loop = (i - 1) * PAIR_STEPS
                head_vector(2 * i, 0, False, 16 * i)
                head_vector(2 * i + 1, 1, False, 16 * i + 8)
            assert own.n - before == PAIR_STEPS
            own.n, own.loop = before + (HEADS // 2 - 1) * PAIR_STEPS, 0
            evac_vector(8 * HEADS - 2, 6, False)
            head_scale(HEADS - 1, 1)
            own.wait()
            head_output(HEADS - 1, 1)

            for q in range(4):
                n = FIRST[("oturn", q)]
                dve.wait_ge(S["o_high"], q + 1)
                dve.scalar_tensor_tensor(half(hl[:, q % 2, :], q // 2), bank[n % RING], sv[:, q % 2:q % 2 + 1],
                                         plain(half(hh[:, q % 2, :], q // 2)), ALU.mult, ALU.subtract).then_inc(S["drained"], 1)
            dve.wait_ge(S["bp_added"], 1)
            for q in range(4):
                n = FIRST[("proj", q)]
                dve.wait_ge(S["filled"], n + 1)
                o = X[:, 2 * q:2 * q + 2, :].rearrange("p t d -> p (t d)")
                dve.tensor_tensor(o, o, bank[n % RING], ALU.add).then_inc(S["drained"], 1)
            dve.wait_ge(S["drained"], drained(FIRST[("proj", 3)]))
            norm(3)
            for q in range(4):
                norm_lows(("norm", 3, q))
            for q in range(2):
                n = FIRST[("latent", q)]
                dve.wait_ge(S["latent_high"], q + 1)
                sub(half(xll[:, :], q), bank[n % RING], half(xlh[:, :], q), "drained")
            def stage_in(e, n, first):
                if not first:
                    dve.wait_ge(S["filled"], MOE0 + 4 * (e - 1))
                dve.tensor_copy(e1s[n][:, :, :], plain(e1[:, bass.ds(e, 1), :, :].rearrange("p o a b -> p (o a) b")))\
                   .then_inc(S["stage_in"], 1)

            def stage_out(e, n, first):
                if not first:
                    dve.wait_ge(S["expert_sum"], 2 * (e - 1))
                dve.tensor_copy(e2s[n][:, :, :], plain(e2[:, bass.ds(e, 1), :, :].rearrange("p o a b -> p (o a) b")))\
                   .then_inc(S["stage_out"], 1)

            dve.wait_ge(S["e1_low"], 4)
            dve.wait_ge(S["moe_low"], 7)
            for n in range(2):
                stage_in(n, n, True)
                stage_out(n, n, True)
            dve.wait_ge(S["probs"], 1)
            own.link(dve.tensor_tensor(pick[:, :, :], prob[:, :, :], biasb[:, :].unsqueeze(1).broadcast_to((P, NT, NE)), ALU.add))
            for t in range(NT):
                own.mark(dve.max(top8[:, t, :], pick[:, t, :]))
            own.wait()
            for t in range(NT):
                own.mark(dve.match_replace(left[:, t, :], top8[:, t, :], pick[:, t, :], -3.0e38))
            own.wait()
            own.link(dve.tensor_tensor(pick[:, :, :], pick[:, :, :], left[:, :, :], ALU.not_equal))
            own.link(dve.tensor_tensor(prob[:, :, :], prob[:, :, :], pick[:, :, :], ALU.mult))
            own.link(dve.reduce_sum(psum8[:, :], prob[:, :, :], AX.X))
            own.link(dve.reciprocal(psum8[:, :], psum8[:, :]))
            own.link(dve.tensor_scalar(psum8[:, :], psum8[:, :], RSCALE, None, ALU.mult))
            dve.tensor_tensor(prob[:, :, :], prob[:, :, :], psum8[:, :].unsqueeze(2).broadcast_to((P, NT, NE)),
                              ALU.mult).then_inc(S["drained"], 1)
            for q in range(2):
                n = FIRST[("gu", 32 + q)]
                product(32 + q, n, n + 1)
            for q in range(2):
                j = 32 + q
                dve.wait_ge(S["high_ready"], j + 1)
                sub(half(sh_l, q), prod[j % NH][:, :], half(sh_h, q), "low_ready")
            for q in range(2):
                n = FIRST[("wturn", q)]
                dve.wait_ge(S["filled"], n + 1)
                dve.tensor_copy(half(wT[:, :], q), bank[n % RING][0:NE, :]).then_inc(S["drained"], 1)

            def hidden(k, u, first):
                dve.wait_ge(S["squared"], 2 + k + 1)
                dve.wait_ge(S["filled"], MOE0 + 2 * k + 2)
                if not first:
                    dve.wait_ge(S["expert_high"], k - 3)
                    dve.wait_ge(S["expert_low"], k - 3)
                dve.tensor_tensor(hp[u], sq[u], bank[(MOE0 + 2 * u + 1) % RING], ALU.mult).then_inc(S["drained"], 2)

            def expert_vector(k, e, u, first):
                if u % 2 and within(k + 2) and not (first and u == 1):
                    stage_out(e + 1, 1 - u // 2, False)
                dve.wait_ge(S["expert_high"], k + 1)
                if not first:
                    dve.wait_ge(S["expert_sum"], k - 3)
                sub(el[u], hp[u], eh[u], "expert_low")
                if within(k + LEAD):
                    hidden(k + LEAD, (u + LEAD) % 4, first and u + LEAD < 4)
                if u % 2 == 0 and within(k + 6):
                    stage_in(e + 3, 1 - u // 2, False)

            for k in range(LEAD):
                hidden(k, k, True)
                if k == 1:
                    stage_in(2, 0, False)
            expert_halves(dve, expert_vector)
            for h in range(2):
                dve.wait_ge(S["acc_high"], h + 1)
                sub(half(al, h), bank[4 + h], half(ah, h), "acc_low")
            for q in range(4):
                dve.wait_ge(S["filled"], FINAL0 + q + 1)
                o = (slice(None), slice(2 * q, 2 * q + 2), slice(None))
                dve.tensor_tensor(res[o].rearrange("p t d -> p (t d)"), X[o].rearrange("p t d -> p (t d)"),
                                  bank[(FINAL0 + q) % RING], ALU.add).then_inc(S["res_ready"], 1)

        @block.tensor
        def _(pe):
            def free(n, count=1):
                for b in range(n, n + count):
                    if b >= RING:
                        last = b - RING
                        if last in KV:
                            pe.wait_ge(S["kv_plain"], last - KV[0] + 1)
                        else:
                            pe.wait_ge(S["drained"], drained(last))

            def mm3(o, lhs, rhs, start, stop, group=True):
                pe.matmul(o, lhs[0], rhs[0], start=start, stop=False, skip_group_check=not group)
                pe.matmul(o, lhs[0], rhs[1], start=False, stop=False, skip_group_check=not group)
                return pe.matmul(o, lhs[1], rhs[0], start=False, stop=stop, skip_group_check=not group)

            def both(h, l, *ix):
                return h[ix], l[ix]

            ALL = slice(None)

            def cols(a, n=P):
                return slice(a, a + n)

            def normal(k, h):
                return both(hh, hl, ALL, k, cols(h * HALF, HALF))

            def norm_turns(entry, src):
                n, q = FIRST[entry], entry[-1]
                free(n)
                k, h = q % 2, q // 2
                for t in range(4):
                    mm = pe.transpose(bank[n % RING][:, t * P:(t + 1) * P], src[:, 4 * h + t, k * P:(k + 1) * P], idf[:, :])
                mm.then_inc(S["filled"], 1)

            def projected(n, o_lhs, o_rhs, extra=None):
                free(n)
                for t in range(2):
                    o = bank[n % RING][:, t * D:(t + 1) * D]
                    for k in range(NK):
                        mm = mm3(o, o_lhs(k, t), o_rhs(k), k == 0, k == NK - 1)
                mm.then_inc(S["filled"], 1)

            def sums(j, lhs, rhs, first, last):
                pe.wait_ge(S["low_ready"], j + 1)
                pe.wait_ge(S["high_ready"], j + 1)
                for t in range(4):
                    tile = 4 * (j % 2) + t
                    o = bank[4 + tile // 2][:, (tile % 2) * D:(tile % 2 + 1) * D]
                    mm = mm3(o, lhs(t), rhs, first and tile % 2 == 0, last, group=False)
                mm.then_inc(S["summed"], 1)

            def hidden_parts(j):
                return lambda t: both(ph[j % NH], pl[j % NH], ALL, cols(t * P))

            pe.wait_ge(S["ident_in"], 16)
            for entry in ORDER[:ATTENTION]:
                kind, n = entry[0], FIRST[entry]
                if kind == "norm":
                    layer, q = entry[1:]
                    pe.wait_ge(S["norm_ready"], 8 * layer + 4 * (q // 2 + 1))
                    norm_turns(entry, xn)
                elif kind == "z":
                    j = entry[1]
                    e, f, h = j // 4, j // 2 % 2, j % 2
                    if j == 0:
                        pe.wait_ge(S["ctx_low"], 1)
                    if j < 2:
                        pe.wait_ge(S["drained"], drained(FIRST[("norm", 0, 2 * h + 1)]))
                    free(n)
                    for k in range(NK):
                        mm = mm3(bank[n % RING], both(ch, cl, ALL, k, cols(e * D + f * P)), normal(k, h), k == 0, k == 1)
                    mm.then_inc(S["filled"], 1)
                elif kind == "y":
                    j = entry[1]
                    if j < 16:
                        e, f = j // 4, j // 2 % 2
                        sums(j, hidden_parts(j), both(ch, cl, ALL, f, cols(e * D, D)), j < 2, j >= 14)
                    else:
                        if j == 16:
                            pe.wait_ge(S["residual"], 1)
                            pe.wait_ge(S["piece_low"], 12)
                        sums(j, hidden_parts(j), both(dnh, dnl, ALL, (j - 16) // 2), j < 18, j >= 30)
                elif kind == "gu":
                    j = entry[1]
                    c, h = (j - 16) // 2, j % 2
                    if j == 16:
                        pe.wait_ge(S["piece_low"], 8)
                    if j < 18:
                        pe.wait_ge(S["drained"], drained(FIRST[("norm", 1, 2 * h + 1)]))
                    free(n, 2)
                    for m in range(2):
                        for k in range(NK):
                            mm = mm3(bank[(n + m) % RING], both(w3h[m], w3l[m], ALL, k, cols(c * P)), normal(k, h), k == 0, k == 1)
                        mm.then_inc(S["filled"], 1)
                elif kind == "spline":
                    k = entry[1]
                    if k == 0:
                        pe.wait_ge(S["ctx_high"], 2)
                        pe.wait_ge(S["zeroed"], 5)
                    free(n, 2)
                    for s in range(2):
                        pe.wait_ge(S["control_low"], 2 * k + s + 1)
                        pe.matmul(bank[(n + s) % RING], u_r[:, :], dst[(2 * k + s) % 4][:, :],
                                  start=True, stop=True).then_inc(S["filled"], 1)
                elif kind == "key":
                    q = entry[1]
                    if q == 0:
                        pe.wait_ge(S["wkv_low"], 1)
                    projected(n, lambda k, t: both(ch, cl, ALL, k, cols((2 * q + t) * P)),
                              lambda k: both(wkvh, wkvl, ALL, k, cols(0, D)))
                elif kind == "value":
                    q = entry[1]
                    free(n)
                    for k in range(NK):
                        mm = mm3(bank[n % RING], both(wkvh, wkvl, ALL, k, cols(D + q // 2 * P)),
                                 both(ch, cl, ALL, k, cols(q % 2 * HALF, HALF)), k == 0, k == 1)
                    mm.then_inc(S["filled"], 1)
                elif kind == "vturn":
                    k = entry[1]
                    free(n)
                    pe.wait_ge(S["v_round"], k + 1)
                    pe.wait_ge(S["identb"], 1)
                    for t in range(NT):
                        mm = pe.transpose(bank[n % RING].bitcast(BF16)[:, t * P:(t + 1) * P],
                                          vround[:, k, t * P:(t + 1) * P], idb[:, :])
                    mm.then_inc(S["filled"], 1)
                elif kind == "query":
                    q = entry[1]
                    if q == 0:
                        pe.wait_ge(S["wq_low"], 1)
                    if q % 2 == 0:
                        pe.wait_ge(S["drained"], drained(FIRST[("norm", 2, q + 1)]))
                    projected(n, lambda k, t: both(hh, hl, ALL, k, cols((2 * q + t) * P)),
                              lambda k: both(wqh, wql, ALL, k))

            def prepare(h, n):
                pe.wait_ge(S["built"], 4 * h + 2)
                for src, b in ((xq[n], 0), (xk[n], 1)):
                    o = bank[2 * prep_slot + b].bitcast(BF16)
                    for t in range(NT):
                        mm = pe.transpose(o[:, t * P:(t + 1) * P], src[:, t, :], idb[:, :])
                mm.then_inc(S["prepped"], 1)

            def turn(g, t, fresh, done):
                if not fresh:
                    pe.wait_ge(S["evac_v"] if t % 2 else S["evac_a"], done)
                pe.wait_ge(S["exped"], g + 1)
                for c in range(NT):
                    mm = pe.transpose(turned[:, c * P:(c + 1) * P],
                                      pu[t % 4][:, c * P:(c + 1) * P].bitcast(BF16), idb[:, :])
                mm.then_inc(S["turn_done"], 1)

            def mix(t, h, done):
                pe.wait_ge(S["evac_a"] if t % 2 else S["evac_v"], done)
                for c in range(NT):
                    mm = pe.matmul(mixed[:, t * HD:(t + 1) * HD], pT[t % 4][:, c * P:(c + 1) * P],
                                   vint[:, c, bass.ds(h * HD, HD)], start=c == 0, stop=c == NT - 1)
                mm.then_inc(S["mix_done"], 1)

            def head_tensor(h, n, first, g0, e0):
                begin = first and n == 0
                for t in range(NT):
                    g = g0 + t
                    if t in (0, 6) and not (begin and t == 0):
                        turn(g - 4, (t - 4) % 8, False, e0 + (t - 3) // 2)
                    if t and not (begin and t < 3):
                        pe.wait_ge(S["exped"], g - 1 if t > 5 else g - 2)
                    if t == 0:
                        pe.wait_ge(S["qT_ready"], h + 1)
                        pe.wait_ge(S["kT_ready"], h + 1)
                    for b in range(2):
                        mm = pe.matmul(scores[tile_slot[t]][:, b * HALF:(b + 1) * HALF],
                                       qT[n][:, t * P:(t + 1) * P], kT[n][:, b * HALF:(b + 1) * HALF],
                                       start=True, stop=True)
                    mm.then_inc(S["scored"], 1)
                    if t in (2, 4) and not (begin and t < 4):
                        turn(g - 4, (t - 4) % 8, begin and t == 4, e0 + (t - 3) // 2)
                    if not (begin and t < 5):
                        if t == 5 and not begin:
                            pe.wait_ge(S["head_out"], h)
                        mix((t - 5) % 8, h - 1 if t < 5 else h, e0 + (t - 5) // 2 + 1)
                    if t % 2 == 0 and not (begin and t < 4):
                        turn(g - 3, (t - 3) % 8, False, e0 + (t - 2) // 2)
                    if t == 5:
                        pe.wait_ge(S["exped"], g - 1)
                        prepare(h + 1, 1 - n)

            pe.wait_ge(S["drained"], drained(FIRST[("query", 3)]))
            prepare(0, 0)
            head_tensor(0, 0, True, 0, 0)
            head_tensor(1, 1, True, 8, 4)
            with pe.Fori(1, HEADS // 2) as i:
                head_tensor(2 * i, 0, False, 16 * i, 8 * i)
                head_tensor(2 * i + 1, 1, False, 16 * i + 8, 8 * i + 4)
            last = 8 * HEADS
            half_last = last // 2
            turn(last - 4, 4, False, half_last - 2)
            mix(3, HEADS - 1, half_last - 2)
            for t in (5, 6, 7):
                turn(last - 8 + t, t, False, half_last - 4 + (t + 1) // 2)
                mix(t - 1, HEADS - 1, half_last - 4 + (t + 1) // 2)
            mix(7, HEADS - 1, half_last)

            pe.wait_ge(S["head_out"], HEADS)
            for q in range(4):
                norm_turns(("oturn", q), O)
            pe.wait_ge(S["moe_low"], 7)
            for q in range(4):
                n = FIRST[("proj", q)]
                if q % 2 == 0:
                    pe.wait_ge(S["drained"], drained(FIRST[("oturn", q + 1)]))
                projected(n, lambda k, t: both(hh, hl, ALL, k, cols((2 * q + t) * P)), lambda k: both(wph, wpl, ALL, k))
            for q in range(4):
                pe.wait_ge(S["norm_ready"], 24 + 4 * (q // 2 + 1))
                norm_turns(("norm", 3, q), xn)
            for h in range(2):
                n = FIRST[("latent", h)]
                pe.wait_ge(S["drained"], drained(FIRST[("norm", 3, 2 * h + 1)]))
                free(n)
                for k in range(NK):
                    mm = mm3(bank[n % RING], both(wdh, wdl, ALL, k), normal(k, h), k == 0, k == 1)
                mm.then_inc(S["filled"], 1)
            n = FIRST[("router", 0)]
            free(n)
            for t in range(NT):
                for k in range(NK):
                    mm = mm3(bank[n % RING][:, t * NE:(t + 1) * NE], both(hh, hl, ALL, k, cols(t * P)), both(wgh, wgl, ALL, k),
                             k == 0, k == 1)
            mm.then_inc(S["filled"], 1)
            for h in range(2):
                n = FIRST[("gu", 32 + h)]
                free(n, 2)
                for m in range(2):
                    for k in range(NK):
                        mm = mm3(bank[(n + m) % RING], both(swh, swl, ALL, k, m), normal(k, h), k == 0, k == 1)
                    mm.then_inc(S["filled"], 1)
            for q in range(2):
                n = FIRST[("wturn", q)]
                free(n)
                pe.wait_ge(S["drained"], drained(FIRST[("router", 0)]))
                for t in range(4):
                    mm = pe.transpose(bank[n % RING][0:NE, t * P:(t + 1) * P], prob[:, 4 * q + t, :], idf[:, :])
                mm.then_inc(S["filled"], 1)

            def gates_ups(k, e, u, first):
                if u % 2 == 0:
                    pe.wait_ge(S["stage_in"], e + 1)
                for m in range(2):
                    pe.wait_ge(S["drained"], drained(MOE0) + 2 * k + m - RING)
                    o = bank[(MOE0 + 2 * u + m) % RING]
                    pe.matmul(o, e1s[u // 2][:, m, :], half(xlh[:, :], u % 2), start=True, stop=False)
                    pe.matmul(o, e1s[u // 2][:, m, :], half(xll[:, :], u % 2), start=False, stop=True).then_inc(S["filled"], 1)

            def expert_tensor(k, e, u, first):
                if within(k + LEAD + 1):
                    gates_ups(k + LEAD + 1, e + (u % 2 + LEAD + 1) // 2, (u + LEAD + 1) % 4, False)
                if u % 2 == 0:
                    pe.wait_ge(S["stage_out"], e + 1)
                pe.wait_ge(S["expert_low"], k + 1)
                begin = first and u < 2
                last = not within(k + 2)
                w = e2s[u // 2][:, :, :].rearrange("p a b -> p (a b)")
                o = bank[4 + u % 2]
                pe.matmul(o, w, eh[u], start=begin, stop=False, skip_group_check=True)
                pe.matmul(o, w, el[u], start=False, stop=last, skip_group_check=True).then_inc(S["expert_sum"], 1)

            for k in range(LEAD + 1):
                gates_ups(k, k // 2, k, True)
            expert_halves(pe, expert_tensor)
            pe.wait_ge(S["acc_low"], 2)
            for q in range(4):
                n = FINAL0 + q
                pe.wait_ge(S["drained"], drained(n - RING))
                for t in range(2):
                    tile = cols((2 * q + t) * P)
                    o = bank[n % RING][:, t * D:(t + 1) * D]
                    mm3(o, both(sh_h, sh_l, ALL, tile), both(s2h, s2l, ALL), True, False)
                    mm = mm3(o, both(ah, al, ALL, tile), both(wuh, wul, ALL), False, True)
                mm.then_inc(S["filled"], 1)


def kernel(**inputs):
    import concourse.bacc as bacc
    from concourse.bass_utils import run_bass_kernel_spmd as run

    a = {k: np.asarray(v) for k, v in inputs.items()}
    turned = lambda v: np.ascontiguousarray(np.swapaxes(v, -1, -2))
    by_input = lambda v: np.ascontiguousarray(v.transpose(2, 0, 1))
    table, stacked, upper = spline_tables()
    i = np.arange(INTER)
    k = np.arange(64) % 16 // 4
    at = (127 * (i // 64) + 2 * (i % 64))[None, None, :] + (np.arange(3) - 1)[None, :, None] + (k - 1)[:, None, None]
    at = np.clip(at, 0, NCP - 1)
    cpw = np.stack([a[f"L0_ffn_{m}_cp"][at] for m in ("gate", "up", "down")])
    arrays = {
        "x": np.ascontiguousarray(a["x"].reshape(T, D)),
        "ident": np.eye(P, dtype=np.float32),
        "ctx_t": turned(a["ctx_2048"].reshape(T, D)),
        "tok": np.ascontiguousarray(a["itok_BxS_13_99985"].reshape(T)),
        "cpw": cpw, "table": table, "stacked": stacked, "upper": np.ascontiguousarray(upper),
        "wq": a["L1_xattn_Wq"], "bq": a["L1_xattn_bq"], "wkv": a["L1_xattn_Wkv"], "bkv": a["L1_xattn_bkv"],
        "bv_t": turned(a["L1_xattn_bkv"][D:].reshape(NK, P)),
        "wp": a["L1_xattn_Wp"], "bp": a["L1_xattn_bp"],
        "sw1_t": turned(a["L1_ffn_sw1"]), "swg_t": turned(a["L1_ffn_swg"]), "sw2_t": turned(a["L1_ffn_sw2"]),
        "rw1_t": by_input(a["L1_ffn_rw1"]), "rwg_t": by_input(a["L1_ffn_rwg"]), "rw2_t": by_input(a["L1_ffn_rw2"]),
        "wg_t": turned(a["L1_ffn_Wg"]), "wdown_t": turned(a["L1_ffn_Wdown"]), "wup_t": turned(a["L1_ffn_Wup"]),
        "biases": a["L1_ffn_biases"],
    }
    nc = bacc.Bacc("TRN2", target_bir_lowering=False, num_devices=1)
    args = {n: nc.dram_tensor(f"in_{n}", v.shape, mybir.dt.from_np(v.dtype), kind="ExternalInput").ap()
            for n, v in arrays.items()}
    out = nc.dram_tensor("out", (T, D), FP32, kind="ExternalOutput").ap()
    build(nc, out=out, **args)
    r = run(nc, [{f"in_{n}": v for n, v in arrays.items()}], core_ids=[0])
    return r.results[0]["out"].reshape(a["x"].shape)
```

```python
import math
from contextlib import ExitStack

import numpy as np
import concourse.bass as bass
from concourse import mybir

FP32, FP32R, BF16 = mybir.dt.float32, mybir.dt.float32r, mybir.dt.bfloat16
I32, U16, U8 = mybir.dt.int32, mybir.dt.uint16, mybir.dt.uint8
ACT, ALU, AX = mybir.ActivationFunctionType, mybir.AluOpType, mybir.AxisListType

P = 128
T, D = 1024, 256
NT, NK = T // P, D // P
HALF = 512
NE0 = 4
VOCAB = 12500
INTER = 1024
NC = INTER // P
NCP = int(INTER * D / 128.9)
HEADS, HD = 16, 16
NE, LAT, HID, TOPK = 16, 64, 128, 8
RSCALE = 2.5
EPS = 1e-5
MAGIC = 12582912.0
RING = 4


def spline_tables():
    n = T * D
    t = np.linspace(0.0, NCP - 1.0, n, dtype=np.float64)
    seg = np.clip(np.floor(t).astype(np.int64), 0, NCP - 2).reshape(INTER, 2, P)
    step = (NCP - 1.0) / (n - 1)
    i = np.arange(INTER)
    first = 127 * (i // 64) + 2 * (i % 64)
    cr = 0.5 * np.array([[0, -1, 2, -1], [2, 0, -5, 3], [0, 1, 4, -3], [0, 0, -1, 1]], np.float64)
    a = np.zeros((4, 4, 2, 2, INTER))
    for c in range(2):
        middle = (256.0 * i + 128.0 * c + 63.5) * step
        for side in range(2):
            g = middle - (first - 1 + c + side)
            for q in range(4):
                for p in range(q, 4):
                    a[:, q, side, c] += cr[:, p, None] * math.comb(p, q) * g ** (p - q)
    u = ((np.arange(P) - 63.5) * step)[None, :] ** np.arange(4)[:, None]
    high = round_12(np.tile(u, (4, 1)).astype(np.float32))
    low = round_12((np.tile(u, (4, 1)) - high).astype(np.float32))
    stacked = np.zeros((2, 2, 2, 16, P), np.float32)
    by_side = np.zeros((P, 2, P), np.float32)
    for side in range(2):
        stacked[:] = 0.0
        stacked[:, side, 0], stacked[:, side, 1] = high, low
        by_side[:, side] = stacked.reshape(P, P)
    upper = (seg - (first[:, None, None] - 1 + np.arange(2)[None, :, None])).transpose(2, 1, 0)
    assert upper.min() == 0 and upper.max() == 1
    by_row = a.reshape(16, 2, 2, INTER).transpose(1, 0, 2, 3)
    table = np.broadcast_to(by_row[None, :, None], (2, 2, 2, 16, 2, INTER)).reshape(P, 2, INTER).astype(np.float32)
    return table, by_side, upper.astype(np.int32)


def round_12(x):
    b = x.view(np.uint32).astype(np.uint64)
    b = (b + 0x7FF + ((b >> 12) & 1)) & 0xFFFFF000
    return b.astype(np.uint32).view(np.float32)


class Chain:

    def __init__(self, eng, sem):
        self.eng, self.sem, self.n, self.loop = eng, sem, 0, 0

    def mark(self, ins):
        ins.then_inc(self.sem, 1)
        self.n += 1

    def wait(self):
        self.eng.wait_ge(self.sem, self.loop + self.n)

    def wait_for(self, n):
        self.eng.wait_ge(self.sem, self.loop + n)

    def link(self, ins):
        self.mark(ins)
        self.wait()


def schedule():
    order = [("norm", 0, n) for n in range(4)]
    order += [("z", j) for j in range(3)] + [("spline", 0)]
    for j in range(16):
        if j + 3 < 16:
            order.append(("z", j + 3))
        order.append(("y", j))
        if 1 + j < 12:
            order.append(("spline", 1 + j))
    order += [("key", n) for n in range(4)] + [("value", 0), ("value", 1)]
    order += [("norm", 1, n) for n in range(4)] + [("value", 2), ("value", 3), ("gu", 16)]
    for j in range(16, 32):
        if j + 1 < 32:
            order.append(("gu", j + 1))
        order.append(("y", j))
        if j == 29:
            order += [("vturn", 0), ("vturn", 1)]
    order += [("norm", 2, n) for n in range(4)] + [("query", n) for n in range(4)]
    order += [("oturn", n) for n in range(4)] + [("proj", n) for n in range(4)]
    order += [("norm", 3, n) for n in range(4)]
    order += [("latent", 0), ("latent", 1), ("router", 0), ("gu", 32), ("gu", 33), ("wturn", 0), ("wturn", 1)]
    return order


BANKS = {"spline": 2, "gu": 2, "y": 0}
ORDER = schedule()
FIRST, _n = {}, 0
for _entry in ORDER:
    FIRST[_entry] = _n
    _n += BANKS.get(_entry[0], 1)
MOE0 = _n
FINAL0 = MOE0 + 4 * NE
KV = sorted(FIRST[e] for e in ORDER if e[0] in ("key", "value"))
ATTENTION = ORDER.index(("query", 3)) + 1


def drained(n):
    return n + 1 - sum(k <= n for k in KV)


def build(nc, x, ident, ctx_t, tok, cpw, table, stacked, upper, wq, bq, wkv, bkv, bv_t, wp, bp,
          sw1_t, swg_t, sw2_t, rw1_t, rwg_t, rw2_t, wg_t, wdown_t, wup_t, biases, out):
    x_v = x.rearrange("(t p) d -> p t d", p=P)
    out_v = out.rearrange("(t p) d -> p t d", p=P)
    wrow = nc.dram_tensor("router_rows", (NE, T), FP32, kind="Internal").ap()

    es = ExitStack()
    with es:
        limit = nc.sbuf_usable_end
        at = {"": (nc.sbuf_base + 63) // 64 * 64}

        def place(region, name, shape, dt):
            size = int(np.prod(shape[1:])) * {FP32: 4, FP32R: 4, I32: 4, BF16: 2, U16: 2, U8: 1}[dt]
            offset = at[region]
            at[region] = offset + (size + 63) // 64 * 64
            assert at[region] <= limit, (name, at[region], limit)
            return nc.alloc_sbuf_tensor_at(name, shape, dt, offset=offset)

        def sem(name):
            return es.enter_context(nc.semaphore(name))

        X = place("", "X", [P, NT, D], FP32)
        xn = place("", "xn", [P, NT, D], FP32)
        hh = place("", "hh", [P, NK, T], FP32R)
        hl = place("", "hl", [P, NK, T], FP32R)
        idf = place("", "idf", [P, P], FP32)
        idb = place("", "idb", [P, P], BF16)
        NH = 3
        gate_s = [place("", f"gate_s{n}", [P, HALF], FP32) for n in range(NH)]
        prod = [place("", f"prod{n}", [P, HALF], FP32) for n in range(NH)]
        ph = [place("", f"ph{n}", [P, HALF], FP32R) for n in range(NH)]
        pl = [place("", f"pl{n}", [P, HALF], FP32R) for n in range(NH)]
        stats = place("", "stats", [P, NT, 6], FP32)
        mv = place("", "mv", [P, NT, 2], FP32)
        std = place("", "std", [P, NT], FP32)
        shift = place("", "shift", [P, NT], FP32)
        rstd = place("", "rstd", [P, NT], FP32)
        eps = place("", "eps", [P, 1], FP32)
        kparts = place("", "kparts", [P, NT, 3, D + HD], BF16)
        vint = place("", "vint", [P, NT, D], BF16)
        sv = place("", "sv", [P, NK], FP32)
        rsv = place("", "rsv", [P, NK], FP32)
        bk = place("", "bk", [P, D], FP32)
        bv = place("", "bv", [P, NK], FP32)
        base = at[""]
        at["A"] = base
        ch = place("A", "ch", [P, NK, T], FP32R)
        cl = place("A", "cl", [P, NK, T], FP32R)
        wkvh = place("A", "wkvh", [P, NK, 2 * D], FP32R)
        wkvl = place("A", "wkvl", [P, NK, 2 * D], FP32R)
        w3h = [place("A", f"w3h{m}", [P, NK, T], FP32R) for m in range(2)]
        w3l = [place("A", f"w3l{m}", [P, NK, T], FP32R) for m in range(2)]
        at["S"] = at["A"]
        dnh = place("A", "dnh", [P, NC, D], FP32R)
        dnl = place("A", "dnl", [P, NC, D], FP32R)
        craw = place("S", "craw", [P, NK, T], FP32)
        wkvraw = place("S", "wkvraw", [P, NK, 2 * D], FP32)
        toki = place("S", "toki", [P, T], I32)
        side = place("A", "side", [P, 2, T], I32)
        u_raw = prod[NH - 1][:, 0:2 * P]
        u_r = place("A", "u_r", [P, 2, P], FP32R)
        mask = [place("A", f"mask{e}", [P, T], BF16) for e in range(NE0)]
        at["K"] = at["A"]
        cps = [place("A", f"cps{n}", [P, 2, T], FP32) for n in range(2)]
        tab = place("A", "tab", [P, 2, T], FP32)
        df = [place("A", f"df{n}", [P, HALF], FP32) for n in range(2)]
        dst = [place("A", f"dst{n}", [P, HALF], FP32R) for n in range(2)]
        kraw = place("K", "kraw", [P, NT, D], FP32)
        vt = place("K", "vt", [P, NK, T], FP32)
        kmax = place("K", "kmax", [P, NT * HEADS], FP32)
        ks = place("K", "ks", [P, NT * HEADS], FP32)
        krs = place("K", "krs", [P, NT * HEADS], FP32)
        vround = place("K", "vround", [P, NK, T], BF16)
        at["B"] = base
        qraw = place("B", "qraw", [P, NT, D], FP32)
        qint = place("B", "qint", [P, NT, D + HD], BF16)
        qmax = place("B", "qmax", [P, NT, HEADS], FP32)
        qs = place("B", "qs", [P, NT, HEADS + 1], FP32)
        qrs = place("B", "qrs", [P, NT, HEADS], FP32)
        nqs = place("B", "nqs", [P, NT, HEADS + 1], FP32)
        xq = [place("B", f"xq{n}", [P, NT, P], BF16) for n in range(2)]
        xk = [place("B", f"xk{n}", [P, NT, P], BF16) for n in range(2)]
        qT = [place("B", f"qT{n}", [P, T], BF16) for n in range(2)]
        kT = [place("B", f"kT{n}", [P, T], BF16) for n in range(2)]
        pu = [place("B", f"pu{n}", [P, T], U16) for n in range(4)]
        pT = [place("B", f"pT{n}", [P, T], BF16) for n in range(4)]
        smax = [place("B", f"smax{n}", [P, 2], FP32) for n in range(4)]
        qsh = [place("B", f"qsh{n}", [P, NT], FP32) for n in range(2)]
        nqsh = [place("B", f"nqsh{n}", [P, NT], FP32) for n in range(2)]
        zsum = [place("B", f"zsum{n}", [P, NT], FP32) for n in range(2)]
        rz = [place("B", f"rz{n}", [P, NT], FP32) for n in range(2)]
        O = place("B", "O", [P, NT, D], FP32)
        at["C"] = at["B"]
        wqraw = place("C", "wqraw", [P, NK, D], FP32)
        wqh = place("C", "wqh", [P, NK, D], FP32R)
        wql = place("C", "wql", [P, NK, D], FP32R)
        wpraw = place("C", "wpraw", [P, NK, D], FP32)
        wph = place("C", "wph", [P, NK, D], FP32R)
        wpl = place("C", "wpl", [P, NK, D], FP32R)
        bqb = place("C", "bqb", [P, D], FP32)
        bpb = place("C", "bpb", [P, D], FP32)
        swraw = place("C", "swraw", [P, NK, 2, HID], FP32)
        swh = place("C", "swh", [P, NK, 2, HID], FP32R)
        swl = place("C", "swl", [P, NK, 2, HID], FP32R)
        s2raw = place("C", "s2raw", [P, D], FP32)
        s2h = place("C", "s2h", [P, D], FP32R)
        s2l = place("C", "s2l", [P, D], FP32R)
        wgraw = place("C", "wgraw", [P, NK, NE], FP32)
        wgh = place("C", "wgh", [P, NK, NE], FP32R)
        wgl = place("C", "wgl", [P, NK, NE], FP32R)
        wdraw = place("C", "wdraw", [P, NK, 2 * LAT], FP32)
        wdh = place("C", "wdh", [P, NK, 2 * LAT], FP32R)
        wdl = place("C", "wdl", [P, NK, 2 * LAT], FP32R)
        wuraw = place("C", "wuraw", [P, D], FP32)
        wuh = place("C", "wuh", [P, D], FP32R)
        wul = place("C", "wul", [P, D], FP32R)
        biasb = place("C", "biasb", [P, NE], FP32)
        e1 = place("C", "e1", [P, NE, 2, HID], FP32R)
        e2 = place("C", "e2", [P, NE, 2, LAT], FP32R)
        e1raw = place("C", "e1raw", [P, NE, 2, HID], FP32)
        e2raw = place("C", "e2raw", [P, NE, LAT], FP32)
        e1s = [place("C", f"e1s{n}", [P, 2, HID], FP32R) for n in range(2)]
        e2s = [place("C", f"e2s{n}", [P, 2, LAT], FP32R) for n in range(2)]
        at["D"] = base
        xlh = place("D", "xlh", [P, T], FP32R)
        xll = place("D", "xll", [P, T], FP32R)
        prob = place("D", "prob", [P, NT, NE], FP32)
        pick = place("D", "pick", [P, NT, NE], FP32)
        left = place("D", "left", [P, NT, NE], FP32)
        top8 = place("D", "top8", [P, NT, TOPK], FP32)
        psum8 = place("D", "psum8", [P, NT], FP32)
        wT = place("D", "wT", [NE, T], FP32)
        wb = [place("D", f"wb{n}", [P, T], FP32) for n in range(2)]
        sq = [place("D", f"sq{n}", [P, HALF], FP32)[:, :] for n in range(4)]
        hp = [place("D", f"hp{n}", [P, HALF], FP32)[:, :] for n in range(4)]
        eh = [place("D", f"eh{n}", [P, HALF], FP32R)[:, :] for n in range(4)]
        el = [place("D", f"el{n}", [P, HALF], FP32R)[:, :] for n in range(4)]
        (ah, sh_h), (al, sh_l), res = (hh[:, 0, :], hh[:, 1, :]), (hl[:, 0, :], hl[:, 1, :]), xn
        assert at["D"] <= at["B"], (at["D"], at["B"])

        psum = es.enter_context(nc.psum_tensor("psum", [P, 8, HALF], FP32))
        bank = [psum[:, n, :] for n in range(8)]
        scores = [psum[:, 2 * n:2 * n + 2, :].rearrange("p b k -> p (b k)") for n in range(3)]
        turned = bank[6].bitcast(BF16)
        mixed = bank[7][:, 0:P]
        ups, gates_of = bank[0:4], bank[6:8]

        S = {n: sem(n) for n in (
            "x_in0", "x_in1", "ident_in", "identb", "ctx_in", "tok_in", "cp_in0", "cp_in1", "cp_in2", "u_in", "tab_in", "side_in", "wkv_in", "wq_in", "moe_in",
            "e1_in", "wrow_out", "wb_in0", "wb_in1", "stage_in", "stage_out", "out_done",
            "zeroed", "filled", "drained", "vec_own", "act_own", "summed", "residual",
            "variance", "std_ready", "scales_ready", "norm_ready", "norm_rest", "norm_high", "ctx_high", "ctx_low", "mask_ready",
            "activated", "masked", "high_ready", "low_ready",
            "control", "control_high", "control_low", "selected", "piece_high",
            "kv_plain", "k_biased", "k_scales", "k_steps", "k_ready", "v_round", "wkv_high", "wkv_low",
            "wq_high", "wq_low", "bp_added", "q_ready", "built", "prepped", "qT_ready", "kT_ready",
            "scored", "maxed", "exped", "turn_done", "evac_v", "evac_a", "mix_done", "head_out",
            "o_high", "moe_high", "moe_low", "e1_low", "latent_high", "latent_low",
            "probs", "weights", "rectified", "squared", "scaled", "expert_high", "expert_low", "expert_sum",
            "acc_high", "acc_low", "res_ready")}
        block = es.enter_context(nc.Block())
        def half(ap, n):
            return ap[:, n * HALF:(n + 1) * HALF]

        def plain(ap):
            return ap.bitcast(FP32) if ap.dtype == FP32R else ap

        def piece(k, high):
            m, c, h = k // 4, k // 2 % 2, k % 2
            raw = bank[FIRST[("spline", k)] % RING]
            if m < 2:
                return half((w3h if high else w3l)[m][:, c, :], h), raw
            return (dnh if high else dnl)[:, c::2, h * P:(h + 1) * P], raw.rearrange("p (x q) -> p q x", q=4)

        tile_slot = [(1 + t + (t > 5)) % 3 for t in range(NT)]
        prep_slot = (1 + 6) % 3
        assert (NT + 1) % 3 == 0
        PAIR_STEPS = 2 * (NT + 2)

        LOG255 = math.log(255.0)
        MOE_LOADS = 16 * 12

        def expert_halves(eng, step):
            for k in range(4):
                step(k, k // 2, k, True)
            with eng.Fori(1, NE // 2 - 2) as i:
                for u in range(4):
                    step(4 * i + u, 2 * i + u // 2, u, False)
            for k in range(2 * NE - 8, 2 * NE):
                step(k, k // 2, k % 4, False)

        def within(k):
            return not isinstance(k, int) or k < 2 * NE

        LEAD = 3

        @block.sync
        def _(sp):
            def load(dst, src, name):
                sp.dma_start(dst, src).then_inc(S[name], 16)

            def row(v, n):
                return v.rearrange("(a d) -> a d", a=1).broadcast_to((P, n))

            for n in range(2):
                load(X[:, 4 * n:4 * n + 4, :], x_v[:, 4 * n:4 * n + 4, :], f"x_in{n}")
            load(craw[:, :, :], ctx_t.rearrange("(k p) t -> p k t", p=P), "ctx_in")
            load(idf[:, :], ident, "ident_in")
            load(toki[:, :], row(tok, T), "tok_in")
            load(u_raw, stacked.rearrange("k s p -> k (s p)"), "u_in")
            load(tab[:, :, :], table, "tab_in")
            load(cps[0][:, :, :], cpw[0], "cp_in0")
            load(side[:, :, :], upper, "side_in")
            load(wkvraw[:, :, :], wkv.rearrange("(k p) n -> p k n", p=P), "wkv_in")
            load(bk[:, :], row(bkv[0:D], D), "wkv_in")
            load(bv[:, :], bv_t, "wkv_in")
            load(cps[1][:, :, :], cpw[1], "cp_in1")
            sp.wait_ge(S["control"], 4)
            load(cps[0][:, :, :], cpw[2], "cp_in2")
            sp.wait_ge(S["residual"], 2)
            load(wqraw[:, :, :], wq.rearrange("(k p) n -> p k n", p=P), "wq_in")
            load(bqb[:, :], row(bq, D), "wq_in")
            load(wpraw[:, :, :], wp.rearrange("(k p) n -> p k n", p=P), "moe_in")
            load(bpb[:, :], row(bp, D), "moe_in")
            load(swraw[:, :, 0, :], swg_t.rearrange("(k p) n -> p k n", p=P), "moe_in")
            load(swraw[:, :, 1, :], sw1_t.rearrange("(k p) n -> p k n", p=P), "moe_in")
            load(s2raw[:, :], sw2_t, "moe_in")
            load(wgraw[:, :, :], wg_t.rearrange("(k p) n -> p k n", p=P), "moe_in")
            for n in range(2):
                load(wdraw[:, :, n * LAT:(n + 1) * LAT], wdown_t.rearrange("(k p) n -> p k n", p=P), "moe_in")
                load(wuraw[n * LAT:(n + 1) * LAT, :], wup_t, "moe_in")
            load(biasb[:, :], row(biases, NE), "moe_in")
            load(e2raw[:, :, :], rw2_t, "moe_in")
            for n in range(2):
                for m, w in ((0, rwg_t), (1, rw1_t)):
                    load(e1raw[n * LAT:(n + 1) * LAT, :, m, :], w, "e1_in")
            sp.wait_ge(S["drained"], drained(FIRST[("wturn", 1)]))
            sp.dma_start(wrow, wT[:, :]).then_inc(S["wrow_out"], 16)
            sp.wait_ge(S["wrow_out"], 16)

            def spread(e, n, first):
                if not first:
                    sp.wait_ge(S["scaled"], 2 * (e - 1))
                sp.dma_start(wb[n][:, :], wrow[bass.ds(e, 1), :].broadcast_to((P, T))).then_inc(S[f"wb_in{n}"], 16)

            spread(0, 0, True)
            spread(1, 1, True)
            with sp.Fori(1, NE // 2) as i:
                spread(2 * i, 0, False)
                spread(2 * i + 1, 1, False)
            for n in range(4):
                sp.wait_ge(S["res_ready"], n + 1)
                sp.dma_start(out_v[:, 2 * n:2 * n + 2, :], res[:, 2 * n:2 * n + 2, :]).then_inc(S["out_done"], 16)
            sp.wait_ge(S["out_done"], 64)

        @block.gpsimd
        def _(pool):
            pool.memset(eps[:, :], EPS).then_inc(S["zeroed"], 1)
            pool.wait_ge(S["ident_in"], 16)
            pool.tensor_copy(idb[:, :], idf[:, :]).then_inc(S["identb"], 1)

            def control(k):
                m, c, h = k // 4, k // 2 % 2, k % 2
                if k == 0:
                    pool.wait_ge(S["tab_in"], 16)
                if k % 4 == 0:
                    pool.wait_ge(S[f"cp_in{m}"], 16)
                if k >= 2:
                    pool.wait_ge(S["control_low"], k - 1)
                pool.tensor_tensor(df[k % 2][:, :], half(tab[:, c, :], h), half(cps[m % 2][:, c, :], h),
                                   ALU.mult).then_inc(S["control"], 1)

            pool.wait_ge(S["ctx_high"], 1)
            pool.tensor_tensor(cl[:, :, :], craw[:, :, :], plain(ch[:, :, :]), ALU.subtract).then_inc(S["ctx_low"], 1)
            control(0)
            control(1)
            for entry in ORDER[:ATTENTION]:
                if entry[0] == "z":
                    j = entry[1]
                    pool.wait_ge(S["mask_ready"], min(j // 4 + 1, NE0 - 1))
                    pool.wait_ge(S["activated"], j + 1)
                    pool.tensor_tensor(gate_s[j % NH][:, :], gate_s[j % NH][:, :],
                                       half(mask[j // 4][:, :], j % 2), ALU.mult).then_inc(S["masked"], 1)
                elif entry[0] == "spline" and entry[1] + 2 < 12:
                    control(entry[1] + 2)
                elif entry == ("norm", 1, 0):
                    pool.wait_ge(S["kv_plain"], 4)
                    pool.wait_ge(S["wkv_in"], 48)
                    pool.tensor_tensor(kraw[:, :, :], kraw[:, :, :],
                                       bk[:, :].unsqueeze(1).broadcast_to((P, NT, D)),
                                       ALU.add).then_inc(S["k_biased"], 1)
            kg = kraw[:, :, :].rearrange("p t (h d) -> p (t h) d", d=HD)
            for step, factor in ((1, krs), (2, ks)):
                pool.wait_ge(S["k_scales"], step)
                pool.tensor_tensor(kg, kg, factor[:, :].unsqueeze(2).broadcast_to((P, NT * HEADS, HD)),
                                   ALU.mult).then_inc(S["k_steps"], 1)
            for part in range(2):
                pool.wait_ge(S["k_ready"], part + 1)
                pool.tensor_tensor(kraw[:, :, :], kraw[:, :, :], kparts[:, :, part, 0:D],
                                   ALU.subtract).then_inc(S["k_steps"], 1)
            pool.wait_ge(S["residual"], 2)
            for n in range(2):
                pool.memset(xq[n][:, :, :], 0.0).then_inc(S["zeroed"], 1)
                pool.memset(xk[n][:, :, :], 0.0).then_inc(S["zeroed"], 1)
            pool.memset(qint[:, :, D:], 0.0).then_inc(S["zeroed"], 1)
            pool.memset(kparts[:, :, :, D:], 0.0).then_inc(S["zeroed"], 1)
            pool.memset(qs[:, :, HEADS:], 0.0).then_inc(S["zeroed"], 1)
            pool.memset(nqs[:, :, HEADS:], 0.0).then_inc(S["zeroed"], 1)
            pool.wait_ge(S["zeroed"], 9)
            pool.wait_ge(S["k_ready"], 3)
            pool.wait_ge(S["wq_high"], 1)
            pool.tensor_tensor(wql[:, :, :], wqraw[:, :, :], plain(wqh[:, :, :]), ALU.subtract).then_inc(S["wq_low"], 1)

            def head(h, n, first):
                if not first:
                    pool.wait_ge(S["prepped"], h - 1)
                    pool.wait_ge(S["exped"], 8 * (h - 1))
                pool.tensor_copy(xk[n][:, :, 0:3 * HD].rearrange("p t (r d) -> p t r d", r=3),
                                 kparts[:, :, :, bass.ds(h * HD, HD)]).then_inc(S["built"], 1)
                if first:
                    pool.wait_ge(S["q_ready"], 1)
                pool.tensor_copy(xq[n][:, :, 0:3 * HD].rearrange("p t (r d) -> p t r d", r=3),
                                 qint[:, :, bass.ds(h * HD, HD)].unsqueeze(2)
                                 .broadcast_to((P, NT, 3, HD))).then_inc(S["built"], 1)
                pool.tensor_copy(qsh[n][:, :].unsqueeze(2), qs[:, :, bass.ds(h, 1)]).then_inc(S["built"], 1)
                pool.tensor_copy(nqsh[n][:, :].unsqueeze(2), nqs[:, :, bass.ds(h, 1)]).then_inc(S["built"], 1)

            head(0, 0, True)
            head(1, 1, True)
            pool.wait_ge(S["q_ready"], 2)
            pool.wait_ge(S["norm_ready"], 12)
            pool.wait_ge(S["norm_rest"], 12)
            pool.wait_ge(S["moe_in"], MOE_LOADS)
            pool.tensor_tensor(X[:, :, :], X[:, :, :], bpb[:, :].unsqueeze(1).broadcast_to((P, NT, D)),
                               ALU.add).then_inc(S["bp_added"], 1)

            def low(dst_ap, raw, high, n, name):
                pool.wait_ge(S["moe_high"], n)
                pool.tensor_tensor(dst_ap, raw, plain(high), ALU.subtract).then_inc(S[name], 1)

            low(wpl[:, :, :], wpraw[:, :, :], wph[:, :, :], 1, "moe_low")
            low(swl[:, :, :, :].rearrange("p k m n -> p (k m n)"), swraw[:, :, :, :].rearrange("p k m n -> p (k m n)"),
                swh[:, :, :, :].rearrange("p k m n -> p (k m n)"), 2, "moe_low")
            low(s2l[:, :], s2raw[:, :], s2h[:, :], 3, "moe_low")
            low(wgl[:, :, :], wgraw[:, :, :], wgh[:, :, :], 4, "moe_low")
            low(wdl[:, :, :], wdraw[:, :, :], wdh[:, :, :], 5, "moe_low")
            low(wul[:, :], wuraw[:, :], wuh[:, :], 6, "moe_low")
            low(e2[:, :, 1, :], e2raw[:, :, :], e2[:, :, 0, :], 7, "moe_low")
            head(2, 0, False)
            head(3, 1, False)
            pool.wait_ge(S["built"], 16)
            for g in range(4):
                rows = e1[LAT:P, 4 * g:4 * g + 4, :, :].rearrange("p e m n -> p (e m n)")
                low(rows, e1raw[LAT:P, 4 * g:4 * g + 4, :, :].rearrange("p e m n -> p (e m n)"), rows, 8 + g, "e1_low")
            pool.wait_ge(S["e1_low"], 4)
            with pool.Fori(2, HEADS // 2) as i:
                head(2 * i, 0, False)
                head(2 * i + 1, 1, False)
            head(HEADS, 0, False)

            def scale(k, e, u, first):
                if u % 2 == 0:
                    pool.wait_ge(S[f"wb_in{u // 2}"], 8 * (e - u // 2) + 16)
                pool.wait_ge(S["drained"], drained(MOE0) + 2 * k + 1)
                pool.tensor_tensor(hp[u], hp[u], half(wb[u // 2][:, :], u % 2), ALU.mult).then_inc(S["scaled"], 1)

            expert_halves(pool, scale)

        @block.scalar
        def _(act):
            def copy(o, i, name, **k):
                act.activation(o, i, ACT.Copy, **k).then_inc(S[name], 1)

            def late_constants():
                act.wait_ge(S["u_in"], 16)
                copy(u_r[:, :, :].rearrange("p s n -> p (s n)"), u_raw, "ctx_high")

            def controls(k):
                act.wait_ge(S["control"], k + 1)
                if k >= 2:
                    act.wait_ge(S["filled"], FIRST[("spline", k - 2)] + 2)
                copy(dst[k % 2][:, :], df[k % 2][:, :], "control_high")

            def product_done(j):
                return drained(FIRST[("z", j)] if j < 16 else FIRST[("gu", j)] + 1)

            def highs(j):
                act.wait_ge(S["drained"], product_done(j))
                if j >= NH:
                    act.wait_ge(S["low_ready"], j - NH + 1)
                    act.wait_ge(S["summed"], j - NH + 1)
                copy(ph[j % NH][:, :], prod[j % NH][:, :], "high_ready")

            def root(layer):
                act.wait_ge(S["variance"], 2 * layer + 2)
                if layer == 0:
                    act.wait_ge(S["zeroed"], 1)
                act.activation(std[:, :], mv[:, :, 1], ACT.Sqrt, bias=eps[:, :]).then_inc(S["std_ready"], 1)

            def normalise_rest(layer):
                act.wait_ge(S["scales_ready"], layer + 1)
                for t in range(4, NT):
                    act.activation(xn[:, t, :], X[:, t, :], ACT.Identity, scale=rstd[:, t:t + 1],
                                   bias=shift[:, t:t + 1]).then_inc(S["norm_rest"], 1)

            def gates(j, n, func):
                act.wait_ge(S["filled"], n + 1)
                if j >= NH:
                    act.wait_ge(S["drained"], product_done(j - NH))
                act.activation(gate_s[j % NH][:, :], bank[n % RING], func).then_inc(S["activated"], 1)

            def norm_highs(entry):
                n, q = FIRST[entry], entry[2]
                act.wait_ge(S["filled"], n + 1)
                copy(half(hh[:, q % 2, :], q // 2), bank[n % RING], "norm_high")

            root(0)
            act.wait_ge(S["ctx_in"], 16)
            copy(ch[:, :, :], craw[:, :, :], "ctx_high")
            for entry in ORDER[:ATTENTION]:
                kind, n = entry[0], FIRST[entry]
                if kind == "norm":
                    layer, q = entry[1:]
                    if q == 0:
                        if layer > 1:
                            root(layer)
                        normalise_rest(layer)
                        if layer == 2:
                            act.wait_ge(S["wq_in"], 32)
                            copy(wqh[:, :, :], wqraw[:, :, :], "wq_high")
                    norm_highs(entry)
                    if q == 3 and layer == 0:
                        late_constants()
                        controls(0)
                elif kind in ("z", "gu"):
                    j = entry[1]
                    gates(j, n, ACT.Silu)
                    if 0 < j < 16:
                        highs(j - 1)
                    if j >= 15:
                        highs(j)
                elif kind == "spline":
                    k = entry[1]
                    if k + 1 < 12:
                        controls(k + 1)
                    act.wait_ge(S["selected"], k + 1)
                    if k == 8:
                        act.wait_ge(S["ctx_low"], 1)
                        act.wait_ge(S["wkv_low"], 1)
                        act.wait_ge(S["mask_ready"], 3)
                    copy(*piece(k, True), "piece_high")
                    if k == 2:
                        act.wait_ge(S["wkv_in"], 48)
                        copy(wkvh[:, :, :], wkvraw[:, :, :], "wkv_high")
                elif kind in ("key", "value"):
                    q = entry[1]
                    if entry == ("value", 0):
                        root(1)
                    act.wait_ge(S["filled"], n + 1)
                    if kind == "key":
                        if q == 0:
                            act.wait_ge(S["control_low"], 12)
                            act.wait_ge(S["filled"], FIRST[("spline", 11)] + 2)
                        copy(kraw[:, 2 * q:2 * q + 2, :].rearrange("p t d -> p (t d)"), bank[n % RING], "kv_plain")
                    else:
                        act.activation(half(vt[:, q // 2, :], q % 2), bank[n % RING], ACT.Identity,
                                       bias=bv[:, q // 2:q // 2 + 1]).then_inc(S["kv_plain"], 1)

            act.wait_ge(S["moe_in"], MOE_LOADS)
            copy(wph[:, :, :], wpraw[:, :, :], "moe_high")
            copy(swh[:, :, :, :].rearrange("p k m n -> p (k m n)"), swraw[:, :, :, :].rearrange("p k m n -> p (k m n)"),
                 "moe_high")
            copy(s2h[:, :], s2raw[:, :], "moe_high")
            copy(wgh[:, :, :], wgraw[:, :, :], "moe_high")
            copy(wdh[:, :, :], wdraw[:, :, :], "moe_high")
            copy(wuh[:, :], wuraw[:, :], "moe_high")
            copy(e2[:, :, 0, :], e2raw[:, :, :], "moe_high")

            def key_turn(h, n):
                act.wait_ge(S["prepped"], h + 1)
                copy(kT[n][:, :], bank[2 * prep_slot + 1].bitcast(BF16), "kT_ready")

            def head_scalar(h, n, first, g0):
                for t in range(NT):
                    g = g0 + t
                    if not (first and n == 0 and t < 4):
                        act.wait_ge(S["turn_done"], g - 3)
                    if t == 0 and not first:
                        act.wait_ge(S["head_out"], h - 1)
                    act.wait_ge(S["maxed"], g + 1)
                    act.activation(pu[t % 4][:, :], scores[tile_slot[t]], ACT.Exp, bias=smax[t % 4][:, 1:2],
                                   scale=qsh[n][:, t:t + 1], accum_out=zsum[n][:, t:t + 1]).then_inc(S["exped"], 1)
                    if t == 5:
                        key_turn(h + 1, 1 - n)
                    if t % 2 and not (first and n == 0 and t == 1):
                        evac_scalar(g - 2, (t - 2) % 8, first and n == 0 and t < 7)

            def evac_scalar(g, t, fresh):
                act.wait_ge(S["turn_done"], g + 1)
                if not fresh:
                    act.wait_ge(S["mix_done"], g - 3)
                copy(pT[t % 4][:, :], turned.bitcast(U16), "evac_a")

            act.activation(smax[3][:, 0:1], eps[:, :], ACT.Exp).then_inc(S["act_own"], 1)
            act.wait_ge(S["act_own"], 1)
            act.wait_ge(S["prepped"], 1)
            copy(kT[0][:, :], bank[2 * prep_slot + 1].bitcast(BF16), "kT_ready")
            head_scalar(0, 0, True, 0)
            act.wait_ge(S["e1_in"], 64)
            for g in range(4):
                copy(e1[:, 4 * g:4 * g + 4, :, :].rearrange("p e m n -> p (e m n)"),
                     e1raw[:, 4 * g:4 * g + 4, :, :].rearrange("p e m n -> p (e m n)"), "moe_high")
            head_scalar(1, 1, True, 8)
            with act.Fori(1, HEADS // 2) as i:
                head_scalar(2 * i, 0, False, 16 * i)
                head_scalar(2 * i + 1, 1, False, 16 * i + 8)
            evac_scalar(8 * HEADS - 1, 7, False)

            for q in range(4):
                n = FIRST[("oturn", q)]
                act.wait_ge(S["filled"], n + 1)
                copy(half(hh[:, q % 2, :], q // 2), bank[n % RING], "o_high", scale=sv[:, q % 2:q % 2 + 1])
            root(3)
            normalise_rest(3)
            for q in range(4):
                norm_highs(("norm", 3, q))
            act.wait_ge(S["built"], 4 * (HEADS + 1))
            for q in range(2):
                n = FIRST[("latent", q)]
                act.wait_ge(S["filled"], n + 1)
                copy(half(xlh[:, :], q), bank[n % RING], "latent_high")
            n = FIRST[("router", 0)]
            act.wait_ge(S["filled"], n + 1)
            act.activation(prob[:, :, :].rearrange("p t e -> p (t e)"), bank[n % RING][:, 0:P], ACT.Sigmoid)\
               .then_inc(S["probs"], 1)
            for q in range(2):
                j, n = 32 + q, FIRST[("gu", 32 + q)]
                gates(j, n, ACT.Relu)
                act.wait_ge(S["activated"], j + 1)
                act.activation(gate_s[j % NH][:, :], gate_s[j % NH][:, :], ACT.Square).then_inc(S["squared"], 1)
            act.wait_ge(S["filled"], FIRST[("gu", 33)] + 2)
            for q in range(2):
                act.wait_ge(S["drained"], drained(FIRST[("gu", 32 + q)] + 1))
                copy(half(sh_h, q), prod[(32 + q) % NH][:, :], "high_ready")

            def rectify(k, u, first):
                act.wait_ge(S["filled"], MOE0 + 2 * k + 1)
                if not first:
                    act.wait_ge(S["drained"], drained(MOE0) + 2 * (k - 4) + 1)
                act.activation(sq[u], gates_of[u % 2], ACT.Relu).then_inc(S["rectified"], 1)

            def square(k, u):
                act.wait_ge(S["rectified"], k + 1)
                act.activation(sq[u], sq[u], ACT.Square).then_inc(S["squared"], 1)

            def expert_scalar(k, e, u, first):
                v, fresh = (u + LEAD) % 4, first and u + LEAD < 4
                if within(k + LEAD):
                    rectify(k + LEAD, v, fresh)
                act.wait_ge(S["scaled"], k + 1)
                if not first:
                    act.wait_ge(S["expert_low"], k - 3)
                    act.wait_ge(S["expert_sum"], k - 3)
                copy(eh[u], hp[u], "expert_high")
                if within(k + LEAD):
                    square(k + LEAD, v)

            for k in range(LEAD):
                rectify(k, k, True)
                square(k, k)
            expert_halves(act, expert_scalar)
            for h in range(2):
                act.wait_ge(S["expert_sum"], 2 * NE)
                copy(half(ah, h), bank[4 + h], "acc_high")

        @block.vector
        def _(dve):
            own = Chain(dve, S["vec_own"])

            def sub(o, a, b, name, k=1):
                dve.tensor_tensor(o, plain(a), plain(b), ALU.subtract).then_inc(S[name], k)

            def moments(h):
                for t in range(4 * h, 4 * h + 4):
                    own.mark(dve.bn_stats(stats[:, t, :], X[:, t, :]))
                own.wait()
                for t in range(4 * h, 4 * h + 4):
                    ins = dve.bn_aggr(mv[:, t, :], stats[:, t, :])
                ins.then_inc(S["variance"], 1)

            def norm(layer):
                dve.wait_ge(S["std_ready"], layer + 1)
                own.link(dve.reciprocal(rstd[:, :], std[:, :]))
                dve.scalar_tensor_tensor(shift[:, :], mv[:, :, 0], -1.0, rstd[:, :],
                                         ALU.mult, ALU.mult).then_inc(S["scales_ready"], 1)
                for t in range(4):
                    dve.tensor_scalar(xn[:, t, :], X[:, t, :], mv[:, t, 0:1], rstd[:, t:t + 1],
                                      ALU.subtract, ALU.mult).then_inc(S["norm_ready"], 1)

            def norm_lows(entry):
                n, (layer, q) = FIRST[entry], entry[1:]
                dve.wait_ge(S["norm_high"], 4 * layer + q + 1)
                sub(half(hl[:, q % 2, :], q // 2), bank[n % RING], half(hh[:, q % 2, :], q // 2), "drained")

            def product(j, n, b):
                if j < 16:
                    dve.wait_ge(S["masked"], j + 1)
                elif j < 32:
                    dve.wait_ge(S["activated"], j + 1)
                    dve.wait_ge(S["filled"], n + 2)
                else:
                    dve.wait_ge(S["squared"], j - 31)
                    dve.wait_ge(S["filled"], n + 2)
                if j >= NH:
                    dve.wait_ge(S["high_ready"], j - NH + 1)
                    dve.wait_ge(S["low_ready"], j - NH + 1)
                dve.tensor_tensor(prod[j % NH][:, :], gate_s[j % NH][:, :], bank[b % RING],
                                  ALU.mult).then_inc(S["drained"], 1 + b - n)

            def lows(j):
                dve.wait_ge(S["high_ready"], j + 1)
                if j >= NH:
                    dve.wait_ge(S["summed"], j - NH + 1)
                sub(pl[j % NH][:, :], prod[j % NH][:, :], ph[j % NH][:, :], "low_ready")

            def add_sums(layer, h):
                dve.wait_ge(S["summed"], 16 * layer + 15 + h)
                for b in (2 * h, 2 * h + 1):
                    o = X[:, 2 * b:2 * b + 2, :].rearrange("p t d -> p (t d)")
                    ins = dve.tensor_tensor(o, o, bank[4 + b], ALU.add)
                    own.mark(ins) if b < 3 else ins.then_inc(S["residual"], 1)
                own.wait()
                if h:
                    dve.wait_ge(S["residual"], layer + 1)

            def mask_steps():
                per = VOCAB // NE0
                for e in range(NE0 - 1):
                    own.link(dve.tensor_scalar(mask[e + 1][:, :], toki[:, :], float(per * (e + 1)), None, ALU.is_ge))
                    if e == 0:
                        dve.tensor_scalar(mask[0][:, :], mask[1][:, :], -1.0, 1.0, ALU.mult, ALU.add).then_inc(S["mask_ready"], 1)
                    else:
                        sub(mask[e][:, :], mask[e][:, :], mask[e + 1][:, :], "mask_ready")
                    yield

            def control_lows(k):
                dve.wait_ge(S["control_high"], k + 1)
                d = dst[k % 2][P // 2:, :]
                sub(d, df[k % 2][P // 2:, :], d, "control_low")

            def key_value_steps():
                kg = kraw[:, :, :].rearrange("p t (h d) -> p (t h) d", d=HD)
                kf = kraw[:, :, :].rearrange("p t d -> p (t d)")
                dve.wait_ge(S["k_biased"], 1)
                own.link(dve.tensor_reduce(kmax[:, :], kg, AX.X, ALU.max, apply_absolute_value=True))
                own.link(dve.tensor_scalar(ks[:, :], kmax[:, :], 1.0 / 127.0, 1e-8, ALU.mult, ALU.max))
                dve.reciprocal(krs[:, :], ks[:, :]).then_inc(S["k_scales"], 1)
                yield
                dve.wait_ge(S["kv_plain"], 8)
                own.link(dve.tensor_reduce(sv[:, :], vt[:, :, :], AX.X, ALU.max, apply_absolute_value=True))
                own.link(dve.tensor_scalar(sv[:, :], sv[:, :], 1.0 / 127.0, 1e-8, ALU.mult, ALU.max))
                own.link(dve.reciprocal(rsv[:, :], sv[:, :]))
                yield
                dve.wait_ge(S["k_steps"], 1)
                dve.tensor_scalar(kf, kf, MAGIC, -MAGIC, ALU.add, ALU.add).then_inc(S["k_scales"], 1)
                yield
                for part in range(3):
                    if part < NK:
                        k = part
                        own.link(dve.tensor_scalar(vt[:, k, :], vt[:, k, :], rsv[:, k:k + 1], MAGIC, ALU.mult, ALU.add))
                        dve.tensor_scalar(vround[:, k, :], vt[:, k, :], -MAGIC, None, ALU.add).then_inc(S["v_round"], 1)
                    yield
                    dve.wait_ge(S["k_steps"], part + 2)
                    dve.tensor_copy(kparts[:, :, part, 0:D], kraw[:, :, :]).then_inc(S["k_ready"], 1)
                    yield

            for h in range(2):
                dve.wait_ge(S[f"x_in{h}"], 16)
                moments(h)
            norm(0)
            dve.wait_ge(S["tok_in"], 16)
            masks = mask_steps()
            next(masks)
            kv = key_value_steps()
            for entry in ORDER[:ATTENTION]:
                kind, n = entry[0], FIRST[entry]
                if kind == "norm":
                    layer, q = entry[1:]
                    if q == 0 and layer:
                        for h in range(2):
                            add_sums(layer - 1, h)
                            moments(h)
                        norm(layer)
                    norm_lows(entry)
                    if q == 3 and layer == 0:
                        control_lows(0)
                elif kind == "z":
                    j = entry[1]
                    if j:
                        lows(j - 1)
                    product(j, n, n)
                    next(masks, None)
                    if j == 15:
                        lows(j)
                elif kind == "gu":
                    j = entry[1]
                    product(j, n, n + 1)
                    lows(j)
                    next(kv, None)
                elif kind == "spline":
                    k = entry[1]
                    if k == 0:
                        dve.wait_ge(S["side_in"], 16)
                    dve.wait_ge(S["filled"], n + 2)
                    c, h = k // 2 % 2, k % 2
                    dve.copy_predicated(bank[n % RING], half(side[:, c, :], h),
                                        bank[(n + 1) % RING]).then_inc(S["selected"], 1)
                    if k + 1 < 12:
                        control_lows(k + 1)
                    dve.wait_ge(S["piece_high"], k + 1)
                    o, raw = piece(k, False)
                    sub(o, raw, piece(k, True)[0], "drained", 2)
                    if k == 2:
                        dve.wait_ge(S["wkv_high"], 1)
                        sub(wkvl[:, :, :], wkvraw[:, :, :], wkvh[:, :, :], "wkv_low")
                elif kind == "vturn":
                    k = entry[1]
                    if k == 0:
                        for _ in kv:
                            pass
                    dve.wait_ge(S["filled"], n + 1)
                    dve.tensor_copy(vint[:, :, k * P:(k + 1) * P],
                                    bank[n % RING].bitcast(BF16).rearrange("p (t d) -> p t d", t=NT))\
                       .then_inc(S["drained"], 1)
                elif kind == "query":
                    q = entry[1]
                    if q == 0:
                        dve.wait_ge(S["wq_in"], 32)
                        dve.wait_ge(S["zeroed"], 9)
                    dve.wait_ge(S["filled"], n + 1)
                    dve.tensor_tensor(qraw[:, 2 * q:2 * q + 2, :], bank[n % RING].rearrange("p (t d) -> p t d", t=2),
                                      bqb[:, :].unsqueeze(1).broadcast_to((P, 2, D)), ALU.add).then_inc(S["drained"], 1)
                    dve.wait_ge(S["drained"], drained(n))
                    own.mark(dve.tensor_reduce(qmax[:, 2 * q:2 * q + 2, :],
                                               qraw[:, 2 * q:2 * q + 2, :].rearrange("p t (h d) -> p t h d", d=HD),
                                               AX.X, ALU.max, apply_absolute_value=True))

            own.wait()
            qg = qraw[:, :, :].rearrange("p t (h d) -> p t h d", d=HD)
            own.link(dve.tensor_scalar(qs[:, :, 0:HEADS], qmax[:, :, :], 0.25 / 127.0, 1e-8, ALU.mult, ALU.max))
            own.mark(dve.tensor_scalar(nqs[:, :, 0:HEADS], qs[:, :, 0:HEADS], -1.0, None, ALU.mult))
            own.link(dve.reciprocal(qrs[:, :, :], qs[:, :, 0:HEADS]))
            own.link(dve.tensor_scalar(qrs[:, :, :], qrs[:, :, :], 0.25, None, ALU.mult))
            for a, b in ((0, 2), (2, HEADS)):
                own.link(dve.tensor_tensor(qg[:, :, a:b, :], qg[:, :, a:b, :],
                                           qrs[:, :, a:b].unsqueeze(3).broadcast_to((P, NT, b - a, HD)), ALU.mult))
                dve.tensor_scalar(qint[:, :, a * HD:b * HD], qraw[:, :, a * HD:b * HD], MAGIC, -MAGIC,
                                  ALU.add, ALU.add).then_inc(S["q_ready"], 1)

            def evac_vector(g, t, fresh):
                dve.wait_ge(S["turn_done"], g + 1)
                if not fresh:
                    dve.wait_ge(S["mix_done"], g - 3)
                dve.tensor_copy(pT[t % 4][:, :], turned.bitcast(U16)).then_inc(S["evac_v"], 1)

            def head_scale(h, n):
                dve.wait_ge(S["exped"], 8 * (h + 1))
                own.link(dve.reciprocal(rz[n][:, :], zsum[n][:, :]))
                own.mark(dve.tensor_scalar(rz[n][:, :], rz[n][:, :], 1e-8, None, ALU.max))

            def head_output(h, n):
                dve.wait_ge(S["mix_done"], 8 * h + 8)
                dve.tensor_tensor(O[:, :, bass.ds(h * HD, HD)], mixed.rearrange("p (t d) -> p t d", t=NT),
                                  rz[n][:, :].unsqueeze(2).broadcast_to((P, NT, HD)), ALU.mult).then_inc(S["head_out"], 1)

            def head_vector(h, n, first, g0):
                begin = first and n == 0
                dve.wait_ge(S["built"], 4 * h + 4)
                for t in range(NT):
                    g = g0 + t
                    dve.wait_ge(S["scored"], g + 1)
                    if not (first and n == 0 and t < 4):
                        dve.wait_ge(S["exped"], g - 3)
                    own.mark(dve.reduce_max(smax[t % 4][:, 0:1], scores[tile_slot[t]], AX.X))
                    read = own.n
                    if t == 2 and not begin:
                        head_scale(h - 1, 1 - n)
                    if t == 6:
                        dve.wait_ge(S["prepped"], h + 2)
                        dve.tensor_copy(qT[1 - n][:, :], bank[2 * prep_slot].bitcast(BF16)).then_inc(S["qT_ready"], 1)
                    own.wait_for(read)
                    dve.tensor_scalar(smax[t % 4][:, 1:2], smax[t % 4][:, 0:1], nqsh[n][:, t:t + 1], LOG255,
                                      ALU.mult, ALU.add).then_inc(S["maxed"], 1)
                    if t % 2 and not (begin and t == 1):
                        evac_vector(g - 3, (t - 3) % 8, begin and t < 7)
                    if t == 3 and not begin:
                        own.wait()
                        head_output(h - 1, 1 - n)

            dve.wait_ge(S["prepped"], 1)
            dve.tensor_copy(qT[0][:, :], bank[2 * prep_slot].bitcast(BF16)).then_inc(S["qT_ready"], 1)
            head_vector(0, 0, True, 0)
            head_vector(1, 1, True, 8)
            before = own.n
            with dve.Fori(1, HEADS // 2) as i:
                own.loop = (i - 1) * PAIR_STEPS
                head_vector(2 * i, 0, False, 16 * i)
                head_vector(2 * i + 1, 1, False, 16 * i + 8)
            assert own.n - before == PAIR_STEPS
            own.n, own.loop = before + (HEADS // 2 - 1) * PAIR_STEPS, 0
            evac_vector(8 * HEADS - 2, 6, False)
            head_scale(HEADS - 1, 1)
            own.wait()
            head_output(HEADS - 1, 1)

            for q in range(4):
                n = FIRST[("oturn", q)]
                dve.wait_ge(S["o_high"], q + 1)
                dve.scalar_tensor_tensor(half(hl[:, q % 2, :], q // 2), bank[n % RING], sv[:, q % 2:q % 2 + 1],
                                         plain(half(hh[:, q % 2, :], q // 2)), ALU.mult, ALU.subtract).then_inc(S["drained"], 1)
            dve.wait_ge(S["bp_added"], 1)
            for h in range(2):
                for q in (2 * h, 2 * h + 1):
                    n = FIRST[("proj", q)]
                    dve.wait_ge(S["filled"], n + 1)
                    o = X[:, 2 * q:2 * q + 2, :].rearrange("p t d -> p (t d)")
                    dve.tensor_tensor(o, o, bank[n % RING], ALU.add).then_inc(S["drained"], 1)
                dve.wait_ge(S["drained"], drained(n))
                moments(h)
            norm(3)
            for q in range(4):
                norm_lows(("norm", 3, q))
            for q in range(2):
                n = FIRST[("latent", q)]
                dve.wait_ge(S["latent_high"], q + 1)
                sub(half(xll[:, :], q), bank[n % RING], half(xlh[:, :], q), "drained")
            def stage_in(e, n, first):
                if not first:
                    dve.wait_ge(S["filled"], MOE0 + 4 * (e - 1))
                dve.tensor_copy(e1s[n][:, :, :], plain(e1[:, bass.ds(e, 1), :, :].rearrange("p o a b -> p (o a) b")))\
                   .then_inc(S["stage_in"], 1)

            def stage_out(e, n, first):
                if not first:
                    dve.wait_ge(S["expert_sum"], 2 * (e - 1))
                dve.tensor_copy(e2s[n][:, :, :], plain(e2[:, bass.ds(e, 1), :, :].rearrange("p o a b -> p (o a) b")))\
                   .then_inc(S["stage_out"], 1)

            dve.wait_ge(S["e1_low"], 4)
            dve.wait_ge(S["moe_low"], 7)
            for n in range(2):
                stage_in(n, n, True)
                stage_out(n, n, True)
            dve.wait_ge(S["probs"], 1)
            dve.tensor_tensor(pick[:, :, :], prob[:, :, :], biasb[:, :].unsqueeze(1).broadcast_to((P, NT, NE)),
                              ALU.add).then_inc(S["drained"], 1)
            dve.wait_ge(S["drained"], drained(FIRST[("router", 0)]))
            for t in range(NT):
                own.mark(dve.max(top8[:, t, :], pick[:, t, :]))
            own.wait()
            for t in range(NT):
                own.mark(dve.match_replace(left[:, t, :], top8[:, t, :], pick[:, t, :], -3.0e38))
            own.wait()
            own.link(dve.tensor_tensor(pick[:, :, :], pick[:, :, :], left[:, :, :], ALU.not_equal))
            own.link(dve.tensor_tensor(prob[:, :, :], prob[:, :, :], pick[:, :, :], ALU.mult))
            own.link(dve.reduce_sum(psum8[:, :], prob[:, :, :], AX.X))
            own.link(dve.reciprocal(psum8[:, :], psum8[:, :]))
            own.link(dve.tensor_scalar(psum8[:, :], psum8[:, :], RSCALE, None, ALU.mult))
            dve.tensor_tensor(prob[:, :, :], prob[:, :, :], psum8[:, :].unsqueeze(2).broadcast_to((P, NT, NE)),
                              ALU.mult).then_inc(S["weights"], 1)
            for q in range(2):
                n = FIRST[("gu", 32 + q)]
                product(32 + q, n, n + 1)
            for q in range(2):
                n = FIRST[("wturn", q)]
                dve.wait_ge(S["filled"], n + 1)
                dve.tensor_copy(half(wT[:, :], q), bank[n % RING][0:NE, :]).then_inc(S["drained"], 1)
            for q in range(2):
                j = 32 + q
                dve.wait_ge(S["high_ready"], j + 1)
                sub(half(sh_l, q), prod[j % NH][:, :], half(sh_h, q), "low_ready")

            def hidden(k, u, first):
                dve.wait_ge(S["squared"], 2 + k + 1)
                dve.wait_ge(S["filled"], MOE0 + 2 * k + 2)
                if not first:
                    dve.wait_ge(S["expert_high"], k - 3)
                    dve.wait_ge(S["expert_low"], k - 3)
                dve.tensor_tensor(hp[u], sq[u], ups[u], ALU.mult).then_inc(S["drained"], 2)

            def expert_vector(k, e, u, first):
                if u % 2 and within(k + 2) and not (first and u == 1):
                    stage_out(e + 1, 1 - u // 2, False)
                dve.wait_ge(S["expert_high"], k + 1)
                if not first:
                    dve.wait_ge(S["expert_sum"], k - 3)
                sub(el[u], hp[u], eh[u], "expert_low")
                if within(k + LEAD):
                    hidden(k + LEAD, (u + LEAD) % 4, first and u + LEAD < 4)
                if u % 2 == 0 and within(k + 6):
                    stage_in(e + 3, 1 - u // 2, False)

            for k in range(LEAD):
                hidden(k, k, True)
                if k == 1:
                    stage_in(2, 0, False)
            expert_halves(dve, expert_vector)
            for h in range(2):
                dve.wait_ge(S["acc_high"], h + 1)
                sub(half(al, h), bank[4 + h], half(ah, h), "acc_low")
            for q in range(4):
                dve.wait_ge(S["filled"], FINAL0 + q + 1)
                o = (slice(None), slice(2 * q, 2 * q + 2), slice(None))
                dve.tensor_tensor(res[o].rearrange("p t d -> p (t d)"), X[o].rearrange("p t d -> p (t d)"),
                                  bank[(FINAL0 + q) % RING], ALU.add).then_inc(S["res_ready"], 1)

        @block.tensor
        def _(pe):
            def free(n, count=1):
                for b in range(n, n + count):
                    if b >= RING:
                        last = b - RING
                        if last in KV:
                            pe.wait_ge(S["kv_plain"], KV.index(last) + 1)
                        else:
                            pe.wait_ge(S["drained"], drained(last))

            def mm3(o, lhs, rhs, start, stop, group=True):
                pe.matmul(o, lhs[0], rhs[0], start=start, stop=False, skip_group_check=not group)
                pe.matmul(o, lhs[0], rhs[1], start=False, stop=False, skip_group_check=not group)
                return pe.matmul(o, lhs[1], rhs[0], start=False, stop=stop, skip_group_check=not group)

            def both(h, l, *ix):
                return h[ix], l[ix]

            ALL = slice(None)

            def cols(a, n=P):
                return slice(a, a + n)

            def normal(k, h):
                return both(hh, hl, ALL, k, cols(h * HALF, HALF))

            def norm_turns(entry, src):
                n, q = FIRST[entry], entry[-1]
                free(n)
                k, h = q % 2, q // 2
                for t in range(4):
                    mm = pe.transpose(bank[n % RING][:, t * P:(t + 1) * P], src[:, 4 * h + t, k * P:(k + 1) * P], idf[:, :])
                mm.then_inc(S["filled"], 1)

            def projected(n, o_lhs, o_rhs, extra=None):
                free(n)
                for t in range(2):
                    o = bank[n % RING][:, t * D:(t + 1) * D]
                    for k in range(NK):
                        mm = mm3(o, o_lhs(k, t), o_rhs(k), k == 0, k == NK - 1)
                mm.then_inc(S["filled"], 1)

            def sums(j, lhs, rhs, first, last):
                pe.wait_ge(S["low_ready"], j + 1)
                pe.wait_ge(S["high_ready"], j + 1)
                for t in range(4):
                    tile = 4 * (j % 2) + t
                    o = bank[4 + tile // 2][:, (tile % 2) * D:(tile % 2 + 1) * D]
                    mm = mm3(o, lhs(t), rhs, first and tile % 2 == 0, last, group=False)
                mm.then_inc(S["summed"], 1)

            def hidden_parts(j):
                return lambda t: both(ph[j % NH], pl[j % NH], ALL, cols(t * P))

            pe.wait_ge(S["ident_in"], 16)
            for entry in ORDER[:ATTENTION]:
                kind, n = entry[0], FIRST[entry]
                if kind == "norm":
                    layer, q = entry[1:]
                    pe.wait_ge(S["norm_rest" if q > 1 else "norm_ready"], 4 * layer + 4)
                    norm_turns(entry, xn)
                elif kind == "z":
                    j = entry[1]
                    e, f, h = j // 4, j // 2 % 2, j % 2
                    if j == 0:
                        pe.wait_ge(S["ctx_low"], 1)
                    if j < 2:
                        pe.wait_ge(S["drained"], drained(FIRST[("norm", 0, 2 * h + 1)]))
                    free(n)
                    for k in range(NK):
                        mm = mm3(bank[n % RING], both(ch, cl, ALL, k, cols(e * D + f * P)), normal(k, h), k == 0, k == 1)
                    mm.then_inc(S["filled"], 1)
                elif kind == "y":
                    j = entry[1]
                    if j < 16:
                        e, f = j // 4, j // 2 % 2
                        sums(j, hidden_parts(j), both(ch, cl, ALL, f, cols(e * D, D)), j < 2, j >= 14)
                    else:
                        if j == 16:
                            pe.wait_ge(S["residual"], 1)
                            pe.wait_ge(S["drained"], drained(FIRST[("spline", 11)] + 1))
                        sums(j, hidden_parts(j), both(dnh, dnl, ALL, (j - 16) // 2), j < 18, j >= 30)
                elif kind == "gu":
                    j = entry[1]
                    c, h = (j - 16) // 2, j % 2
                    if j == 16:
                        pe.wait_ge(S["drained"], drained(FIRST[("spline", 7)] + 1))
                    if j < 18:
                        pe.wait_ge(S["drained"], drained(FIRST[("norm", 1, 2 * h + 1)]))
                    free(n, 2)
                    for m in range(2):
                        for k in range(NK):
                            mm = mm3(bank[(n + m) % RING], both(w3h[m], w3l[m], ALL, k, cols(c * P)), normal(k, h), k == 0, k == 1)
                        mm.then_inc(S["filled"], 1)
                elif kind == "spline":
                    k = entry[1]
                    if k == 0:
                        pe.wait_ge(S["ctx_high"], 2)
                    free(n, 2)
                    pe.wait_ge(S["control_low"], k + 1)
                    for s in range(2):
                        pe.matmul(bank[(n + s) % RING], u_r[:, s, :], dst[k % 2][:, :],
                                  start=True, stop=True).then_inc(S["filled"], 1)
                elif kind == "key":
                    q = entry[1]
                    if q == 0:
                        pe.wait_ge(S["wkv_low"], 1)
                    projected(n, lambda k, t: both(ch, cl, ALL, k, cols((2 * q + t) * P)),
                              lambda k: both(wkvh, wkvl, ALL, k, cols(0, D)))
                elif kind == "value":
                    q = entry[1]
                    free(n)
                    for k in range(NK):
                        mm = mm3(bank[n % RING], both(wkvh, wkvl, ALL, k, cols(D + q // 2 * P)),
                                 both(ch, cl, ALL, k, cols(q % 2 * HALF, HALF)), k == 0, k == 1)
                    mm.then_inc(S["filled"], 1)
                elif kind == "vturn":
                    k = entry[1]
                    free(n)
                    pe.wait_ge(S["v_round"], k + 1)
                    pe.wait_ge(S["identb"], 1)
                    for t in range(NT):
                        mm = pe.transpose(bank[n % RING].bitcast(BF16)[:, t * P:(t + 1) * P],
                                          vround[:, k, t * P:(t + 1) * P], idb[:, :])
                    mm.then_inc(S["filled"], 1)
                elif kind == "query":
                    q = entry[1]
                    if q == 0:
                        pe.wait_ge(S["wq_low"], 1)
                    if q % 2 == 0:
                        pe.wait_ge(S["drained"], drained(FIRST[("norm", 2, q + 1)]))
                    projected(n, lambda k, t: both(hh, hl, ALL, k, cols((2 * q + t) * P)),
                              lambda k: both(wqh, wql, ALL, k))

            def prepare(h, n):
                pe.wait_ge(S["built"], 4 * h + 2)
                for src, b in ((xq[n], 0), (xk[n], 1)):
                    o = bank[2 * prep_slot + b].bitcast(BF16)
                    for t in range(NT):
                        mm = pe.transpose(o[:, t * P:(t + 1) * P], src[:, t, :], idb[:, :])
                mm.then_inc(S["prepped"], 1)

            def turn(g, t, fresh, done):
                if not fresh:
                    pe.wait_ge(S["evac_v"] if t % 2 else S["evac_a"], done)
                pe.wait_ge(S["exped"], g + 1)
                for c in range(NT):
                    mm = pe.transpose(turned[:, c * P:(c + 1) * P],
                                      pu[t % 4][:, c * P:(c + 1) * P].bitcast(BF16), idb[:, :])
                mm.then_inc(S["turn_done"], 1)

            def mix(t, h, done):
                pe.wait_ge(S["evac_a"] if t % 2 else S["evac_v"], done)
                for c in range(NT):
                    mm = pe.matmul(mixed[:, t * HD:(t + 1) * HD], pT[t % 4][:, c * P:(c + 1) * P],
                                   vint[:, c, bass.ds(h * HD, HD)], start=c == 0, stop=c == NT - 1)
                mm.then_inc(S["mix_done"], 1)

            def head_tensor(h, n, first, g0, e0):
                begin = first and n == 0
                for t in range(NT):
                    g = g0 + t
                    if t in (0, 6) and not (begin and t == 0):
                        turn(g - 4, (t - 4) % 8, False, e0 + (t - 3) // 2)
                    if t and not (begin and t < 3):
                        pe.wait_ge(S["exped"], g - 1 if t > 5 else g - 2)
                    if t == 0:
                        pe.wait_ge(S["qT_ready"], h + 1)
                        pe.wait_ge(S["kT_ready"], h + 1)
                    for b in range(2):
                        mm = pe.matmul(scores[tile_slot[t]][:, b * HALF:(b + 1) * HALF],
                                       qT[n][:, t * P:(t + 1) * P], kT[n][:, b * HALF:(b + 1) * HALF],
                                       start=True, stop=True)
                    mm.then_inc(S["scored"], 1)
                    if t in (2, 4) and not (begin and t < 4):
                        turn(g - 4, (t - 4) % 8, begin and t == 4, e0 + (t - 3) // 2)
                    if not (begin and t < 5):
                        if t == 5 and not begin:
                            pe.wait_ge(S["head_out"], h)
                        mix((t - 5) % 8, h - 1 if t < 5 else h, e0 + (t - 5) // 2 + 1)
                    if t % 2 == 0 and not (begin and t < 4):
                        turn(g - 3, (t - 3) % 8, False, e0 + (t - 2) // 2)
                    if t == 5:
                        pe.wait_ge(S["exped"], g - 1)
                        prepare(h + 1, 1 - n)

            pe.wait_ge(S["drained"], drained(FIRST[("query", 3)]))
            prepare(0, 0)
            head_tensor(0, 0, True, 0, 0)
            head_tensor(1, 1, True, 8, 4)
            with pe.Fori(1, HEADS // 2) as i:
                head_tensor(2 * i, 0, False, 16 * i, 8 * i)
                head_tensor(2 * i + 1, 1, False, 16 * i + 8, 8 * i + 4)
            last = 8 * HEADS
            half_last = last // 2
            turn(last - 4, 4, False, half_last - 2)
            mix(3, HEADS - 1, half_last - 2)
            for t in (5, 6, 7):
                turn(last - 8 + t, t, False, half_last - 4 + (t + 1) // 2)
                mix(t - 1, HEADS - 1, half_last - 4 + (t + 1) // 2)
            mix(7, HEADS - 1, half_last)

            pe.wait_ge(S["head_out"], HEADS)
            for q in range(4):
                norm_turns(("oturn", q), O)
            pe.wait_ge(S["moe_low"], 7)
            for q in range(4):
                n = FIRST[("proj", q)]
                if q % 2 == 0:
                    pe.wait_ge(S["drained"], drained(FIRST[("oturn", q + 1)]))
                projected(n, lambda k, t: both(hh, hl, ALL, k, cols((2 * q + t) * P)), lambda k: both(wph, wpl, ALL, k))
            for q in range(4):
                pe.wait_ge(S["norm_rest" if q > 1 else "norm_ready"], 16)
                norm_turns(("norm", 3, q), xn)
            for h in range(2):
                n = FIRST[("latent", h)]
                pe.wait_ge(S["drained"], drained(FIRST[("norm", 3, 2 * h + 1)]))
                free(n)
                for k in range(NK):
                    mm = mm3(bank[n % RING], both(wdh, wdl, ALL, k), normal(k, h), k == 0, k == 1)
                mm.then_inc(S["filled"], 1)
            n = FIRST[("router", 0)]
            free(n)
            for t in range(NT):
                for k in range(NK):
                    mm = mm3(bank[n % RING][:, t * NE:(t + 1) * NE], both(hh, hl, ALL, k, cols(t * P)), both(wgh, wgl, ALL, k),
                             k == 0, k == 1)
            mm.then_inc(S["filled"], 1)
            for h in range(2):
                n = FIRST[("gu", 32 + h)]
                free(n, 2)
                for m in range(2):
                    for k in range(NK):
                        mm = mm3(bank[(n + m) % RING], both(swh, swl, ALL, k, m), normal(k, h), k == 0, k == 1)
                    mm.then_inc(S["filled"], 1)
            for q in range(2):
                n = FIRST[("wturn", q)]
                free(n)
                pe.wait_ge(S["weights"], 1)
                for t in range(4):
                    mm = pe.transpose(bank[n % RING][0:NE, t * P:(t + 1) * P], prob[:, 4 * q + t, :], idf[:, :])
                mm.then_inc(S["filled"], 1)

            def gates_ups(k, e, u, first):
                if u % 2 == 0:
                    pe.wait_ge(S["stage_in"], e + 1)
                for m in range(2):
                    if m == 0 and not (first and u < 2):
                        pe.wait_ge(S["rectified"], k - 1)
                    elif m:
                        pe.wait_ge(S["drained"], drained(MOE0) - 1 + (0 if first else 2 * (k - 3)))
                    o = ups[u] if m else gates_of[u % 2]
                    pe.matmul(o, e1s[u // 2][:, m, :], half(xlh[:, :], u % 2), start=True, stop=False)
                    pe.matmul(o, e1s[u // 2][:, m, :], half(xll[:, :], u % 2), start=False, stop=True).then_inc(S["filled"], 1)

            def expert_tensor(k, e, u, first):
                if within(k + LEAD + 1):
                    gates_ups(k + LEAD + 1, e + (u % 2 + LEAD + 1) // 2, (u + LEAD + 1) % 4, False)
                if u % 2 == 0:
                    pe.wait_ge(S["stage_out"], e + 1)
                pe.wait_ge(S["expert_low"], k + 1)
                begin = first and u < 2
                last = not within(k + 2)
                w = e2s[u // 2][:, :, :].rearrange("p a b -> p (a b)")
                o = bank[4 + u % 2]
                pe.matmul(o, w, eh[u], start=begin, stop=False, skip_group_check=True)
                pe.matmul(o, w, el[u], start=False, stop=last, skip_group_check=True).then_inc(S["expert_sum"], 1)

            for k in range(LEAD + 1):
                gates_ups(k, k // 2, k, True)
            expert_halves(pe, expert_tensor)
            pe.wait_ge(S["acc_low"], 2)
            for q in range(4):
                n = FINAL0 + q
                if q == 0:
                    pe.wait_ge(S["drained"], drained(FINAL0 - 1))
                for t in range(2):
                    tile = cols((2 * q + t) * P)
                    o = bank[n % RING][:, t * D:(t + 1) * D]
                    mm3(o, both(sh_h, sh_l, ALL, tile), both(s2h, s2l, ALL), True, False)
                    mm = mm3(o, both(ah, al, ALL, tile), both(wuh, wul, ALL), False, True)
                mm.then_inc(S["filled"], 1)


def kernel(**inputs):
    import concourse.bacc as bacc
    from concourse.bass_utils import run_bass_kernel_spmd as run

    a = {k: np.asarray(v) for k, v in inputs.items()}
    turned = lambda v: np.ascontiguousarray(np.swapaxes(v, -1, -2))
    by_input = lambda v: np.ascontiguousarray(v.transpose(2, 0, 1))
    table, stacked, upper = spline_tables()
    i = np.arange(INTER)
    side, k = np.arange(P)[:, None, None] // 32 % 2, np.arange(P)[:, None, None] % 16 // 4
    at = (127 * (i // 64) + 2 * (i % 64))[None, None, :] + np.arange(2)[None, :, None] + side - 1 + k - 1
    at = np.clip(at, 0, NCP - 1)
    cpw = np.stack([a[f"L0_ffn_{m}_cp"][at] for m in ("gate", "up", "down")])
    arrays = {
        "x": np.ascontiguousarray(a["x"].reshape(T, D)),
        "ident": np.eye(P, dtype=np.float32),
        "ctx_t": turned(a["ctx_2048"].reshape(T, D)),
        "tok": np.ascontiguousarray(a["itok_BxS_13_99985"].reshape(T)),
        "cpw": cpw, "table": table, "stacked": stacked, "upper": np.ascontiguousarray(upper),
        "wq": a["L1_xattn_Wq"], "bq": a["L1_xattn_bq"], "wkv": a["L1_xattn_Wkv"], "bkv": a["L1_xattn_bkv"],
        "bv_t": turned(a["L1_xattn_bkv"][D:].reshape(NK, P)),
        "wp": a["L1_xattn_Wp"], "bp": a["L1_xattn_bp"],
        "sw1_t": turned(a["L1_ffn_sw1"]), "swg_t": turned(a["L1_ffn_swg"]), "sw2_t": turned(a["L1_ffn_sw2"]),
        "rw1_t": by_input(a["L1_ffn_rw1"]), "rwg_t": by_input(a["L1_ffn_rwg"]), "rw2_t": by_input(a["L1_ffn_rw2"]),
        "wg_t": turned(a["L1_ffn_Wg"]), "wdown_t": turned(a["L1_ffn_Wdown"]), "wup_t": turned(a["L1_ffn_Wup"]),
        "biases": a["L1_ffn_biases"],
    }
    nc = bacc.Bacc("TRN2", target_bir_lowering=False, num_devices=1)
    args = {n: nc.dram_tensor(f"in_{n}", v.shape, mybir.dt.from_np(v.dtype), kind="ExternalInput").ap()
            for n, v in arrays.items()}
    out = nc.dram_tensor("out", (T, D), FP32, kind="ExternalOutput").ap()
    build(nc, out=out, **args)
    r = run(nc, [{f"in_{n}": v for n, v in arrays.items()}], core_ids=[0])
    return r.results[0]["out"].reshape(a["x"].shape)
```

```python
import math
from contextlib import ExitStack

import numpy as np
import concourse.bass as bass
from concourse import mybir

FP32, FP32R, BF16 = mybir.dt.float32, mybir.dt.float32r, mybir.dt.bfloat16
I32, U16, U8 = mybir.dt.int32, mybir.dt.uint16, mybir.dt.uint8
ACT, ALU, AX = mybir.ActivationFunctionType, mybir.AluOpType, mybir.AxisListType

P = 128
T, D = 1024, 256
NT, NK = T // P, D // P
HALF = 512
NE0 = 4
VOCAB = 12500
INTER = 1024
NC = INTER // P
NCP = int(INTER * D / 128.9)
HEADS, HD = 16, 16
NE, LAT, HID, TOPK = 16, 64, 128, 8
RSCALE = 2.5
EPS = 1e-5
MAGIC = 12582912.0
RING = 4


def spline_tables():
    n = T * D
    t = np.linspace(0.0, NCP - 1.0, n, dtype=np.float64)
    seg = np.clip(np.floor(t).astype(np.int64), 0, NCP - 2).reshape(INTER, 2, P)
    step = (NCP - 1.0) / (n - 1)
    i = np.arange(INTER)
    first = 127 * (i // 64) + 2 * (i % 64)
    cr = 0.5 * np.array([[0, -1, 2, -1], [2, 0, -5, 3], [0, 1, 4, -3], [0, 0, -1, 1]], np.float64)
    a = np.zeros((4, 4, 2, 2, INTER))
    for c in range(2):
        middle = (256.0 * i + 128.0 * c + 63.5) * step
        for side in range(2):
            g = middle - (first - 1 + c + side)
            for q in range(4):
                for p in range(q, 4):
                    a[:, q, side, c] += cr[:, p, None] * math.comb(p, q) * g ** (p - q)
    u = ((np.arange(P) - 63.5) * step)[None, :] ** np.arange(4)[:, None]
    high = round_12(np.tile(u, (4, 1)).astype(np.float32))
    low = round_12((np.tile(u, (4, 1)) - high).astype(np.float32))
    stacked = np.zeros((2, 2, 2, 16, P), np.float32)
    by_side = np.zeros((P, 2, P), np.float32)
    for side in range(2):
        stacked[:] = 0.0
        stacked[:, side, 0], stacked[:, side, 1] = high, low
        by_side[:, side] = stacked.reshape(P, P)
    upper = (seg - (first[:, None, None] - 1 + np.arange(2)[None, :, None])).transpose(2, 1, 0)
    assert upper.min() == 0 and upper.max() == 1
    by_row = a.reshape(16, 2, 2, INTER).transpose(1, 0, 2, 3)
    table = np.broadcast_to(by_row[None, :, None], (2, 2, 2, 16, 2, INTER)).reshape(P, 2, INTER).astype(np.float32)
    return table, by_side, upper.astype(np.int32)


def round_12(x):
    b = x.view(np.uint32).astype(np.uint64)
    b = (b + 0x7FF + ((b >> 12) & 1)) & 0xFFFFF000
    return b.astype(np.uint32).view(np.float32)


class Chain:

    def __init__(self, eng, sem):
        self.eng, self.sem, self.n, self.loop = eng, sem, 0, 0

    def mark(self, ins):
        ins.then_inc(self.sem, 1)
        self.n += 1

    def wait(self):
        self.eng.wait_ge(self.sem, self.loop + self.n)

    def link(self, ins):
        self.mark(ins)
        self.wait()


def schedule():
    order = [("norm", 0, n) for n in range(4)]
    order += [("z", j) for j in range(3)] + [("spline", 0)]
    for j in range(16):
        if j + 3 < 16:
            order.append(("z", j + 3))
        order.append(("y", j))
        if 1 + j < 12:
            order.append(("spline", 1 + j))
    order += [("key", n) for n in range(4)] + [("value", 0), ("value", 1)]
    order += [("norm", 1, n) for n in range(4)] + [("value", 2), ("value", 3), ("gu", 16)]
    for j in range(16, 32):
        if j + 1 < 32:
            order.append(("gu", j + 1))
        order.append(("y", j))
        if j == 29:
            order += [("vturn", 0), ("vturn", 1)]
    order += [("norm", 2, n) for n in range(4)] + [("query", n) for n in range(4)]
    order += [("oturn", n) for n in range(4)] + [("proj", n) for n in range(4)]
    order += [("norm", 3, n) for n in range(4)]
    order += [("router", 0), ("latent", 0), ("latent", 1), ("gu", 32), ("wturn", 0), ("wturn", 1), ("gu", 33)]
    return order


BANKS = {"spline": 2, "gu": 2, "y": 0}
ORDER = schedule()
FIRST, _n = {}, 0
for _entry in ORDER:
    FIRST[_entry] = _n
    _n += BANKS.get(_entry[0], 1)
MOE0 = _n
FINAL0 = MOE0 + 4 * NE
KV = sorted(FIRST[e] for e in ORDER if e[0] in ("key", "value"))
ATTENTION = ORDER.index(("query", 3)) + 1


def drained(n):
    return n + 1 - sum(k <= n for k in KV)


def build(nc, x, ident, ctx_t, tok, cpw, table, stacked, upper, wq, bq, wkv, bkv, bv_t, wp, bp,
          sw1_t, swg_t, sw2_t, rw1_t, rwg_t, rw2_t, wg_t, wdown_t, wup_t, biases, out):
    x_v = x.rearrange("(t p) d -> p t d", p=P)
    out_v = out.rearrange("(t p) d -> p t d", p=P)
    wrow = nc.dram_tensor("router_rows", (NE, T), FP32, kind="Internal").ap()

    es = ExitStack()
    with es:
        limit = nc.sbuf_usable_end
        at = {"": (nc.sbuf_base + 63) // 64 * 64}

        def place(region, name, shape, dt):
            size = int(np.prod(shape[1:])) * {FP32: 4, FP32R: 4, I32: 4, BF16: 2, U16: 2, U8: 1}[dt]
            offset = at[region]
            at[region] = offset + (size + 63) // 64 * 64
            assert at[region] <= limit, (name, at[region], limit)
            return nc.alloc_sbuf_tensor_at(name, shape, dt, offset=offset)

        def sem(name):
            return es.enter_context(nc.semaphore(name))

        X = place("", "X", [P, NT, D], FP32)
        xn = place("", "xn", [P, NT, D], FP32)
        hh = place("", "hh", [P, NK, T], FP32R)
        hl = place("", "hl", [P, NK, T], FP32R)
        idf = place("", "idf", [P, P], FP32)
        idb = place("", "idb", [P, P], BF16)
        NH = 3
        gate_s = [place("", f"gate_s{n}", [P, HALF], FP32) for n in range(NH)]
        prod = [place("", f"prod{n}", [P, HALF], FP32) for n in range(NH)]
        ph = [place("", f"ph{n}", [P, HALF], FP32R) for n in range(NH)]
        pl = [place("", f"pl{n}", [P, HALF], FP32R) for n in range(NH)]
        stats = place("", "stats", [P, NT, 6], FP32)
        mv = place("", "mv", [P, NT, 2], FP32)
        std = place("", "std", [P, NT], FP32)
        shift = place("", "shift", [P, NT], FP32)
        rstd = place("", "rstd", [P, NT], FP32)
        eps = place("", "eps", [P, 1], FP32)
        kparts = place("", "kparts", [P, NT, 3, D + HD], BF16)
        vint = place("", "vint", [P, NT, D], BF16)
        sv = place("", "sv", [P, NK], FP32)
        rsv = place("", "rsv", [P, NK], FP32)
        bk = place("", "bk", [P, D], FP32)
        bv = place("", "bv", [P, NK], FP32)
        base = at[""]
        at["A"] = base
        ch = place("A", "ch", [P, NK, T], FP32R)
        cl = place("A", "cl", [P, NK, T], FP32R)
        wkvh = place("A", "wkvh", [P, NK, 2 * D], FP32R)
        wkvl = place("A", "wkvl", [P, NK, 2 * D], FP32R)
        w3h = [place("A", f"w3h{m}", [P, NK, T], FP32R) for m in range(2)]
        w3l = [place("A", f"w3l{m}", [P, NK, T], FP32R) for m in range(2)]
        at["S"] = at["A"]
        dnh = place("A", "dnh", [P, NC, D], FP32R)
        dnl = place("A", "dnl", [P, NC, D], FP32R)
        craw = place("S", "craw", [P, NK, T], FP32)
        wkvraw = place("S", "wkvraw", [P, NK, 2 * D], FP32)
        toki = place("S", "toki", [P, T], I32)
        side = place("A", "side", [P, 2, T], I32)
        u_raw = prod[NH - 1][:, 0:2 * P]
        u_r = place("A", "u_r", [P, 2, P], FP32R)
        mask = [place("A", f"mask{e}", [P, T], BF16) for e in range(NE0)]
        at["K"] = at["A"]
        cps = [place("A", f"cps{n}", [P, 2, T], FP32) for n in range(2)]
        tab = place("A", "tab", [P, 2, T], FP32)
        df = [place("A", f"df{n}", [P, HALF], FP32) for n in range(2)]
        dst = [place("A", f"dst{n}", [P, HALF], FP32R) for n in range(2)]
        kraw = place("K", "kraw", [P, NT, D], FP32)
        vt = place("K", "vt", [P, NK, T], FP32)
        kmax = place("K", "kmax", [P, NT * HEADS], FP32)
        ks = place("K", "ks", [P, NT * HEADS], FP32)
        krs = place("K", "krs", [P, NT * HEADS], FP32)
        vround = place("K", "vround", [P, NK, T], BF16)
        at["B"] = base
        at["P"] = at["B"]
        qraw = place("B", "qraw", [P, NT, D], FP32)
        qint = place("B", "qint", [P, NT, D + HD], BF16)
        qmax = place("B", "qmax", [P, NT, HEADS], FP32)
        qs = place("B", "qs", [P, NT, HEADS + 1], FP32)
        qrs = place("B", "qrs", [P, NT, HEADS], FP32)
        nqs = place("B", "nqs", [P, NT, HEADS + 1], FP32)
        xq = place("B", "xq", [P, NT, P], BF16)
        xk = place("B", "xk", [P, NT, P], BF16)
        qT = [place("B", f"qT{n}", [P, T], BF16) for n in range(3)]
        kT = [place("B", f"kT{n}", [P, T], BF16) for n in range(3)]
        pu = [place("P" if n == 2 else "B", f"pu{n}", [P, 2 * T], U16) for n in range(3)]
        pT = [place("P" if n == 2 else "B", f"pT{n}", [P, 2 * T], BF16) for n in range(3)]
        assert 2 * (2 * T * 2) <= NT * D * 4
        smax = [place("B", f"smax{n}", [P, 2], FP32) for n in range(4)]
        qsh = [place("B", f"qsh{n}", [P, NT], FP32) for n in range(3)]
        nqsh = [place("B", f"nqsh{n}", [P, NT], FP32) for n in range(3)]
        zsum = [place("B", f"zsum{n}", [P, NT], FP32) for n in range(3)]
        rz = [place("B", f"rz{n}", [P, NT], FP32) for n in range(3)]
        O = place("B", "O", [P, NT, D], FP32)
        at["C"] = at["B"]
        wqraw = place("C", "wqraw", [P, NK, D], FP32)
        wqh = place("C", "wqh", [P, NK, D], FP32R)
        wql = place("C", "wql", [P, NK, D], FP32R)
        wpraw = place("C", "wpraw", [P, NK, D], FP32)
        wph = place("C", "wph", [P, NK, D], FP32R)
        wpl = place("C", "wpl", [P, NK, D], FP32R)
        bqb = place("C", "bqb", [P, D], FP32)
        bpb = place("C", "bpb", [P, D], FP32)
        swraw = place("C", "swraw", [P, NK, 2, HID], FP32)
        swh = place("C", "swh", [P, NK, 2, HID], FP32R)
        swl = place("C", "swl", [P, NK, 2, HID], FP32R)
        s2raw = place("C", "s2raw", [P, D], FP32)
        s2h = place("C", "s2h", [P, D], FP32R)
        s2l = place("C", "s2l", [P, D], FP32R)
        wgraw = place("C", "wgraw", [P, NK, NE], FP32)
        wgs = place("C", "wgs", [P, NK, 2, NE], FP32R)
        wgh, wgl = wgs[:, :, 0, :], wgs[:, :, 1, :]
        wdraw = place("C", "wdraw", [P, NK, 2 * LAT], FP32)
        wdh = place("C", "wdh", [P, NK, 2 * LAT], FP32R)
        wdl = place("C", "wdl", [P, NK, 2 * LAT], FP32R)
        wuraw = place("C", "wuraw", [P, D], FP32)
        wuh = place("C", "wuh", [P, D], FP32R)
        wul = place("C", "wul", [P, D], FP32R)
        biasb = place("C", "biasb", [P, NE], FP32)
        e1 = place("C", "e1", [P, NE, 2, HID], FP32R)
        e2 = place("C", "e2", [P, NE, 2, LAT], FP32R)
        e1raw = place("C", "e1raw", [P, NE, 2, HID], FP32)
        e2raw = place("C", "e2raw", [P, NE, LAT], FP32)
        e1s = [place("C", f"e1s{n}", [P, 2, HID], FP32R) for n in range(2)]
        e2s = [place("C", f"e2s{n}", [P, 2, LAT], FP32R) for n in range(2)]
        at["D"] = base
        xlh = place("D", "xlh", [P, T], FP32R)
        xll = place("D", "xll", [P, T], FP32R)
        prob = place("D", "prob", [P, NT, NE], FP32)
        pick = place("D", "pick", [P, NT, NE], FP32)
        left = place("D", "left", [P, NT, NE], FP32)
        top8 = place("D", "top8", [P, NT, TOPK], FP32)
        psum8 = place("D", "psum8", [P, NT], FP32)
        wT = place("D", "wT", [NE, T], FP32)
        wb = [place("D", f"wb{n}", [P, T], FP32) for n in range(2)]
        sq = [place("D", f"sq{n}", [P, HALF], FP32)[:, :] for n in range(4)]
        hp = [place("D", f"hp{n}", [P, HALF], FP32)[:, :] for n in range(4)]
        eh = [place("D", f"eh{n}", [P, HALF], FP32R)[:, :] for n in range(4)]
        el = [place("D", f"el{n}", [P, HALF], FP32R)[:, :] for n in range(4)]
        (ah, sh_h), (al, sh_l), res = (hh[:, 0, :], hh[:, 1, :]), (hl[:, 0, :], hl[:, 1, :]), xn
        assert at["D"] <= at["B"], (at["D"], at["B"])

        psum = es.enter_context(nc.psum_tensor("psum", [P, 8, HALF], FP32))
        bank = [psum[:, n, :] for n in range(8)]
        scores = [psum[:, 2 * n:2 * n + 2, :].rearrange("p b k -> p (b k)") for n in range(3)]
        operand = bank[6].bitcast(BF16)
        mixed = bank[7][:, 0:P]
        ups, gates_of = bank[0:4], bank[6:8]

        S = {n: sem(n) for n in (
            "x_in0", "x_in1", "ident_in", "identb", "ctx_in", "tok_in", "cp_in0", "cp_in1", "cp_in2", "u_in", "tab_in", "side_in", "wkv_in", "wq_in", "moe_in",
            "e1_in", "wrow_out", "wb_in0", "wb_in1", "stage_in", "stage_out", "out_done",
            "zeroed", "filled", "drained", "vec_own", "act_own", "summed", "residual",
            "variance", "std_ready", "scales_ready", "norm_ready", "norm_rest", "norm_high", "ctx_high", "ctx_low", "mask_ready",
            "activated", "masked", "high_ready", "low_ready",
            "control", "control_high", "control_low", "selected", "piece_high",
            "kv_plain", "k_biased", "k_scales", "k_steps", "k_ready", "v_round", "wkv_high", "wkv_low",
            "wq_high", "wq_low", "bp_added", "q_ready", "built", "prepped", "qT_ready", "kT_ready",
            "scored", "reduced", "maxed", "exped", "turn_passed", "offset_passed",
            "turned0", "turned1", "turned2", "pT_ready", "mix_done", "head_out",
            "o_high", "moe_high", "moe_low", "e1_low", "latent_high",
            "probs", "weights", "rectified", "squared", "scaled", "expert_high", "expert_low", "expert_sum",
            "acc_high", "acc_low", "res_ready")}
        block = es.enter_context(nc.Block())
        def half(ap, n):
            return ap[:, n * HALF:(n + 1) * HALF]

        def plain(ap):
            return ap.bitcast(FP32) if ap.dtype == FP32R else ap

        def piece(k, high):
            m, c, h = k // 4, k // 2 % 2, k % 2
            raw = bank[FIRST[("spline", k)] % RING]
            if m < 2:
                return half((w3h if high else w3l)[m][:, c, :], h), raw
            return (dnh if high else dnl)[:, c::2, h * P:(h + 1) * P], raw.rearrange("p (x q) -> p q x", q=4)

        TRIO_STEPS = 3 * 2

        def slot(n, t):
            return (NT * n + t) % 3

        def pair(n, t):
            return (4 * n + t // 2) % 3

        def part(buffers, n, t):
            return buffers[pair(n, t)][:, t % 2 * T:(t % 2 + 1) * T]

        def turned(i, n, t):
            return S[f"turned{pair(n, t)}"], 64 * i + 16 * ((4 * n + t // 2) // 3 + 1)

        LOG255 = math.log(255.0)

        def offset(eng, n, t):
            eng.tensor_scalar(smax[t % 4][:, 1:2], smax[t % 4][:, 0:1], nqsh[n][:, t:t + 1], LOG255,
                              ALU.mult, ALU.add).then_inc(S["maxed"], 1)

        MOE_LOADS = 16 * 12

        def expert_halves(eng, step):
            for k in range(4):
                step(k, k // 2, k, True)
            with eng.Fori(1, NE // 2 - 2) as i:
                for u in range(4):
                    step(4 * i + u, 2 * i + u // 2, u, False)
            for k in range(2 * NE - 8, 2 * NE):
                step(k, k // 2, k % 4, False)

        def within(k):
            return not isinstance(k, int) or k < 2 * NE

        LEAD = 3

        @block.sync
        def _(sp):
            def load(dst, src, name):
                sp.dma_start(dst, src).then_inc(S[name], 16)

            def row(v, n):
                return v.rearrange("(a d) -> a d", a=1).broadcast_to((P, n))

            for n in range(2):
                load(X[:, 4 * n:4 * n + 4, :], x_v[:, 4 * n:4 * n + 4, :], f"x_in{n}")
            load(craw[:, :, :], ctx_t.rearrange("(k p) t -> p k t", p=P), "ctx_in")
            load(idf[:, :], ident, "ident_in")
            load(toki[:, :], row(tok, T), "tok_in")
            load(u_raw, stacked.rearrange("k s p -> k (s p)"), "u_in")
            load(tab[:, :, :], table, "tab_in")
            load(cps[0][:, :, :], cpw[0], "cp_in0")
            load(side[:, :, :], upper, "side_in")
            load(wkvraw[:, :, :], wkv.rearrange("(k p) n -> p k n", p=P), "wkv_in")
            load(bk[:, :], row(bkv[0:D], D), "wkv_in")
            load(bv[:, :], bv_t, "wkv_in")
            load(cps[1][:, :, :], cpw[1], "cp_in1")
            sp.wait_ge(S["control"], 4)
            load(cps[0][:, :, :], cpw[2], "cp_in2")
            sp.wait_ge(S["residual"], 2)
            load(wqraw[:, :, :], wq.rearrange("(k p) n -> p k n", p=P), "wq_in")
            load(bqb[:, :], row(bq, D), "wq_in")
            load(wpraw[:, :, :], wp.rearrange("(k p) n -> p k n", p=P), "moe_in")
            load(bpb[:, :], row(bp, D), "moe_in")
            load(swraw[:, :, 0, :], swg_t.rearrange("(k p) n -> p k n", p=P), "moe_in")
            load(swraw[:, :, 1, :], sw1_t.rearrange("(k p) n -> p k n", p=P), "moe_in")
            load(s2raw[:, :], sw2_t, "moe_in")
            load(wgraw[:, :, :], wg_t.rearrange("(k p) n -> p k n", p=P), "moe_in")
            for n in range(2):
                load(wdraw[:, :, n * LAT:(n + 1) * LAT], wdown_t.rearrange("(k p) n -> p k n", p=P), "moe_in")
                load(wuraw[n * LAT:(n + 1) * LAT, :], wup_t, "moe_in")
            load(biasb[:, :], row(biases, NE), "moe_in")
            load(e2raw[:, :, :], rw2_t, "moe_in")
            for n in range(2):
                for m, w in ((0, rwg_t), (1, rw1_t)):
                    load(e1raw[n * LAT:(n + 1) * LAT, :, m, :], w, "e1_in")

            def head_turns(g0, n):
                for t in range(1, NT, 2):
                    sp.wait_ge(S["exped"], g0 + t + 1)
                    sp.sem_inc(S["turn_passed"], 1)
                    if not (n == 0 and t < 6):
                        sp.wait_ge(S["mix_done"], g0 + t - 5)
                        sp.sem_inc(S["turn_passed"], 1)
                    m = pair(n, t)
                    sp.dma_start_transpose(pT[m][:, :].rearrange("p (c q) -> p c q", q=P),
                                           pu[m][:, :].bitcast(BF16)).then_inc(S[f"turned{m}"], 16)

            head_turns(0, 0)
            with sp.Fori(0, (HEADS - 1) // 3) as i:
                for n in (1, 2, 3):
                    head_turns(24 * i + 8 * n, n)
            sp.wait_ge(S["drained"], drained(FIRST[("wturn", 1)]))
            sp.dma_start(wrow, wT[:, :]).then_inc(S["wrow_out"], 16)
            sp.wait_ge(S["wrow_out"], 16)

            def spread(e, n, first):
                if not first:
                    sp.wait_ge(S["scaled"], 2 * (e - 1))
                sp.dma_start(wb[n][:, :], wrow[bass.ds(e, 1), :].broadcast_to((P, T))).then_inc(S[f"wb_in{n}"], 16)

            spread(0, 0, True)
            spread(1, 1, True)
            with sp.Fori(1, NE // 2) as i:
                spread(2 * i, 0, False)
                spread(2 * i + 1, 1, False)
            for n in range(4):
                sp.wait_ge(S["res_ready"], n + 1)
                sp.dma_start(out_v[:, 2 * n:2 * n + 2, :], res[:, 2 * n:2 * n + 2, :]).then_inc(S["out_done"], 16)
            sp.wait_ge(S["out_done"], 64)

        @block.gpsimd
        def _(pool):
            pool.memset(eps[:, :], EPS).then_inc(S["zeroed"], 1)
            pool.wait_ge(S["ident_in"], 16)
            pool.tensor_copy(idb[:, :], idf[:, :]).then_inc(S["identb"], 1)

            def control(k):
                m, c, h = k // 4, k // 2 % 2, k % 2
                if k == 0:
                    pool.wait_ge(S["tab_in"], 16)
                if k % 4 == 0:
                    pool.wait_ge(S[f"cp_in{m}"], 16)
                if k >= 2:
                    pool.wait_ge(S["control_low"], k - 1)
                pool.tensor_tensor(df[k % 2][:, :], half(tab[:, c, :], h), half(cps[m % 2][:, c, :], h),
                                   ALU.mult).then_inc(S["control"], 1)

            pool.wait_ge(S["ctx_high"], 1)
            pool.tensor_tensor(cl[:, :, :], craw[:, :, :], plain(ch[:, :, :]), ALU.subtract).then_inc(S["ctx_low"], 1)
            control(0)
            control(1)
            for entry in ORDER[:ATTENTION]:
                if entry[0] == "z":
                    j = entry[1]
                    pool.wait_ge(S["mask_ready"], min(j // 4 + 1, NE0 - 1))
                    pool.wait_ge(S["activated"], j + 1)
                    pool.tensor_tensor(gate_s[j % NH][:, :], gate_s[j % NH][:, :],
                                       half(mask[j // 4][:, :], j % 2), ALU.mult).then_inc(S["masked"], 1)
                elif entry[0] == "spline" and entry[1] + 2 < 12:
                    control(entry[1] + 2)
                elif entry == ("norm", 1, 0):
                    pool.wait_ge(S["kv_plain"], 4)
                    pool.wait_ge(S["wkv_in"], 48)
                    pool.tensor_tensor(kraw[:, :, :], kraw[:, :, :],
                                       bk[:, :].unsqueeze(1).broadcast_to((P, NT, D)),
                                       ALU.add).then_inc(S["k_biased"], 1)
            kg = kraw[:, :, :].rearrange("p t (h d) -> p (t h) d", d=HD)
            for step, factor in ((1, krs), (2, ks)):
                pool.wait_ge(S["k_scales"], step)
                pool.tensor_tensor(kg, kg, factor[:, :].unsqueeze(2).broadcast_to((P, NT * HEADS, HD)),
                                   ALU.mult).then_inc(S["k_steps"], 1)
            for part in range(2):
                pool.wait_ge(S["k_ready"], part + 1)
                pool.tensor_tensor(kraw[:, :, :], kraw[:, :, :], kparts[:, :, part, 0:D],
                                   ALU.subtract).then_inc(S["k_steps"], 1)
            pool.wait_ge(S["residual"], 2)
            pool.memset(xq[:, :, :], 0.0).then_inc(S["zeroed"], 1)
            pool.memset(xk[:, :, :], 0.0).then_inc(S["zeroed"], 1)
            pool.memset(qint[:, :, D:], 0.0).then_inc(S["zeroed"], 1)
            pool.memset(kparts[:, :, :, D:], 0.0).then_inc(S["zeroed"], 1)
            pool.memset(qs[:, :, HEADS:], 0.0).then_inc(S["zeroed"], 1)
            pool.memset(nqs[:, :, HEADS:], 0.0).then_inc(S["zeroed"], 1)
            pool.wait_ge(S["zeroed"], 7)
            pool.wait_ge(S["k_ready"], 3)
            pool.wait_ge(S["wq_high"], 1)
            pool.tensor_tensor(wql[:, :, :], wqraw[:, :, :], plain(wqh[:, :, :]), ALU.subtract).then_inc(S["wq_low"], 1)

            def queries(h, part_no):
                t = slice(part_no * NT // 2, (part_no + 1) * NT // 2)
                pool.tensor_copy(xq[:, t, 0:3 * HD].rearrange("p t (r d) -> p t r d", r=3),
                                 qint[:, t, bass.ds(h * HD, HD)].unsqueeze(2)
                                 .broadcast_to((P, NT // 2, 3, HD))).then_inc(S["built"], 1)

            def keys(h, part_no):
                t = slice(part_no * NT // 2, (part_no + 1) * NT // 2)
                pool.tensor_copy(xk[:, t, 0:3 * HD].rearrange("p t (r d) -> p t r d", r=3),
                                 kparts[:, t, :, bass.ds(h * HD, HD)]).then_inc(S["built"], 1)

            def scales(h, n):
                pool.tensor_copy(qsh[n][:, :].unsqueeze(2), qs[:, :, bass.ds(h, 1)]).then_inc(S["built"], 1)
                pool.tensor_copy(nqsh[n][:, :].unsqueeze(2), nqs[:, :, bass.ds(h, 1)]).then_inc(S["built"], 1)

            def head_offsets(h, n, g0):
                pool.wait_ge(S["built"], 6 * h + 6)
                for t in range(NT):
                    pool.wait_ge(S["reduced"], g0 + t + 1)
                    pool.sem_inc(S["offset_passed"], 1)
                    offset(pool, n, t)
                    if t == 0:
                        pool.wait_ge(S["prepped"], 2 * h + 2)
                    if t in (0, 1):
                        queries(h + 1, int(t > 0))
                    if t == 2:
                        pool.wait_ge(S["exped"], 8 * (h - 1))
                        scales(h + 1, (n + 1) % 3)
                    if t in (3, 4):
                        keys(h + 1, int(t > 3))

            for q in range(2):
                keys(0, q)
            pool.wait_ge(S["q_ready"], 1)
            for q in range(2):
                queries(0, q)
            scales(0, 0)
            pool.wait_ge(S["prepped"], 2)
            for q in range(2):
                queries(1, q)
            scales(1, 1)
            for q in range(2):
                keys(1, q)
            pool.wait_ge(S["q_ready"], 2)
            pool.wait_ge(S["norm_ready"], 12)
            pool.wait_ge(S["norm_rest"], 12)
            pool.wait_ge(S["moe_in"], MOE_LOADS)
            pool.tensor_tensor(X[:, :, :], X[:, :, :], bpb[:, :].unsqueeze(1).broadcast_to((P, NT, D)),
                               ALU.add).then_inc(S["bp_added"], 1)

            def low(dst_ap, raw, high, n, name):
                pool.wait_ge(S["moe_high"], n)
                pool.tensor_tensor(dst_ap, raw, plain(high), ALU.subtract).then_inc(S[name], 1)

            low(wpl[:, :, :], wpraw[:, :, :], wph[:, :, :], 1, "moe_low")
            low(swl[:, :, :, :].rearrange("p k m n -> p (k m n)"), swraw[:, :, :, :].rearrange("p k m n -> p (k m n)"),
                swh[:, :, :, :].rearrange("p k m n -> p (k m n)"), 2, "moe_low")
            low(s2l[:, :], s2raw[:, :], s2h[:, :], 3, "moe_low")
            low(wgl[:, :, :], wgraw[:, :, :], wgh[:, :, :], 4, "moe_low")
            low(wdl[:, :, :], wdraw[:, :, :], wdh[:, :, :], 5, "moe_low")
            low(wul[:, :], wuraw[:, :], wuh[:, :], 6, "moe_low")
            low(e2[:, :, 1, :], e2raw[:, :, :], e2[:, :, 0, :], 7, "moe_low")
            with pool.Fori(0, (HEADS - 1) // 3) as i:
                for n in (1, 2, 3):
                    head_offsets(3 * i + n, n % 3, 24 * i + 8 * n)
            for g in range(4):
                rows = e1[LAT:P, 4 * g:4 * g + 4, :, :].rearrange("p e m n -> p (e m n)")
                low(rows, e1raw[LAT:P, 4 * g:4 * g + 4, :, :].rearrange("p e m n -> p (e m n)"), rows, 8 + g, "e1_low")
            pool.wait_ge(S["e1_low"], 4)

            def scale(k, e, u, first):
                if u % 2 == 0:
                    pool.wait_ge(S[f"wb_in{u // 2}"], 8 * (e - u // 2) + 16)
                pool.wait_ge(S["drained"], drained(MOE0) + 2 * k + 1)
                pool.tensor_tensor(hp[u], hp[u], half(wb[u // 2][:, :], u % 2), ALU.mult).then_inc(S["scaled"], 1)

            expert_halves(pool, scale)

        @block.scalar
        def _(act):
            def copy(o, i, name, **k):
                act.activation(o, i, ACT.Copy, **k).then_inc(S[name], 1)

            def late_constants():
                act.wait_ge(S["u_in"], 16)
                copy(u_r[:, :, :].rearrange("p s n -> p (s n)"), u_raw, "ctx_high")

            def controls(k):
                act.wait_ge(S["control"], k + 1)
                if k >= 2:
                    act.wait_ge(S["filled"], FIRST[("spline", k - 2)] + 2)
                copy(dst[k % 2][:, :], df[k % 2][:, :], "control_high")

            def product_done(j):
                return drained(FIRST[("z", j)] if j < 16 else FIRST[("gu", j)] + 1)

            def highs(j):
                act.wait_ge(S["drained"], product_done(j))
                if j >= NH:
                    act.wait_ge(S["low_ready"], j - NH + 1)
                    act.wait_ge(S["summed"], j - NH + 1)
                copy(ph[j % NH][:, :], prod[j % NH][:, :], "high_ready")

            def root(layer):
                act.wait_ge(S["variance"], 2 * layer + 2)
                if layer == 0:
                    act.wait_ge(S["zeroed"], 1)
                act.activation(std[:, :], mv[:, :, 1], ACT.Sqrt, bias=eps[:, :]).then_inc(S["std_ready"], 1)

            def normalise_rest(layer):
                act.wait_ge(S["scales_ready"], layer + 1)
                for t in range(4, NT):
                    act.activation(xn[:, t, :], X[:, t, :], ACT.Identity, scale=rstd[:, t:t + 1],
                                   bias=shift[:, t:t + 1]).then_inc(S["norm_rest"], 1)

            def gates(j, n, func):
                act.wait_ge(S["filled"], n + 1)
                if j >= NH:
                    act.wait_ge(S["drained"], product_done(j - NH))
                act.activation(gate_s[j % NH][:, :], bank[n % RING], func).then_inc(S["activated"], 1)

            def norm_highs(entry):
                n, q = FIRST[entry], entry[2]
                act.wait_ge(S["filled"], n + 1)
                copy(half(hh[:, q % 2, :], q // 2), bank[n % RING], "norm_high")

            root(0)
            act.wait_ge(S["ctx_in"], 16)
            copy(ch[:, :, :], craw[:, :, :], "ctx_high")
            for entry in ORDER[:ATTENTION]:
                kind, n = entry[0], FIRST[entry]
                if kind == "norm":
                    layer, q = entry[1:]
                    if q == 0:
                        if layer > 1:
                            root(layer)
                        normalise_rest(layer)
                        if layer == 2:
                            act.wait_ge(S["wq_in"], 32)
                            copy(wqh[:, :, :], wqraw[:, :, :], "wq_high")
                    norm_highs(entry)
                    if q == 3 and layer == 0:
                        late_constants()
                        controls(0)
                elif kind in ("z", "gu"):
                    j = entry[1]
                    gates(j, n, ACT.Silu)
                    if 0 < j < 16:
                        highs(j - 1)
                    if j >= 15:
                        highs(j)
                elif kind == "spline":
                    k = entry[1]
                    if k + 1 < 12:
                        controls(k + 1)
                    act.wait_ge(S["selected"], k + 1)
                    if k == 8:
                        act.wait_ge(S["ctx_low"], 1)
                        act.wait_ge(S["wkv_low"], 1)
                        act.wait_ge(S["mask_ready"], 3)
                    copy(*piece(k, True), "piece_high")
                    if k == 2:
                        act.wait_ge(S["wkv_in"], 48)
                        copy(wkvh[:, :, :], wkvraw[:, :, :], "wkv_high")
                elif kind in ("key", "value"):
                    q = entry[1]
                    if entry == ("value", 0):
                        root(1)
                    act.wait_ge(S["filled"], n + 1)
                    if kind == "key":
                        if q == 0:
                            act.wait_ge(S["control_low"], 12)
                            act.wait_ge(S["filled"], FIRST[("spline", 11)] + 2)
                        copy(kraw[:, 2 * q:2 * q + 2, :].rearrange("p t d -> p (t d)"), bank[n % RING], "kv_plain")
                    else:
                        act.activation(half(vt[:, q // 2, :], q % 2), bank[n % RING], ACT.Identity,
                                       bias=bv[:, q // 2:q // 2 + 1]).then_inc(S["kv_plain"], 1)

            act.wait_ge(S["moe_in"], MOE_LOADS)
            copy(wph[:, :, :], wpraw[:, :, :], "moe_high")
            copy(swh[:, :, :, :].rearrange("p k m n -> p (k m n)"), swraw[:, :, :, :].rearrange("p k m n -> p (k m n)"),
                 "moe_high")
            copy(s2h[:, :], s2raw[:, :], "moe_high")
            copy(wgh[:, :, :], wgraw[:, :, :], "moe_high")
            copy(wdh[:, :, :], wdraw[:, :, :], "moe_high")
            copy(wuh[:, :], wuraw[:, :], "moe_high")
            copy(e2[:, :, 0, :], e2raw[:, :, :], "moe_high")

            def head_scalar(i, n):
                h, g0, begin = 3 * i + n, 24 * i + 8 * n, n == 0
                for t in range(NT):
                    if t % 2 == 0 and not (begin and t < 6):
                        act.wait_ge(*turned(i, n, t - 6))
                    act.wait_ge(S["maxed"], g0 + t + 1)
                    act.activation(part(pu, n, t), scores[slot(n, t)], ACT.Exp, bias=smax[t % 4][:, 1:2],
                                   scale=qsh[n % 3][:, t:t + 1], accum_out=zsum[n % 3][:, t:t + 1]).then_inc(S["exped"], 1)
                    if t in (2, 3):
                        act.wait_ge(S["prepped"], 2 * h + 3)
                        copy(half(qT[(n + 1) % 3][:, :], int(t > 2)), half(operand, int(t > 2)), "qT_ready")
                    if t == 5:
                        act.wait_ge(S["prepped"], 2 * h + 4)
                        copy(kT[(n + 1) % 3][:, :], operand, "kT_ready")

            act.activation(smax[3][:, 0:1], eps[:, :], ACT.Exp).then_inc(S["act_own"], 1)
            act.wait_ge(S["act_own"], 1)
            act.wait_ge(S["prepped"], 1)
            for q in range(2):
                copy(half(qT[0][:, :], q), half(operand, q), "qT_ready")
            act.wait_ge(S["prepped"], 2)
            copy(kT[0][:, :], operand, "kT_ready")
            head_scalar(0, 0)
            with act.Fori(0, (HEADS - 1) // 3) as i:
                for n in (1, 2, 3):
                    head_scalar(i, n)

            act.wait_ge(S["e1_in"], 64)
            for g in range(4):
                copy(e1[:, 4 * g:4 * g + 4, :, :].rearrange("p e m n -> p (e m n)"),
                     e1raw[:, 4 * g:4 * g + 4, :, :].rearrange("p e m n -> p (e m n)"), "moe_high")

            for q in range(4):
                n = FIRST[("oturn", q)]
                act.wait_ge(S["filled"], n + 1)
                copy(half(hh[:, q % 2, :], q // 2), bank[n % RING], "o_high", scale=sv[:, q % 2:q % 2 + 1])
            root(3)
            normalise_rest(3)
            act.wait_ge(S["built"], 6 * (HEADS + 1))
            for q in range(4):
                norm_highs(("norm", 3, q))
            n = FIRST[("router", 0)]
            act.wait_ge(S["drained"], drained(n))
            act.activation(prob[:, :, :], prob[:, :, :], ACT.Sigmoid).then_inc(S["probs"], 1)
            for q in range(2):
                n = FIRST[("latent", q)]
                act.wait_ge(S["filled"], n + 1)
                copy(half(xlh[:, :], q), bank[n % RING], "latent_high")
            for q in range(2):
                j, n = 32 + q, FIRST[("gu", 32 + q)]
                gates(j, n, ACT.Relu)
                act.wait_ge(S["activated"], j + 1)
                act.activation(gate_s[j % NH][:, :], gate_s[j % NH][:, :], ACT.Square).then_inc(S["squared"], 1)
            act.wait_ge(S["filled"], FIRST[("gu", 33)] + 2)
            for q in range(2):
                act.wait_ge(S["drained"], drained(FIRST[("gu", 32 + q)] + 1))
                copy(half(sh_h, q), prod[(32 + q) % NH][:, :], "high_ready")

            def rectify(k, u, first):
                act.wait_ge(S["filled"], MOE0 + 2 * k + 1)
                if not first:
                    act.wait_ge(S["drained"], drained(MOE0) + 2 * (k - 4) + 1)
                act.activation(sq[u], gates_of[u % 2], ACT.Relu).then_inc(S["rectified"], 1)

            def square(k, u):
                act.wait_ge(S["rectified"], k + 1)
                act.activation(sq[u], sq[u], ACT.Square).then_inc(S["squared"], 1)

            def expert_scalar(k, e, u, first):
                v, fresh = (u + LEAD) % 4, first and u + LEAD < 4
                if within(k + LEAD):
                    rectify(k + LEAD, v, fresh)
                act.wait_ge(S["scaled"], k + 1)
                if not first:
                    act.wait_ge(S["expert_low"], k - 3)
                    act.wait_ge(S["expert_sum"], k - 3)
                copy(eh[u], hp[u], "expert_high")
                if within(k + LEAD):
                    square(k + LEAD, v)

            for k in range(LEAD):
                rectify(k, k, True)
                square(k, k)
            expert_halves(act, expert_scalar)
            for h in range(2):
                act.wait_ge(S["expert_sum"], 2 * NE)
                copy(half(ah, h), bank[4 + h], "acc_high")

        @block.vector
        def _(dve):
            own = Chain(dve, S["vec_own"])

            def sub(o, a, b, name, k=1):
                dve.tensor_tensor(o, plain(a), plain(b), ALU.subtract).then_inc(S[name], k)

            def moments(h):
                for t in range(4 * h, 4 * h + 4):
                    own.mark(dve.bn_stats(stats[:, t, :], X[:, t, :]))
                own.wait()
                for t in range(4 * h, 4 * h + 4):
                    ins = dve.bn_aggr(mv[:, t, :], stats[:, t, :])
                ins.then_inc(S["variance"], 1)

            def norm(layer):
                dve.wait_ge(S["std_ready"], layer + 1)
                own.link(dve.reciprocal(rstd[:, :], std[:, :]))
                dve.scalar_tensor_tensor(shift[:, :], mv[:, :, 0], -1.0, rstd[:, :],
                                         ALU.mult, ALU.mult).then_inc(S["scales_ready"], 1)
                for t in range(4):
                    dve.tensor_scalar(xn[:, t, :], X[:, t, :], mv[:, t, 0:1], rstd[:, t:t + 1],
                                      ALU.subtract, ALU.mult).then_inc(S["norm_ready"], 1)

            def norm_lows(entry):
                n, (layer, q) = FIRST[entry], entry[1:]
                dve.wait_ge(S["norm_high"], 4 * layer + q + 1)
                sub(half(hl[:, q % 2, :], q // 2), bank[n % RING], half(hh[:, q % 2, :], q // 2), "drained")

            def product(j, n, b):
                if j < 16:
                    dve.wait_ge(S["masked"], j + 1)
                elif j < 32:
                    dve.wait_ge(S["activated"], j + 1)
                    dve.wait_ge(S["filled"], n + 2)
                else:
                    dve.wait_ge(S["squared"], j - 31)
                    dve.wait_ge(S["filled"], n + 2)
                if j >= NH:
                    dve.wait_ge(S["high_ready"], j - NH + 1)
                    dve.wait_ge(S["low_ready"], j - NH + 1)
                dve.tensor_tensor(prod[j % NH][:, :], gate_s[j % NH][:, :], bank[b % RING],
                                  ALU.mult).then_inc(S["drained"], 1 + b - n)

            def lows(j):
                dve.wait_ge(S["high_ready"], j + 1)
                if j >= NH:
                    dve.wait_ge(S["summed"], j - NH + 1)
                sub(pl[j % NH][:, :], prod[j % NH][:, :], ph[j % NH][:, :], "low_ready")

            def add_sums(layer, h):
                dve.wait_ge(S["summed"], 16 * layer + 15 + h)
                for b in (2 * h, 2 * h + 1):
                    o = X[:, 2 * b:2 * b + 2, :].rearrange("p t d -> p (t d)")
                    ins = dve.tensor_tensor(o, o, bank[4 + b], ALU.add)
                    own.mark(ins) if b < 3 else ins.then_inc(S["residual"], 1)
                own.wait()
                if h:
                    dve.wait_ge(S["residual"], layer + 1)

            def mask_steps():
                per = VOCAB // NE0
                for e in range(NE0 - 1):
                    own.link(dve.tensor_scalar(mask[e + 1][:, :], toki[:, :], float(per * (e + 1)), None, ALU.is_ge))
                    if e == 0:
                        dve.tensor_scalar(mask[0][:, :], mask[1][:, :], -1.0, 1.0, ALU.mult, ALU.add).then_inc(S["mask_ready"], 1)
                    else:
                        sub(mask[e][:, :], mask[e][:, :], mask[e + 1][:, :], "mask_ready")
                    yield

            def control_lows(k):
                dve.wait_ge(S["control_high"], k + 1)
                d = dst[k % 2][P // 2:, :]
                sub(d, df[k % 2][P // 2:, :], d, "control_low")

            def key_value_steps():
                kg = kraw[:, :, :].rearrange("p t (h d) -> p (t h) d", d=HD)
                kf = kraw[:, :, :].rearrange("p t d -> p (t d)")
                dve.wait_ge(S["k_biased"], 1)
                own.link(dve.tensor_reduce(kmax[:, :], kg, AX.X, ALU.max, apply_absolute_value=True))
                own.link(dve.tensor_scalar(ks[:, :], kmax[:, :], 1.0 / 127.0, 1e-8, ALU.mult, ALU.max))
                dve.reciprocal(krs[:, :], ks[:, :]).then_inc(S["k_scales"], 1)
                yield
                dve.wait_ge(S["kv_plain"], 8)
                own.link(dve.tensor_reduce(sv[:, :], vt[:, :, :], AX.X, ALU.max, apply_absolute_value=True))
                own.link(dve.tensor_scalar(sv[:, :], sv[:, :], 1.0 / 127.0, 1e-8, ALU.mult, ALU.max))
                own.link(dve.reciprocal(rsv[:, :], sv[:, :]))
                yield
                dve.wait_ge(S["k_steps"], 1)
                dve.tensor_scalar(kf, kf, MAGIC, -MAGIC, ALU.add, ALU.add).then_inc(S["k_scales"], 1)
                yield
                for part in range(3):
                    if part < NK:
                        k = part
                        own.link(dve.tensor_scalar(vt[:, k, :], vt[:, k, :], rsv[:, k:k + 1], MAGIC, ALU.mult, ALU.add))
                        dve.tensor_scalar(vround[:, k, :], vt[:, k, :], -MAGIC, None, ALU.add).then_inc(S["v_round"], 1)
                    yield
                    dve.wait_ge(S["k_steps"], part + 2)
                    dve.tensor_copy(kparts[:, :, part, 0:D], kraw[:, :, :]).then_inc(S["k_ready"], 1)
                    yield

            for h in range(2):
                dve.wait_ge(S[f"x_in{h}"], 16)
                moments(h)
            norm(0)
            dve.wait_ge(S["tok_in"], 16)
            masks = mask_steps()
            next(masks)
            kv = key_value_steps()
            for entry in ORDER[:ATTENTION]:
                kind, n = entry[0], FIRST[entry]
                if kind == "norm":
                    layer, q = entry[1:]
                    if q == 0 and layer:
                        for h in range(2):
                            add_sums(layer - 1, h)
                            moments(h)
                        norm(layer)
                    norm_lows(entry)
                    if q == 3 and layer == 0:
                        control_lows(0)
                elif kind == "z":
                    j = entry[1]
                    if j:
                        lows(j - 1)
                    product(j, n, n)
                    next(masks, None)
                    if j == 15:
                        lows(j)
                elif kind == "gu":
                    j = entry[1]
                    product(j, n, n + 1)
                    lows(j)
                    next(kv, None)
                elif kind == "spline":
                    k = entry[1]
                    if k == 0:
                        dve.wait_ge(S["side_in"], 16)
                    dve.wait_ge(S["filled"], n + 2)
                    c, h = k // 2 % 2, k % 2
                    dve.copy_predicated(bank[n % RING], half(side[:, c, :], h),
                                        bank[(n + 1) % RING]).then_inc(S["selected"], 1)
                    if k + 1 < 12:
                        control_lows(k + 1)
                    dve.wait_ge(S["piece_high"], k + 1)
                    o, raw = piece(k, False)
                    sub(o, raw, piece(k, True)[0], "drained", 2)
                    if k == 2:
                        dve.wait_ge(S["wkv_high"], 1)
                        sub(wkvl[:, :, :], wkvraw[:, :, :], wkvh[:, :, :], "wkv_low")
                elif kind == "vturn":
                    k = entry[1]
                    if k == 0:
                        for _ in kv:
                            pass
                    dve.wait_ge(S["filled"], n + 1)
                    dve.tensor_copy(vint[:, :, k * P:(k + 1) * P],
                                    bank[n % RING].bitcast(BF16).rearrange("p (t d) -> p t d", t=NT))\
                       .then_inc(S["drained"], 1)
                elif kind == "query":
                    q = entry[1]
                    if q == 0:
                        dve.wait_ge(S["wq_in"], 32)
                        dve.wait_ge(S["zeroed"], 7)
                    dve.wait_ge(S["filled"], n + 1)
                    dve.tensor_tensor(qraw[:, 2 * q:2 * q + 2, :], bank[n % RING].rearrange("p (t d) -> p t d", t=2),
                                      bqb[:, :].unsqueeze(1).broadcast_to((P, 2, D)), ALU.add).then_inc(S["drained"], 1)
                    dve.wait_ge(S["drained"], drained(n))
                    own.mark(dve.tensor_reduce(qmax[:, 2 * q:2 * q + 2, :],
                                               qraw[:, 2 * q:2 * q + 2, :].rearrange("p t (h d) -> p t h d", d=HD),
                                               AX.X, ALU.max, apply_absolute_value=True))

            own.wait()
            qg = qraw[:, :, :].rearrange("p t (h d) -> p t h d", d=HD)
            own.link(dve.tensor_scalar(qs[:, :, 0:HEADS], qmax[:, :, :], 0.25 / 127.0, 1e-8, ALU.mult, ALU.max))
            own.mark(dve.tensor_scalar(nqs[:, :, 0:HEADS], qs[:, :, 0:HEADS], -1.0, None, ALU.mult))
            own.link(dve.reciprocal(qrs[:, :, :], qs[:, :, 0:HEADS]))
            own.link(dve.tensor_scalar(qrs[:, :, :], qrs[:, :, :], 0.25, None, ALU.mult))
            for a, b in ((0, 2), (2, HEADS)):
                own.link(dve.tensor_tensor(qg[:, :, a:b, :], qg[:, :, a:b, :],
                                           qrs[:, :, a:b].unsqueeze(3).broadcast_to((P, NT, b - a, HD)), ALU.mult))
                dve.tensor_scalar(qint[:, :, a * HD:b * HD], qraw[:, :, a * HD:b * HD], MAGIC, -MAGIC,
                                  ALU.add, ALU.add).then_inc(S["q_ready"], 1)

            def whole(i, n, t):
                dve.wait_ge(*turned(i, n, t))
                p = pT[pair(n, t)]
                dve.tensor_copy(p[:, :], p[:, :].bitcast(U16)).then_inc(S["pT_ready"], 1)

            def head_inverse(h, n):
                dve.wait_ge(S["exped"], 8 * (h + 1))
                own.mark(dve.reciprocal(rz[n][:, :], zsum[n][:, :]))

            def head_scale(h, n):
                own.wait()
                own.mark(dve.tensor_scalar(rz[n][:, :], rz[n][:, :], 1e-8, None, ALU.max))

            def head_output(h, n):
                dve.wait_ge(S["mix_done"], 8 * h + 8)
                dve.tensor_tensor(O[:, :, bass.ds(h * HD, HD)], mixed.rearrange("p (t d) -> p t d", t=NT),
                                  rz[n][:, :].unsqueeze(2).broadcast_to((P, NT, HD)), ALU.mult).then_inc(S["head_out"], 1)

            def head_vector(i, n):
                h, g0, begin = 3 * i + n, 24 * i + 8 * n, n == 0
                if begin:
                    dve.wait_ge(S["built"], 6)
                for t in range(NT):
                    g = g0 + t
                    dve.wait_ge(S["scored"], g + 1)
                    if not (begin and t < 4):
                        dve.wait_ge(S["exped"], g - 3)
                    dve.reduce_max(smax[t % 4][:, 0:1], scores[slot(n, t)], AX.X).then_inc(S["reduced"], 1)
                    if begin:
                        dve.wait_ge(S["reduced"], t + 1)
                        offset(dve, n % 3, t)
                    if t % 2 == 1 and not (begin and t < 5):
                        whole(i, n, t - 5)
                    if t == 2 and not begin:
                        head_inverse(h - 1, (n - 1) % 3)
                    if t == 4 and not begin:
                        head_scale(h - 1, (n - 1) % 3)
                    if t == 5 and not begin:
                        own.wait()
                        head_output(h - 1, (n - 1) % 3)

            head_vector(0, 0)
            before = own.n
            with dve.Fori(0, (HEADS - 1) // 3) as i:
                own.loop = i * TRIO_STEPS
                for n in (1, 2, 3):
                    head_vector(i, n)
            assert own.n - before == TRIO_STEPS
            own.n, own.loop = before + (HEADS - 1) // 3 * TRIO_STEPS, 0
            for t in (4, 6):
                whole((HEADS - 2) // 3, 3, t)
            head_inverse(HEADS - 1, (HEADS - 1) % 3)
            head_scale(HEADS - 1, (HEADS - 1) % 3)
            own.wait()
            head_output(HEADS - 1, (HEADS - 1) % 3)

            for q in range(4):
                n = FIRST[("oturn", q)]
                dve.wait_ge(S["o_high"], q + 1)
                dve.scalar_tensor_tensor(half(hl[:, q % 2, :], q // 2), bank[n % RING], sv[:, q % 2:q % 2 + 1],
                                         plain(half(hh[:, q % 2, :], q // 2)), ALU.mult, ALU.subtract).then_inc(S["drained"], 1)
            dve.wait_ge(S["bp_added"], 1)
            for h in range(2):
                for q in (2 * h, 2 * h + 1):
                    n = FIRST[("proj", q)]
                    dve.wait_ge(S["filled"], n + 1)
                    o = X[:, 2 * q:2 * q + 2, :].rearrange("p t d -> p (t d)")
                    dve.tensor_tensor(o, o, bank[n % RING], ALU.add).then_inc(S["drained"], 1)
                dve.wait_ge(S["drained"], drained(n))
                moments(h)
            norm(3)
            for q in range(4):
                norm_lows(("norm", 3, q))
            def stage_in(e, n, first):
                if not first:
                    dve.wait_ge(S["filled"], MOE0 + 4 * (e - 1))
                dve.tensor_copy(e1s[n][:, :, :], plain(e1[:, bass.ds(e, 1), :, :].rearrange("p o a b -> p (o a) b")))\
                   .then_inc(S["stage_in"], 1)

            def stage_out(e, n, first):
                if not first:
                    dve.wait_ge(S["expert_sum"], 2 * (e - 1))
                dve.tensor_copy(e2s[n][:, :, :], plain(e2[:, bass.ds(e, 1), :, :].rearrange("p o a b -> p (o a) b")))\
                   .then_inc(S["stage_out"], 1)

            dve.wait_ge(S["e1_low"], 4)
            dve.wait_ge(S["moe_low"], 7)
            for n in range(2):
                stage_in(n, n, True)
                stage_out(n, n, True)
            n = FIRST[("router", 0)]
            dve.wait_ge(S["filled"], n + 1)
            dve.reduce_sum(prob[:, :, :], bank[n % RING][:, 0:NT * 2 * NE].rearrange("p (t a e) -> p t e a", t=NT, a=2),
                           AX.X).then_inc(S["drained"], 1)
            dve.wait_ge(S["probs"], 1)
            own.link(dve.tensor_tensor(pick[:, :, :], prob[:, :, :],
                                       biasb[:, :].unsqueeze(1).broadcast_to((P, NT, NE)), ALU.add))
            for t in range(NT):
                own.mark(dve.max(top8[:, t, :], pick[:, t, :]))
            own.wait()
            for t in range(NT):
                own.mark(dve.match_replace(left[:, t, :], top8[:, t, :], pick[:, t, :], -3.0e38))
            own.wait()
            own.link(dve.tensor_tensor(pick[:, :, :], pick[:, :, :], left[:, :, :], ALU.not_equal))
            own.link(dve.tensor_tensor(prob[:, :, :], prob[:, :, :], pick[:, :, :], ALU.mult))
            own.link(dve.reduce_sum(psum8[:, :], prob[:, :, :], AX.X))
            own.link(dve.reciprocal(psum8[:, :], psum8[:, :]))
            own.link(dve.tensor_scalar(psum8[:, :], psum8[:, :], RSCALE, None, ALU.mult))
            dve.tensor_tensor(prob[:, :, :], prob[:, :, :], psum8[:, :].unsqueeze(2).broadcast_to((P, NT, NE)),
                              ALU.mult).then_inc(S["weights"], 1)
            for q in range(2):
                n = FIRST[("latent", q)]
                dve.wait_ge(S["latent_high"], q + 1)
                sub(half(xll[:, :], q), bank[n % RING], half(xlh[:, :], q), "drained")
            n = FIRST[("gu", 32)]
            product(32, n, n + 1)
            for q in range(2):
                n = FIRST[("wturn", q)]
                dve.wait_ge(S["filled"], n + 1)
                dve.tensor_copy(half(wT[:, :], q), bank[n % RING][0:NE, :]).then_inc(S["drained"], 1)
            n = FIRST[("gu", 33)]
            product(33, n, n + 1)
            for q in range(2):
                j = 32 + q
                dve.wait_ge(S["high_ready"], j + 1)
                sub(half(sh_l, q), prod[j % NH][:, :], half(sh_h, q), "low_ready")

            def hidden(k, u, first):
                dve.wait_ge(S["squared"], 2 + k + 1)
                dve.wait_ge(S["filled"], MOE0 + 2 * k + 2)
                if not first:
                    dve.wait_ge(S["expert_high"], k - 3)
                    dve.wait_ge(S["expert_low"], k - 3)
                dve.tensor_tensor(hp[u], sq[u], ups[u], ALU.mult).then_inc(S["drained"], 2)

            def expert_vector(k, e, u, first):
                if u % 2 and within(k + 2) and not (first and u == 1):
                    stage_out(e + 1, 1 - u // 2, False)
                dve.wait_ge(S["expert_high"], k + 1)
                if not first:
                    dve.wait_ge(S["expert_sum"], k - 3)
                sub(el[u], hp[u], eh[u], "expert_low")
                if within(k + LEAD):
                    hidden(k + LEAD, (u + LEAD) % 4, first and u + LEAD < 4)
                if u % 2 == 0 and within(k + 6):
                    stage_in(e + 3, 1 - u // 2, False)

            for k in range(LEAD):
                hidden(k, k, True)
                if k == 1:
                    stage_in(2, 0, False)
            expert_halves(dve, expert_vector)
            for h in range(2):
                dve.wait_ge(S["acc_high"], h + 1)
                sub(half(al, h), bank[4 + h], half(ah, h), "acc_low")
            for q in range(4):
                dve.wait_ge(S["filled"], FINAL0 + q + 1)
                o = (slice(None), slice(2 * q, 2 * q + 2), slice(None))
                dve.tensor_tensor(res[o].rearrange("p t d -> p (t d)"), X[o].rearrange("p t d -> p (t d)"),
                                  bank[q], ALU.add).then_inc(S["res_ready"], 1)

        @block.tensor
        def _(pe):
            def free(n, count=1):
                for b in range(n, n + count):
                    if b >= RING:
                        last = b - RING
                        if last in KV:
                            pe.wait_ge(S["kv_plain"], KV.index(last) + 1)
                        else:
                            pe.wait_ge(S["drained"], drained(last))

            def mm3(o, lhs, rhs, start, stop, group=True):
                pe.matmul(o, lhs[0], rhs[0], start=start, stop=False, skip_group_check=not group)
                pe.matmul(o, lhs[0], rhs[1], start=False, stop=False, skip_group_check=not group)
                return pe.matmul(o, lhs[1], rhs[0], start=False, stop=stop, skip_group_check=not group)

            def both(h, l, *ix):
                return h[ix], l[ix]

            ALL = slice(None)

            def cols(a, n=P):
                return slice(a, a + n)

            def normal(k, h):
                return both(hh, hl, ALL, k, cols(h * HALF, HALF))

            def norm_turns(entry, src):
                n, q = FIRST[entry], entry[-1]
                free(n)
                k, h = q % 2, q // 2
                for t in range(4):
                    mm = pe.transpose(bank[n % RING][:, t * P:(t + 1) * P], src[:, 4 * h + t, k * P:(k + 1) * P], idf[:, :])
                mm.then_inc(S["filled"], 1)

            def projected(n, o_lhs, o_rhs, extra=None):
                free(n)
                for t in range(2):
                    o = bank[n % RING][:, t * D:(t + 1) * D]
                    for k in range(NK):
                        mm = mm3(o, o_lhs(k, t), o_rhs(k), k == 0, k == NK - 1)
                mm.then_inc(S["filled"], 1)

            def sums(j, lhs, rhs, first, last):
                pe.wait_ge(S["low_ready"], j + 1)
                pe.wait_ge(S["high_ready"], j + 1)
                for t in range(4):
                    tile = 4 * (j % 2) + t
                    o = bank[4 + tile // 2][:, (tile % 2) * D:(tile % 2 + 1) * D]
                    mm = mm3(o, lhs(t), rhs, first and tile % 2 == 0, last, group=False)
                mm.then_inc(S["summed"], 1)

            def hidden_parts(j):
                return lambda t: both(ph[j % NH], pl[j % NH], ALL, cols(t * P))

            pe.wait_ge(S["ident_in"], 16)
            for entry in ORDER[:ATTENTION]:
                kind, n = entry[0], FIRST[entry]
                if kind == "norm":
                    layer, q = entry[1:]
                    pe.wait_ge(S["norm_rest" if q > 1 else "norm_ready"], 4 * layer + 4)
                    norm_turns(entry, xn)
                elif kind == "z":
                    j = entry[1]
                    e, f, h = j // 4, j // 2 % 2, j % 2
                    if j == 0:
                        pe.wait_ge(S["ctx_low"], 1)
                    if j < 2:
                        pe.wait_ge(S["drained"], drained(FIRST[("norm", 0, 2 * h + 1)]))
                    free(n)
                    for k in range(NK):
                        mm = mm3(bank[n % RING], both(ch, cl, ALL, k, cols(e * D + f * P)), normal(k, h), k == 0, k == 1)
                    mm.then_inc(S["filled"], 1)
                elif kind == "y":
                    j = entry[1]
                    if j < 16:
                        e, f = j // 4, j // 2 % 2
                        sums(j, hidden_parts(j), both(ch, cl, ALL, f, cols(e * D, D)), j < 2, j >= 14)
                    else:
                        if j == 16:
                            pe.wait_ge(S["residual"], 1)
                            pe.wait_ge(S["drained"], drained(FIRST[("spline", 11)] + 1))
                        sums(j, hidden_parts(j), both(dnh, dnl, ALL, (j - 16) // 2), j < 18, j >= 30)
                elif kind == "gu":
                    j = entry[1]
                    c, h = (j - 16) // 2, j % 2
                    if j == 16:
                        pe.wait_ge(S["drained"], drained(FIRST[("spline", 7)] + 1))
                    if j < 18:
                        pe.wait_ge(S["drained"], drained(FIRST[("norm", 1, 2 * h + 1)]))
                    free(n, 2)
                    for m in range(2):
                        for k in range(NK):
                            mm = mm3(bank[(n + m) % RING], both(w3h[m], w3l[m], ALL, k, cols(c * P)), normal(k, h), k == 0, k == 1)
                        mm.then_inc(S["filled"], 1)
                elif kind == "spline":
                    k = entry[1]
                    if k == 0:
                        pe.wait_ge(S["ctx_high"], 2)
                    free(n, 2)
                    pe.wait_ge(S["control_low"], k + 1)
                    for s in range(2):
                        pe.matmul(bank[(n + s) % RING], u_r[:, s, :], dst[k % 2][:, :],
                                  start=True, stop=True).then_inc(S["filled"], 1)
                elif kind == "key":
                    q = entry[1]
                    if q == 0:
                        pe.wait_ge(S["wkv_low"], 1)
                    projected(n, lambda k, t: both(ch, cl, ALL, k, cols((2 * q + t) * P)),
                              lambda k: both(wkvh, wkvl, ALL, k, cols(0, D)))
                elif kind == "value":
                    q = entry[1]
                    free(n)
                    for k in range(NK):
                        mm = mm3(bank[n % RING], both(wkvh, wkvl, ALL, k, cols(D + q // 2 * P)),
                                 both(ch, cl, ALL, k, cols(q % 2 * HALF, HALF)), k == 0, k == 1)
                    mm.then_inc(S["filled"], 1)
                elif kind == "vturn":
                    k = entry[1]
                    free(n)
                    pe.wait_ge(S["v_round"], k + 1)
                    pe.wait_ge(S["identb"], 1)
                    for t in range(NT):
                        mm = pe.transpose(bank[n % RING].bitcast(BF16)[:, t * P:(t + 1) * P],
                                          vround[:, k, t * P:(t + 1) * P], idb[:, :])
                    mm.then_inc(S["filled"], 1)
                elif kind == "query":
                    q = entry[1]
                    if q == 0:
                        pe.wait_ge(S["wq_low"], 1)
                    if q % 2 == 0:
                        pe.wait_ge(S["drained"], drained(FIRST[("norm", 2, q + 1)]))
                    projected(n, lambda k, t: both(hh, hl, ALL, k, cols((2 * q + t) * P)),
                              lambda k: both(wqh, wql, ALL, k))

            def prepare(x):
                for t in range(NT):
                    mm = pe.transpose(operand[:, t * P:(t + 1) * P], x[:, t, :], idb[:, :])
                mm.then_inc(S["prepped"], 1)

            def prepare_queries(h, first):
                pe.wait_ge(S["built"], 6 if first else 6 * h + 2)
                if not first:
                    pe.wait_ge(S["kT_ready"], h)
                prepare(xq)

            def prepare_keys(h):
                pe.wait_ge(S["qT_ready"], 2 * h + 2)
                pe.wait_ge(S["built"], 6 * h + 6)
                prepare(xk)

            def mix(i, n, t):
                pe.wait_ge(S["pT_ready"], 12 * i + 4 * n + t // 2 + 1)
                p, h = part(pT, n, t), 3 * i + n if t >= 0 else 3 * i + n - 1
                t %= NT
                for c in range(NT):
                    mm = pe.matmul(mixed[:, t * HD:(t + 1) * HD], p[:, c * P:(c + 1) * P],
                                   vint[:, c, bass.ds(h * HD, HD)], start=c == 0, stop=c == NT - 1)
                mm.then_inc(S["mix_done"], 1)

            def head_tensor(i, n):
                h, g0, begin = 3 * i + n, 24 * i + 8 * n, n == 0
                for t in range(NT):
                    g = g0 + t
                    if not (begin and t < 3):
                        pe.wait_ge(S["exped"], g - 2)
                    if t == 0:
                        pe.wait_ge(S["qT_ready"], 2 * h + 2)
                        pe.wait_ge(S["kT_ready"], h + 1)
                    for b in range(2):
                        mm = pe.matmul(scores[slot(n, t)][:, b * HALF:(b + 1) * HALF],
                                       qT[n % 3][:, t * P:(t + 1) * P], kT[n % 3][:, b * HALF:(b + 1) * HALF],
                                       start=True, stop=True)
                    mm.then_inc(S["scored"], 1)
                    if not (begin and t < 7):
                        if t == 7 and not begin:
                            pe.wait_ge(S["head_out"], h)
                        mix(i, n, t - 7)
                    if t == 4:
                        prepare_queries(h + 1, False)
                    if t == 6:
                        prepare_keys(h + 1)

            pe.wait_ge(S["drained"], drained(FIRST[("query", 3)]))
            prepare_queries(0, True)
            prepare_keys(0)
            head_tensor(0, 0)
            with pe.Fori(0, (HEADS - 1) // 3) as i:
                for n in (1, 2, 3):
                    head_tensor(i, n)
            for t in range(1, NT):
                mix((HEADS - 2) // 3, 3, t)

            pe.wait_ge(S["head_out"], HEADS)
            for q in range(4):
                norm_turns(("oturn", q), O)
            pe.wait_ge(S["moe_low"], 7)
            for q in range(4):
                n = FIRST[("proj", q)]
                if q % 2 == 0:
                    pe.wait_ge(S["drained"], drained(FIRST[("oturn", q + 1)]))
                projected(n, lambda k, t: both(hh, hl, ALL, k, cols((2 * q + t) * P)), lambda k: both(wph, wpl, ALL, k))
            for q in range(4):
                pe.wait_ge(S["norm_rest" if q > 1 else "norm_ready"], 16)
                norm_turns(("norm", 3, q), xn)

            n = FIRST[("router", 0)]
            free(n)
            for t in range(NT):
                if t % 4 == 0:
                    pe.wait_ge(S["drained"], drained(FIRST[("norm", 3, 2 * (t // 4) + 1)]))
                o = bank[n % RING][:, t * 2 * NE:(t + 1) * 2 * NE]
                for k in range(NK):
                    w = wgs[:, k, :, :].rearrange("p a e -> p (a e)")
                    pe.matmul(o, hh[:, k, cols(t * P)], w, start=k == 0, stop=False)
                    mm = pe.matmul(o, hl[:, k, cols(t * P)], w, start=False, stop=k == NK - 1)
            mm.then_inc(S["filled"], 1)
            for h in range(2):
                n = FIRST[("latent", h)]
                free(n)
                for k in range(NK):
                    mm = mm3(bank[n % RING], both(wdh, wdl, ALL, k), normal(k, h), k == 0, k == 1)
                mm.then_inc(S["filled"], 1)
            def shared(h):
                n = FIRST[("gu", 32 + h)]
                free(n, 2)
                for m in range(2):
                    for k in range(NK):
                        mm = mm3(bank[(n + m) % RING], both(swh, swl, ALL, k, m), normal(k, h), k == 0, k == 1)
                    mm.then_inc(S["filled"], 1)

            shared(0)
            for q in range(2):
                n = FIRST[("wturn", q)]
                free(n)
                pe.wait_ge(S["weights"], 1)
                for t in range(4):
                    mm = pe.transpose(bank[n % RING][0:NE, t * P:(t + 1) * P], prob[:, 4 * q + t, :], idf[:, :])
                mm.then_inc(S["filled"], 1)
            shared(1)

            def gates_ups(k, e, u, first):
                if u % 2 == 0:
                    pe.wait_ge(S["stage_in"], e + 1)
                for m in range(2):
                    if m == 0 and not (first and u < 2):
                        pe.wait_ge(S["rectified"], k - 1)
                    elif m:
                        pe.wait_ge(S["drained"], drained(MOE0) - 1 + (0 if first else 2 * (k - 3)))
                    o = ups[u] if m else gates_of[u % 2]
                    pe.matmul(o, e1s[u // 2][:, m, :], half(xlh[:, :], u % 2), start=True, stop=False)
                    pe.matmul(o, e1s[u // 2][:, m, :], half(xll[:, :], u % 2), start=False, stop=True).then_inc(S["filled"], 1)

            def shared_out(q):
                pe.wait_ge(S["drained"], drained(MOE0) + 2 * (2 * NE - LEAD - 1 + q) + 1)
                for t in range(2):
                    mm3(bank[q][:, t * D:(t + 1) * D], both(sh_h, sh_l, ALL, cols((2 * q + t) * P)),
                        both(s2h, s2l, ALL), t == 0, False, group=False)

            def expert_tensor(k, e, u, first):
                if within(k + LEAD + 1):
                    gates_ups(k + LEAD + 1, e + (u % 2 + LEAD + 1) // 2, (u + LEAD + 1) % 4, False)
                else:
                    shared_out(k + LEAD + 1 - 2 * NE)
                if u % 2 == 0:
                    pe.wait_ge(S["stage_out"], e + 1)
                pe.wait_ge(S["expert_low"], k + 1)
                begin = first and u < 2
                last = not within(k + 2)
                w = e2s[u // 2][:, :, :].rearrange("p a b -> p (a b)")
                o = bank[4 + u % 2]
                pe.matmul(o, w, eh[u], start=begin, stop=False, skip_group_check=True)
                pe.matmul(o, w, el[u], start=False, stop=last, skip_group_check=True).then_inc(S["expert_sum"], 1)

            for k in range(LEAD + 1):
                gates_ups(k, k // 2, k, True)
            expert_halves(pe, expert_tensor)
            pe.wait_ge(S["acc_low"], 2)
            for q in range(4):
                for t in range(2):
                    mm = mm3(bank[q][:, t * D:(t + 1) * D], both(ah, al, ALL, cols((2 * q + t) * P)),
                             both(wuh, wul, ALL), False, True, group=False)
                mm.then_inc(S["filled"], 1)


def kernel(**inputs):
    import concourse.bacc as bacc
    from concourse.bass_utils import run_bass_kernel_spmd as run

    a = {k: np.asarray(v) for k, v in inputs.items()}
    turned = lambda v: np.ascontiguousarray(np.swapaxes(v, -1, -2))
    by_input = lambda v: np.ascontiguousarray(v.transpose(2, 0, 1))
    table, stacked, upper = spline_tables()
    i = np.arange(INTER)
    side, k = np.arange(P)[:, None, None] // 32 % 2, np.arange(P)[:, None, None] % 16 // 4
    at = (127 * (i // 64) + 2 * (i % 64))[None, None, :] + np.arange(2)[None, :, None] + side - 1 + k - 1
    at = np.clip(at, 0, NCP - 1)
    cpw = np.stack([a[f"L0_ffn_{m}_cp"][at] for m in ("gate", "up", "down")])
    arrays = {
        "x": np.ascontiguousarray(a["x"].reshape(T, D)),
        "ident": np.eye(P, dtype=np.float32),
        "ctx_t": turned(a["ctx_2048"].reshape(T, D)),
        "tok": np.ascontiguousarray(a["itok_BxS_13_99985"].reshape(T)),
        "cpw": cpw, "table": table, "stacked": stacked, "upper": np.ascontiguousarray(upper),
        "wq": a["L1_xattn_Wq"], "bq": a["L1_xattn_bq"], "wkv": a["L1_xattn_Wkv"], "bkv": a["L1_xattn_bkv"],
        "bv_t": turned(a["L1_xattn_bkv"][D:].reshape(NK, P)),
        "wp": a["L1_xattn_Wp"], "bp": a["L1_xattn_bp"],
        "sw1_t": turned(a["L1_ffn_sw1"]), "swg_t": turned(a["L1_ffn_swg"]), "sw2_t": turned(a["L1_ffn_sw2"]),
        "rw1_t": by_input(a["L1_ffn_rw1"]), "rwg_t": by_input(a["L1_ffn_rwg"]), "rw2_t": by_input(a["L1_ffn_rw2"]),
        "wg_t": turned(a["L1_ffn_Wg"]), "wdown_t": turned(a["L1_ffn_Wdown"]), "wup_t": turned(a["L1_ffn_Wup"]),
        "biases": a["L1_ffn_biases"],
    }
    nc = bacc.Bacc("TRN2", target_bir_lowering=False, num_devices=1)
    args = {n: nc.dram_tensor(f"in_{n}", v.shape, mybir.dt.from_np(v.dtype), kind="ExternalInput").ap()
            for n, v in arrays.items()}
    out = nc.dram_tensor("out", (T, D), FP32, kind="ExternalOutput").ap()
    build(nc, out=out, **args)
    r = run(nc, [{f"in_{n}": v for n, v in arrays.items()}], core_ids=[0])
    return r.results[0]["out"].reshape(a["x"].shape)
```
